# Optimizing a Trainium2 kernel written in Bass

```python
import numpy as np
import jax
import jax.numpy as jnp

def _softmax(x, axis=-1):
    return jax.nn.softmax(x, axis=axis)

def _gelu(x):
    return jax.nn.gelu(x, approximate=True)

def _silu(x):
    return jax.nn.silu(x)

def _sigmoid(x):
    return jax.nn.sigmoid(x)

def _layernorm(x, axis=-1, eps=1e-05):
    m = jnp.mean(x, axis=axis, keepdims=True)
    v = jnp.var(x, axis=axis, keepdims=True)
    return (x - m) / jnp.sqrt(v + eps)

def _scatter_add(tgt, idx, src, axis=0):
    return tgt.at[idx].add(src)

def _segment_sum(src, seg, n):
    return jax.ops.segment_sum(src, seg, n)
kernel_name = 'mk_flamingo_gated_d1_seqx_r4_180e52'

def setup_inputs(seed: int=0):
    np.random.seed(seed)
    _w = jnp.asarray

    def _rec_inputs():
        import jax
        import jax.numpy as jnp
        _rk = jax.random.key(seed)
        x = 7.22e-05 + 1 * jax.random.normal(jax.random.fold_in(_rk, 1), (8, 512, 256), jnp.float32)
        _lenS = 512 - jax.random.randint(jax.random.fold_in(_rk, 7), (8,), 0, max(1, 512 // 4) + 1, jnp.int32)
        _lenS2 = 512 - jax.random.randint(jax.random.fold_in(_rk, 8), (8,), 0, max(1, 512 // 4) + 1, jnp.int32)
        _ctx_768P = jax.random.normal(jax.random.fold_in(_rk, 11), (8, 16, 192), jnp.float32)
        _ctx_768c = jax.random.dirichlet(jax.random.fold_in(_rk, 511), 0.3 * jnp.ones((16,), jnp.float32), (8, 512))
        _ctx_768t = jnp.einsum('bsk,bkd->bsd', _ctx_768c, _ctx_768P)
        _ctx_768t = _ctx_768t * jax.lax.rsqrt(jnp.mean(jnp.square(_ctx_768t)) + 1e-12) * 0.953939
        ctx_768 = -0.000191848 + 0.999787 * (_ctx_768t + 0.3 * jax.random.normal(jax.random.fold_in(_rk, 611), (8, 512, 192), jnp.float32))
        _g = jax.random.normal(jax.random.fold_in(_rk, 9001), (2, 1), jnp.float32)
        _g = jnp.sign(_g) * jnp.maximum(jnp.abs(_g), 1.0) + (_g == 0) * 1.0
        g_xattn = _g[0]
        g_ffn = _g[1]
        return (x, ctx_768, g_xattn, g_ffn)
    x, ctx_768, g_xattn, g_ffn = _rec_inputs()

    def _L0_xattn_setup():
        import jax, jax.numpy as jnp
        import numpy as np
        DIM_Q = 256
        DIM_KV = 192
        N_HEADS = 4

        def _split_heads(x):
            b, l, d = x.shape
            return x.reshape(b, l, N_HEADS, d // N_HEADS).transpose(0, 2, 1, 3)
        key = jax.random.key(seed)
        ks = jax.random.split(key, 7)
        b, lq, lkv = (4, 512, 512)
        q = jax.random.normal(ks[0], (b, lq, DIM_Q), dtype=jnp.float32)
        kv = jax.random.normal(ks[1], (b, lkv, DIM_KV), dtype=jnp.float32)
        s_q = 1.0 / np.sqrt(DIM_Q)
        s_kv = 1.0 / np.sqrt(DIM_KV)
        Wq = jax.random.normal(ks[2], (DIM_Q, DIM_Q), dtype=jnp.float32) * s_q
        Wk = jax.random.normal(ks[3], (DIM_Q, DIM_KV), dtype=jnp.float32) * s_kv
        Wv = jax.random.normal(ks[4], (DIM_Q, DIM_KV), dtype=jnp.float32) * s_kv
        Wo = jax.random.normal(ks[5], (DIM_Q, DIM_Q), dtype=jnp.float32) * s_q
        bo = jax.random.normal(ks[6], (DIM_Q,), dtype=jnp.float32) * 0.01
        return {'q': q, 'kv': kv, 'Wq': Wq, 'Wk': Wk, 'Wv': Wv, 'Wo': Wo, 'bo': bo}
    _L0_xattn_all = _L0_xattn_setup()
    _L0_xattn_in = {k: v for k, v in _L0_xattn_all.items() if k in ('Wq', 'Wk', 'Wv', 'Wo', 'bo')}
    del _L0_xattn_all

    def _L0_ffn_setup():
        import jax, jax.numpy as jnp
        import numpy as np
        B, S, D, E, H, K = (4, 512, 256, 8, 1024, 2)
        EPS = 1e-06

        def _ln(x, scale, bias):
            m = jnp.mean(x, axis=-1, keepdims=True)
            v = jnp.mean(jnp.square(x - m), axis=-1, keepdims=True)
            return (x - m) * jax.lax.rsqrt(v + EPS) * scale + bias
        key = jax.random.key(seed)
        ks = jax.random.split(key, 4)
        s1 = 1.0 / np.sqrt(D)
        s2 = 1.0 / np.sqrt(H)
        return {'x': jax.random.normal(ks[0], (B, S, D), jnp.float32), 'router_ln_scale': jnp.ones((D,), jnp.float32), 'router_ln_bias': jnp.zeros((D,), jnp.float32), 'router_w': jax.random.normal(ks[1], (E, D), jnp.float32) * s1, 'router_b': jnp.zeros((E,), jnp.float32), 'expert_ln_scale': jnp.ones((E, D), jnp.float32), 'expert_ln_bias': jnp.zeros((E, D), jnp.float32), 'w1': jax.random.normal(ks[2], (E, H, D), jnp.float32) * s1, 'b1': jnp.zeros((E, H), jnp.float32), 'w2': jax.random.normal(ks[3], (E, D, H), jnp.float32) * s2, 'b2': jnp.zeros((E, D), jnp.float32)}
    _L0_ffn_all = _L0_ffn_setup()
    _L0_ffn_in = {k: v for k, v in _L0_ffn_all.items() if k in ('router_ln_scale', 'router_ln_bias', 'router_w', 'router_b', 'expert_ln_scale', 'expert_ln_bias', 'w1', 'b1', 'w2', 'b2')}
    del _L0_ffn_all
    return {'x': x, 'ctx_768': ctx_768, 'g_xattn': g_xattn, 'g_ffn': g_ffn, 'L0_xattn_Wq': _L0_xattn_in['Wq'], 'L0_xattn_Wk': _L0_xattn_in['Wk'], 'L0_xattn_Wv': _L0_xattn_in['Wv'], 'L0_xattn_Wo': _L0_xattn_in['Wo'], 'L0_xattn_bo': _L0_xattn_in['bo'], 'L0_ffn_router_ln_scale': _L0_ffn_in['router_ln_scale'], 'L0_ffn_router_ln_bias': _L0_ffn_in['router_ln_bias'], 'L0_ffn_router_w': _L0_ffn_in['router_w'], 'L0_ffn_router_b': _L0_ffn_in['router_b'], 'L0_ffn_expert_ln_scale': _L0_ffn_in['expert_ln_scale'], 'L0_ffn_expert_ln_bias': _L0_ffn_in['expert_ln_bias'], 'L0_ffn_w1': _L0_ffn_in['w1'], 'L0_ffn_b1': _L0_ffn_in['b1'], 'L0_ffn_w2': _L0_ffn_in['w2'], 'L0_ffn_b2': _L0_ffn_in['b2']}

def reference(x, ctx_768, g_xattn, g_ffn, L0_xattn_Wq, L0_xattn_Wk, L0_xattn_Wv, L0_xattn_Wo, L0_xattn_bo, L0_ffn_router_ln_scale, L0_ffn_router_ln_bias, L0_ffn_router_w, L0_ffn_router_b, L0_ffn_expert_ln_scale, L0_ffn_expert_ln_bias, L0_ffn_w1, L0_ffn_b1, L0_ffn_w2, L0_ffn_b2):
    import jax
    import jax.numpy as jnp

    def _L0_xattn_ref(q, kv, Wq, Wk, Wv, Wo, bo):
        import jax, jax.numpy as jnp
        import numpy as np
        DIM_Q = 256
        DIM_KV = 192
        N_HEADS = 4

        def _split_heads(x):
            b, l, d = x.shape
            return x.reshape(b, l, N_HEADS, d // N_HEADS).transpose(0, 2, 1, 3)
        qp = q @ Wq.T
        kp = kv @ Wk.T
        vp = kv @ Wv.T
        qh, kh, vh = (_split_heads(qp), _split_heads(kp), _split_heads(vp))
        scale = (DIM_Q // N_HEADS) ** (-0.5)
        scores = jnp.einsum('bhqd,bhkd->bhqk', qh, kh) * scale
        attn = jax.nn.softmax(scores, axis=-1)
        ctx = jnp.einsum('bhqk,bhkd->bhqd', attn, vh)
        b, h, lq, hd = ctx.shape
        ctx = ctx.transpose(0, 2, 1, 3).reshape(b, lq, h * hd)
        return ctx @ Wo.T + bo

    def _L0_ffn_ref(x, router_ln_scale, router_ln_bias, router_w, router_b, expert_ln_scale, expert_ln_bias, w1, b1, w2, b2):
        import jax, jax.numpy as jnp
        import numpy as np
        B, S, D, E, H, K = (4, 512, 256, 8, 1024, 2)
        EPS = 1e-06

        def _ln(x, scale, bias):
            m = jnp.mean(x, axis=-1, keepdims=True)
            v = jnp.mean(jnp.square(x - m), axis=-1, keepdims=True)
            return (x - m) * jax.lax.rsqrt(v + EPS) * scale + bias
        orig_shape = x.shape
        xf = x.reshape(-1, D)
        T = xf.shape[0]
        logits = _ln(xf, router_ln_scale, router_ln_bias) @ router_w.T + router_b
        probs = jax.nn.softmax(logits, axis=-1)
        topw, topi = jax.lax.top_k(probs, K)
        topw = topw / jnp.sum(topw, axis=-1, keepdims=True)
        gates = jnp.zeros((T, E), xf.dtype).at[jnp.arange(T)[:, None], topi].set(topw)

        def expert(ls, lb, W1, B1, W2, B2):
            h = jax.nn.gelu(_ln(xf, ls, lb) @ W1.T + B1, approximate=False)
            return h @ W2.T + B2
        ys = jax.vmap(expert)(expert_ln_scale, expert_ln_bias, w1, b1, w2, b2)
        out = jnp.einsum('te,etd->td', gates, ys)
        return out.reshape(orig_shape)
    x = x + jnp.tanh(g_xattn[0]) * _L0_xattn_ref(_layernorm(x, axis=-1), ctx_768, L0_xattn_Wq, L0_xattn_Wk, L0_xattn_Wv, L0_xattn_Wo, L0_xattn_bo)
    x = x + jnp.tanh(g_ffn[0]) * _L0_ffn_ref(_layernorm(x, axis=-1), L0_ffn_router_ln_scale, L0_ffn_router_ln_bias, L0_ffn_router_w, L0_ffn_router_b, L0_ffn_expert_ln_scale, L0_ffn_expert_ln_bias, L0_ffn_w1, L0_ffn_b1, L0_ffn_w2, L0_ffn_b2)
    return x

_drawn_inputs = setup_inputs


def setup_inputs(seed=0):
    import zlib

    import numpy as np

    out = dict(_drawn_inputs(seed))
    spreads = {'L0_ffn_router_ln_scale': (1.0, 0.2),
     'L0_ffn_router_ln_bias': (0.0, 0.1),
     'L0_ffn_router_b': (0.0, 0.1),
     'L0_ffn_expert_ln_scale': (1.0, 0.2),
     'L0_ffn_expert_ln_bias': (0.0, 0.1),
     'L0_ffn_b1': (0.0, 0.1),
     'L0_ffn_b2': (0.0, 0.1)}
    factors = {}
    for name, (base, spread) in spreads.items():
        noise = np.random.default_rng([zlib.crc32(name.encode()), seed]).standard_normal(out[name].shape)
        drawn = base * np.exp(spread * noise) if base else spread * noise
        out[name] = jnp.asarray(drawn.astype(out[name].dtype))
    for name, factor in factors.items():
        out[name] = (out[name] * factor).astype(out[name].dtype)
    return out
```

```python
from contextlib import ExitStack

import concourse.bass as bass
from concourse import mybir

ALU = mybir.AluOpType
ACT = mybir.ActivationFunctionType
AX = mybir.AxisListType
F32 = mybir.dt.float32
F16 = mybir.dt.float16
I32 = mybir.dt.int32

P = 128
W_SCALE = 64.0
LN_EPS, LN2_EPS = 1e-5, 1e-6
FAR_BELOW = -3.0e38
TILE = 256
ROW_EXTRA = 4
COL_TOKEN, COL_G2, COL_DG, COL_E1 = range(4)


def build(nc, x, ctxT, g_xattn, g_ffn, WqT, WkT, WvT, WoT, bo, rls, rlb, rwT, rb, els, elb, w1T, b1, w2T, b2, out):
    B, S, D = x.shape
    DKV = ctxT.shape[1]
    E, _, H = w1T.shape
    HEADS, HD = 4, D // 4
    T = B * S
    NT_TOK = S // P
    DC = D // P
    KVP = DKV // 2
    HC = H // P
    NT = (2 * T) // TILE + E - 1
    REGION = T + TILE
    ROW = D + ROW_EXTRA
    UNITS = NT_TOK * HEADS
    QSCALE = float(HD) ** -0.5
    assert D == 256 and S == 512 and HD == 64 and H == 1024 and UNITS == 16 and HEADS == 4

    x_v = x.rearrange("b (j p) d -> b p j d", p=P)
    out_v = out.rearrange("b s d -> (b s) d")
    ctx_v = ctxT.rearrange("b (c p) s -> b p c s", p=KVP)
    w1_v = w1T.rearrange("e (c p) h -> (e c) p h", p=P)
    w2_v = w2T.rearrange("e (s c p) d -> (e s) p c d", p=P, s=2)
    rows_dram = nc.dram_tensor("expert_rows", (E * REGION + TILE, ROW), F32, kind="Internal").ap()
    acc_dram = nc.dram_tensor("acc_rows", (T + TILE, D), F32, kind="Internal").ap()
    acc_v = acc_dram[0:T, :].rearrange("(b j p) d -> b p j d", p=P, j=NT_TOK)

    def bc(ap1, n):
        return ap1.rearrange("(a d) -> a d", a=1).to_broadcast([n, ap1.shape[0]])

    with ExitStack() as stack:

        def sb(name, shape, dt=F32):
            return stack.enter_context(nc.sbuf_tensor(name, shape, dt))

        def sem(name):
            return stack.enter_context(nc.semaphore(name))

        w1_hi, w1_lo = sb("w1_hi", [P, E * DC * H], F16), sb("w1_lo", [P, E * DC * H], F16)
        arena = sb("arena", [P, E * HC * D])
        arena16 = arena[:, :].bitcast(F16)
        w2_hi, w2_lo = arena16[:, 0:E * HC * D], arena16[:, E * HC * D:2 * E * HC * D]
        used = [0, 0]

        def take(n_bytes, dt=F32):
            at = used[0]
            used[0] += n_bytes
            assert used[0] <= E * HC * D * 4
            v = arena[:, at // 4:(at + n_bytes) // 4]
            return v if dt is F32 else v.bitcast(dt)

        def heads_of():
            return take(HEADS * S * 2, F16).rearrange("p (h s) -> p h s", h=HEADS)

        q_st = [heads_of() for _ in range(2)]
        k_hl = [heads_of() for _ in range(2)]
        k_lh = [heads_of() for _ in range(2)]
        v_hi = [take(NT_TOK * D * 2, F16).rearrange("p (j d) -> p j d", j=NT_TOK) for _ in range(2)]
        v_lo = [take(NT_TOK * D * 2, F16).rearrange("p (j d) -> p j d", j=NT_TOK) for _ in range(2)]
        prob = [take(S * 4) for _ in range(2)]
        pT_hi = [take(S * 2, F16) for _ in range(2)]
        pT_lo = [take(S * 2, F16) for _ in range(2)]
        x_in = take(NT_TOK * D * 4).rearrange("p (j d) -> p j d", j=NT_TOK)
        ctx_in = take(2 * S * 4).rearrange("p (c s) -> p c s", c=2)
        ctx_hi = take(2 * S * 2, F16).rearrange("p (c s) -> p c s", c=2)
        ctx_lo = take(2 * S * 2, F16).rearrange("p (c s) -> p c s", c=2)
        xT_hi = take(DC * S * 2, F16).rearrange("p (c s) -> p c s", c=DC)
        xT_lo = take(DC * S * 2, F16).rearrange("p (c s) -> p c s", c=DC)

        late = sb("late", [P, 6144])
        xn = late[:, 0:1024].rearrange("p (j d) -> p j d", j=NT_TOK)
        o_n = [late[:, 1024 * (1 + i):1024 * (2 + i)].rearrange("p (j d) -> p j d", j=NT_TOK) for i in range(2)]
        oT_hi = late[:, 3072:3584].bitcast(F16).rearrange("p (c s) -> p c s", c=DC)
        oT_lo = late[:, 3584:4096].bitcast(F16).rearrange("p (c s) -> p c s", c=DC)
        zrT_hi = late[:, 4096:4608].bitcast(F16).rearrange("p (c s) -> p c s", c=DC)
        zrT_lo = late[:, 4608:5120].bitcast(F16).rearrange("p (c s) -> p c s", c=DC)
        x2 = late[:, 5120:6144].rearrange("p (j d) -> p j d", j=NT_TOK)
        hid = late[:, 0:2048].rearrange("p (m n) -> p m n", n=2 * TILE)
        h_hi = [late[:, 2048 + 1024 * i:3072 + 1024 * i].bitcast(F16) for i in range(2)]
        h_lo = [late[:, 4096 + 1024 * i:5120 + 1024 * i].bitcast(F16) for i in range(2)]

        stage = [sb(f"stage{i}", [P, H]) for i in range(2)]
        wq_hi, wq_lo = sb("wq_hi", [P, DC, D], F16), sb("wq_lo", [P, DC, D], F16)
        wo_hi, wo_lo = sb("wo_hi", [P, DC, D], F16), sb("wo_lo", [P, DC, D], F16)
        wk_hi, wk_lo = sb("wk_hi", [KVP, 2, D], F16), sb("wk_lo", [KVP, 2, D], F16)
        wv_hi, wv_lo = sb("wv_hi", [KVP, 2, D], F16), sb("wv_lo", [KVP, 2, D], F16)
        rows_w = sb("rows_w", [P, NT_TOK, ROW])
        rows_r = [sb(f"rows_r{i}", [P, 2, ROW]) for i in range(2)]
        z_aff = sb("z_aff", [P, DC, TILE])
        z_hi, z_lo = sb("z_hi", [P, DC, TILE], F16), sb("z_lo", [P, DC, TILE], F16)
        y_out = [sb(f"y_out{i}", [P, 2, D]) for i in range(2)]
        y_idx = [sb(f"y_idx{i}", [P, 2], I32) for i in range(2)]
        b2_all = sb("b2_all", [P, E, D])
        tanh_bo = sb("tanh_bo", [P, D])
        extras = sb("extras", [P, NT, 2, ROW_EXTRA])
        gate = sb("gate", [P, 2])
        els_s, elb_s = sb("els_s", [P, E * DC]), sb("elb_s", [P, E * DC])
        b1_s = sb("b1_s", [P, E * HC])
        ident = sb("ident", [P, P])
        before = sb("before", [P, P], F16)
        ones = sb("ones", [P, P], F16)
        rlb_bc = sb("rlb_bc", [P, DC, P])
        rls_s, rlb_s = sb("rls_s", [P, DC]), sb("rlb_s", [P, DC])
        rw_raw, rw_sc = sb("rw_raw", [P, DC, E]), sb("rw_sc", [P, DC, E])
        rw_hi, rw_lo = sb("rw_hi", [P, DC, E], F16), sb("rw_lo", [P, DC, E], F16)
        rbias = sb("rbias", [P, E])
        gx, gf, gxw = sb("gx", [P, 1]), sb("gf", [P, 1]), sb("gxw", [P, 1])
        stats = sb("stats", [P, 2, NT_TOK, 6])
        mv = sb("mv", [P, 2, NT_TOK, 2])
        rs = sb("rs", [P, 8, NT_TOK])
        half = sb("half", [P, NT_TOK])
        neg_max = sb("neg_max", [P, 2])
        p_sum, p_inv = sb("p_sum", [P, 2, HEADS]), sb("p_inv", [P, HEADS])
        code = sb("code", [P, NT_TOK, E])
        code_i = sb("code_i", [P, NT_TOK, E], I32)
        region_i, region_f = sb("region_i", [P, E], I32), sb("region_f", [P, E])
        base = sb("base", [P, E])
        tok_i, tok_f = sb("tok_i", [P, T // P], I32), sb("tok_f", [P, T // P])
        pad_i = sb("pad_i", [P, 2], I32)
        pad_rows = sb("pad_rows", [P, 2, ROW])
        logit, logit2 = sb("logit", [P, NT_TOK, E]), sb("logit2", [P, NT_TOK, E])
        hot1, hot2 = sb("hot1", [P, NT_TOK, E]), sb("hot2", [P, NT_TOK, E])
        hot16 = sb("hot16", [P, NT_TOK, E], F16)
        tmp8 = sb("tmp8", [P, NT_TOK, E])
        top = sb("top", [P, 8, NT_TOK])
        place = sb("place", [P, NT_TOK, E])
        slot_f, slot_i = sb("slot_f", [P, 2, NT_TOK]), sb("slot_i", [P, 2, NT_TOK], I32)
        tile_i, tile_f = sb("tile_i", [P, NT], I32), sb("tile_f", [P, NT])
        cnt_i, cnt_f = sb("cnt_i", [P, E], I32), sb("cnt_f", [P, E])
        cum, one8 = sb("cum", [P, E]), sb("one8", [P, E])
        past, past_n = sb("past", [P, NT, E]), sb("past_n", [P, NT, E])
        tab = sb("tab", [P, 4, NT])
        tile_expert, tile_row = sb("tile_expert", [P, NT], I32), sb("tile_row", [P, NT], I32)
        pad_at = sb("pad_at", [P, E], I32)

        psum = stack.enter_context(nc.psum_tensor("psum", [P, 8, 512], F32))
        bank_s = [psum[:, i, :] for i in (0, 1)]
        bank_t = [psum[:, i, :] for i in (2, 3)]
        bank_o = [psum[:, i, :] for i in (4, 5)]
        bank_m = [psum[:, i, :] for i in (6, 7)]
        bank_h = [psum[:, i, :] for i in (0, 1, 2, 3)]
        bank_y = [psum[:, i, :] for i in (4, 5)]
        bank_z = psum[:, 6, :]

        small_in = sem("small_in")
        wqkvo_in = [sem(f"wqkvo_in{i}") for i in range(2)]
        x_loaded, ctx_loaded, xres_loaded = sem("x_loaded"), sem("ctx_loaded"), sem("xres_loaded")
        stage_in = [sem(f"stage_in{i}") for i in range(2)]
        const_pool, const_dve = sem("const_pool"), sem("const_dve")
        gates_done, gates_tanh, rbias_mm, rbias_done = sem("gates_done"), sem("gates_tanh"), sem("rbias_mm"), sem("rbias_done")
        wqkvo_hi, wqkvo_lo = sem("wqkvo_hi"), sem("wqkvo_lo")
        ln_stats, ln_done, ln_step = sem("ln_stats"), sem("ln_done"), sem("ln_step")
        ctx_hi_done, ctx_lo_done = sem("ctx_hi_done"), sem("ctx_lo_done")
        res_ready = sem("res_ready")
        side_mm, side_hi, side_done = sem("side_mm"), sem("side_hi"), sem("side_done")
        score_mm, max_done, exp_done = sem("score_mm"), sem("max_done"), sem("exp_done")
        pT_mm, pT_hi_done, pT_lo_done, pv_mm = sem("pT_mm"), sem("pT_hi_done"), sem("pT_lo_done"), sem("pv_mm")
        on_done = sem("on_done")
        x2_stored = sem("x2_stored")
        z_stats = sem("z_stats")
        z_done, z_step = sem("z_done"), sem("z_step")
        dve, chain = sem("dve"), sem("chain")
        masked, gap_sub, inv_done, gate_step = sem("masked"), sem("gap_sub"), sem("inv_done"), sem("gate_step")
        x_bn, z_bn = sem("x_bn"), sem("z_bn")
        gap_done, gap_exp = sem("gap_done"), sem("gap_exp")
        rows_ready, rows_sent = sem("rows_ready"), sem("rows_sent")
        stage_scaled, stage_hi, stage_lo = sem("stage_scaled"), sem("stage_hi"), sem("stage_lo")
        w2_lo_done = sem("w2_lo_done")
        pads_ready, pads_sent, tables = sem("pads_ready"), sem("pads_sent"), sem("tables")
        rows_in = [sem(f"rows_in{i}") for i in range(2)]
        zT_mm, z_aff_done, z_hi_done, z_lo_done = sem("zT_mm"), sem("z_aff_done"), sem("z_hi_done"), sem("z_lo_done")
        h_mm, gelu_done, h_hi_done, h_lo_done = sem("h_mm"), sem("gelu_done"), sem("h_hi_done"), sem("h_lo_done")
        y_mm, y_done, y_added = sem("y_mm"), sem("y_done"), sem("y_added")
        out_stored = sem("out_stored")
        settled = sem("settled")

        PRE = ["xT0", "xT1", "q0", "q1", "k0", "k1", "v0", "v1"]
        POST = ["oT0", "oT1", "out0", "out1", "zT0", "zT1", "logits", "prefix"]
        BOTH = ["oT0", "oT1", "out0", "out1", "xT0", "xT1", "q0", "q1", "k0", "zT0", "zT1", "k1", "logits", "v0", "v1", "prefix"]
        NO_HI = ("out0", "out1", "logits", "prefix")

        def numbered(names, units, n0, hi0):
            rows, hi = [], hi0
            for i, (name, u) in enumerate(zip(names, units)):
                rows.append((name, u, n0 + i, hi, i % 2))
                hi += name not in NO_HI
            return rows

        FIRST = numbered(PRE, range(8), 0, 0)
        LAST = numbered(POST, range(8), 16 * B - 8, 8 * B + 4 * (B - 1))

        def steps_of(b):
            if isinstance(b, int) and b == 0:
                return numbered(PRE, range(0, UNITS, 2), 8, 8)
            if isinstance(b, int) and b == B - 1:
                return numbered(POST, [BOTH.index(s) for s in POST], b * 16, (b + 1) * 8 + (b - 1) * 4)
            return numbered(BOTH, range(UNITS), b * 16, (b + 1) * 8 + (b - 1) * 4)

        def wait(eng, s, n):
            if not isinstance(n, int) or n > 0:
                eng.wait_ge(s, n)

        def settle(eng):
            eng.sem_inc(settled, 1)

        def over_batches(eng, body):
            body(0, 0)
            with eng.Fori(0, (B - 2) // 2) as i:
                body(i * 2 + 1, 1)
                body(i * 2 + 2, 0)
            body(B - 1, (B - 1) % 2)

        def over_tiles(eng, body):
            body(0, 0)
            with eng.Fori(0, (NT - 3) // 2) as i:
                body(i * 2 + 1, 1)
                body(i * 2 + 2, 0)

        PIECES = E * DC
        SMALL_LOADS = 11
        block = stack.enter_context(nc.Block())

        @block.sync
        def _(sp):
            sp.dma_start(x_in, x_v[0]).then_inc(x_loaded, 16)
            sp.dma_start(ctx_in[0:KVP], ctx_v[0]).then_inc(ctx_loaded, 16)
            sp.dma_start(stage[0][:, 0:512].rearrange("p (c n) -> p c n", c=DC), WqT.rearrange("(c p) n -> p c n", p=P)).then_inc(wqkvo_in[0], 16)
            sp.dma_start(stage[0][:, 512:1024].rearrange("p (c n) -> p c n", c=DC), WoT.rearrange("(c p) n -> p c n", p=P)).then_inc(wqkvo_in[0], 16)
            sp.dma_start(stage[1][0:KVP, 0:512].rearrange("p (c n) -> p c n", c=2), WkT.rearrange("(c p) n -> p c n", p=KVP)).then_inc(wqkvo_in[1], 16)
            sp.dma_start(stage[1][0:KVP, 512:1024].rearrange("p (c n) -> p c n", c=2), WvT.rearrange("(c p) n -> p c n", p=KVP)).then_inc(wqkvo_in[1], 16)
            sp.dma_start(gx[:, :], bc(g_xattn, P)).then_inc(small_in, 16)
            sp.dma_start(gf[:, :], bc(g_ffn, P)).then_inc(small_in, 16)
            sp.dma_start(tanh_bo[:, :], bc(bo, P)).then_inc(small_in, 16)
            sp.dma_start(rbias[:, :], bc(rb, P)).then_inc(small_in, 16)
            sp.dma_start(rls_s[:, :], rls).then_inc(small_in, 16)
            sp.dma_start(rlb_s[:, :], rlb).then_inc(small_in, 16)
            sp.dma_start(rw_raw[:, :, :], rwT.rearrange("(c p) e -> p c e", p=P)).then_inc(small_in, 16)
            sp.dma_start(els_s[:, :], els).then_inc(small_in, 16)
            sp.dma_start(elb_s[:, :], elb).then_inc(small_in, 16)
            sp.dma_start(b1_s[:, :], b1).then_inc(small_in, 16)
            sp.dma_start(b2_all[:, :, :].rearrange("p e d -> p (e d)"), bc(b2.rearrange("e d -> (e d)"), P)).then_inc(small_in, 16)
            sp.dma_start(x2, x_v[0]).then_inc(xres_loaded, 16)
            sp.wait_ge(pads_ready, 1)
            sp.dma_start(rows_dram[E * REGION:E * REGION + TILE, :].rearrange("(s p) n -> p s n", p=P), pad_rows[:, :, :]).then_inc(pads_sent, 16)
            sp.dma_start(acc_dram[T:T + TILE, :].rearrange("(s p) n -> p s n", p=P), pad_rows[:, :, 0:D]).then_inc(pads_sent, 16)

            def batch(b, par):
                if not (isinstance(b, int) and b == B - 1):
                    wait(sp, ln_done, b + 1)
                    settle(sp)
                    sp.dma_start(x_in, x_v[b + 1] if isinstance(b, int) else x_v[bass.ds(b + 1, 1)].rearrange("a p j d -> (a p) j d")).then_inc(x_loaded, 16)
                    sp.wait_ge(ctx_hi_done, b + 1)
                    sp.wait_ge(ctx_lo_done, b + 1)
                    settle(sp)
                    sp.dma_start(ctx_in[0:KVP], ctx_v[b + 1] if isinstance(b, int) else ctx_v[bass.ds(b + 1, 1)].rearrange("a p c s -> (a p) c s")).then_inc(ctx_loaded, 16)
                for s in range(2):
                    n = b * 2 + s
                    if isinstance(b, int) and b == 0:
                        sp.wait_ge(wqkvo_lo, 4)
                    else:
                        sp.wait_ge(stage_lo, n - 1)
                        settle(sp)
                    sp.dma_start(stage[s][:, :], w1_v[n] if isinstance(b, int) else w1_v[bass.ds(n, 1)].rearrange("a p h -> (a p) h")).then_inc(stage_in[s], 16)
                if not (isinstance(b, int) and b == 0):
                    store_x2(b - 1)
                    sp.wait_ge(z_done, b)
                    settle(sp)
                    sp.wait_ge(x2_stored, 16 * b)
                    settle(sp)
                    sp.dma_start(x2, x_v[b] if isinstance(b, int) else x_v[bass.ds(b, 1)].rearrange("a p j d -> (a p) j d")).then_inc(xres_loaded, 16)

            def store_x2(b):
                sp.wait_ge(z_stats, b + 1)
                settle(sp)
                sp.dma_start(acc_v[b] if isinstance(b, int) else acc_v[bass.ds(b, 1)].rearrange("a p j d -> (a p) j d"), x2).then_inc(x2_stored, 16)

            over_batches(sp, batch)
            for n in range(PIECES):
                sp.wait_ge(stage_lo, PIECES + n - 1)
                sp.dma_start(stage[n % 2][:, :].rearrange("p (c d) -> p c d", d=D), w2_v[n]).then_inc(stage_in[n % 2], 16)
                if n == 1:
                    store_x2(B - 1)
            sp.wait_ge(tables, 2)
            for e in range(E):
                at = sp.value_load(pad_at[0:1, e:e + 1], min_val=e * REGION, max_val=e * REGION + T)
                sp.dma_start(rows_dram[bass.ds(at, TILE), :].rearrange("(s p) n -> p s n", p=P), pad_rows[:, :, :]).then_inc(pads_sent, 16)
            sp.wait_ge(pads_sent, 16 * (2 + E))
            sp.wait_ge(rows_sent, 16 * 2 * NT_TOK * B)

            def load_rows(j, par):
                at = sp.value_load(tile_row[0:1, j:j + 1] if isinstance(j, int) else tile_row[0:1, bass.ds(j, 1)], min_val=0, max_val=E * REGION)
                sp.dma_start(rows_r[par][:, :, :], rows_dram[bass.ds(at, TILE), :].rearrange("(s p) n -> p s n", p=P)).then_inc(rows_in[par], 16)

            load_rows(0, 0)
            load_rows(1, 1)

            def more_rows(j, par):
                sp.wait_ge(zT_mm, j + 1)
                sp.wait_ge(z_lo_done, j + 1)
                settle(sp)
                load_rows(j + 2, par)

            over_tiles(sp, more_rows)
            sp.wait_ge(x2_stored, 16 * B)
            sp.wait_ge(y_added, 16 * 2 * NT)
            sp.dma_start(out_v, acc_dram[0:T, :]).then_inc(out_stored, 16)
            sp.wait_ge(out_stored, 16)

        @block.gpsimd
        def _(pool):
            pool.memset(ident[:, :], 0.0).then_inc(const_pool, 1)
            pool.memset(before[:, :], 1.0).then_inc(const_pool, 1)
            pool.memset(pad_rows[:, :, :], 0.0).then_inc(const_pool, 1)
            pool.memset(half[:, :], -0.5).then_inc(const_pool, 1)
            pool.iota(code_i[:, :, :], pattern=[[0, NT_TOK], [-1, E]], base=E, channel_multiplier=0).then_inc(const_pool, 1)
            pool.iota(region_i[:, :], pattern=[[REGION, E]], base=0, channel_multiplier=0).then_inc(const_pool, 1)
            pool.iota(tok_i[:, :], pattern=[[P, T // P]], base=0, channel_multiplier=1).then_inc(const_pool, 1)
            pool.iota(tile_i[:, :], pattern=[[1, NT]], base=0, channel_multiplier=0).then_inc(const_pool, 1)
            pool.iota(pad_i[:, :], pattern=[[P, 2]], base=T, channel_multiplier=1).then_inc(const_pool, 1)
            pool.wait_ge(const_pool, 9)
            pool.affine_select(out=ident[:, :], in_=ident[:, :], compare_op=ALU.not_equal, fill=1.0, base=0,
                               pattern=[[-1, P]], channel_multiplier=1).then_inc(const_pool, 1)
            pool.affine_select(out=before[:, :], in_=before[:, :], compare_op=ALU.is_gt, fill=0.0, base=0,
                               pattern=[[1, P]], channel_multiplier=-1).then_inc(const_pool, 1)

            def step(s, count, ins):
                ins.then_inc(s, 1)
                pool.wait_ge(s, count)
                settle(pool)

            LN_STEPS, Z_STEPS = 2, 7

            def normalise_x(b):
                pool.wait_ge(ln_stats, b + 1)
                settle(pool)
                c = b * LN_STEPS
                step(ln_step, c + 1, pool.tensor_scalar(rs[:, 0, :], mv[:, 0, :, 1], LN_EPS, None, ALU.add))
                step(ln_step, c + 2, pool.tensor_tensor(rs[:, 1, :], rs[:, 0, :], half[:, :], ALU.pow))
                for j in range(NT_TOK):
                    last = pool.tensor_scalar(xn[:, j, :], x_in[:, j, :], mv[:, 0, j, 0:1], rs[:, 1, j:j + 1], ALU.subtract, ALU.mult)
                last.then_inc(ln_done, 1)

            def ctx_low(b):
                pool.wait_ge(ctx_hi_done, b + 1)
                pool.tensor_tensor(ctx_lo[0:KVP], ctx_in[0:KVP], ctx_hi[0:KVP], ALU.subtract).then_inc(ctx_lo_done, 1)

            def residual(b):
                pool.wait_ge(xres_loaded, 16 * (b + 1))
                pool.tensor_tensor(x2, x2, tanh_bo[:, :].unsqueeze(1).to_broadcast([P, NT_TOK, D]), ALU.add).then_inc(res_ready, 1)

            def normalise_z(b):
                pool.wait_ge(z_stats, b + 1)
                settle(pool)
                c = b * Z_STEPS
                var = mv[:, 1, :, 1]
                step(z_step, c + 1, pool.tensor_scalar(rs[:, 2, :], var, LN_EPS, None, ALU.add))
                step(z_step, c + 2, pool.tensor_tensor(rs[:, 3, :], rs[:, 2, :], half[:, :], ALU.pow))
                step(z_step, c + 3, pool.tensor_tensor(rs[:, 4, :], rs[:, 3, :], rs[:, 3, :], ALU.mult))
                step(z_step, c + 4, pool.tensor_tensor(rs[:, 5, :], rs[:, 4, :], var, ALU.mult))
                step(z_step, c + 5, pool.tensor_scalar(rs[:, 5, :], rs[:, 5, :], LN2_EPS, None, ALU.add))
                step(z_step, c + 6, pool.tensor_tensor(rs[:, 6, :], rs[:, 5, :], half[:, :], ALU.pow))
                step(z_step, c + 7, pool.tensor_tensor(rs[:, 7, :], rs[:, 3, :], rs[:, 6, :], ALU.mult))
                settle(pool)
                for j in range(NT_TOK):
                    last = pool.tensor_scalar(rows_w[:, j, 0:D], x2[:, j, :], mv[:, 1, j, 0:1], rs[:, 7, j:j + 1], ALU.subtract, ALU.mult)
                last.then_inc(z_done, 1)

            def stage_low(n, lo, s):
                pool.wait_ge(stage_hi, n + 1)
                pool.tensor_tensor(lo[0], stage[s][:, :], lo[1], ALU.subtract).then_inc(stage_lo, 1)

            def scatter(b):
                pool.wait_ge(rows_ready, b + 1)
                settle(pool)
                for k in range(2):
                    for j in range(NT_TOK):
                        pool.indirect_dma_start(rows_dram[:, :], bass.IndirectOffsetOnAxis(ap=slot_i[:, k, j:j + 1], axis=0),
                                                rows_w[:, j, :], None).then_inc(rows_sent, 16)
                pool.wait_ge(rows_sent, (b + 1) * 2 * NT_TOK * 16)

            def w1_piece(t, n):
                return t[:, n * H:(n + 1) * H] if isinstance(n, int) else t[:, bass.ds(n * H, H)]

            pool.wait_ge(gates_done, 1)
            ctx_low(0)
            normalise_x(0)
            residual(0)

            def batch(b, par):
                if not (isinstance(b, int) and b == B - 1):
                    normalise_x(b + 1)
                    ctx_low(b + 1)
                if not (isinstance(b, int) and b == 0):
                    normalise_z(b - 1)
                for s in range(2):
                    n = b * 2 + s
                    stage_low(n, (w1_piece(w1_lo, n), w1_piece(w1_hi, n)), s)
                if not (isinstance(b, int) and b == 0):
                    residual(b)
                    scatter(b - 1)

            over_batches(pool, batch)
            normalise_z(B - 1)
            for n in range(PIECES):
                lo = w2_lo[:, n * H:(n + 1) * H]
                stage_low(PIECES + n, (lo, w2_hi[:, n * H:(n + 1) * H]), n % 2)

            scatter(B - 1)
            pool.wait_ge(x2_stored, 16 * B)

            def add_rows(j, par):
                pool.wait_ge(y_done, j + 1)
                if not isinstance(j, int) or j > 0:
                    pool.wait_ge(y_added, 32 * j)
                settle(pool)
                for s in range(2):
                    pool.indirect_dma_start(acc_dram[:, :], bass.IndirectOffsetOnAxis(ap=y_idx[par][:, s:s + 1], axis=0),
                                            y_out[par][:, s, :], None, compute_op=ALU.add).then_inc(y_added, 16)

            add_rows(0, 0)
            with pool.Fori(0, (NT - 1) // 2) as i:
                add_rows(i * 2 + 1, 1)
                add_rows(i * 2 + 2, 0)
            pool.wait_ge(y_added, 32 * NT)

        @block.scalar
        def _(act):
            act.wait_ge(small_in, 16 * SMALL_LOADS)
            act.activation(gx[:, :], gx[:, :], ACT.Tanh).then_inc(gates_tanh, 1)
            act.activation(gf[:, :], gf[:, :], ACT.Tanh).then_inc(gates_tanh, 1)

            def ctx_high(b):
                act.wait_ge(ctx_loaded, 16 * (b + 1))
                if not (isinstance(b, int) and b == 0):
                    act.wait_ge(side_mm, (b - 1) * 16 if not isinstance(b, int) else max((b - 1) * 16, 8))
                act.activation(ctx_hi[0:KVP], ctx_in[0:KVP], ACT.Copy).then_inc(ctx_hi_done, 1)

            def side_high(name, b, n, m):
                if name in NO_HI:
                    return
                act.wait_ge(side_mm, n + 1)
                src = bank_m[m]
                par = b % 2 if isinstance(b, int) else None
                if name[:-1] == "xT":
                    act.activation(xT_hi[:, int(name[-1]), :], src, ACT.Copy).then_inc(side_hi, 1)
                elif name[:-1] == "oT":
                    act.activation(oT_hi[:, int(name[-1]), :], src, ACT.Copy).then_inc(side_hi, 1)
                elif name[:-1] == "zT":
                    act.activation(zrT_hi[:, int(name[-1]), :], src, ACT.Copy).then_inc(side_hi, 1)

            def proj_high(name, par, n, m):
                act.wait_ge(side_mm, n + 1)
                c, src = int(name[-1]), bank_m[m]
                if name[0] == "v":
                    act.activation(v_hi[par][:, 2 * c:2 * c + 2, :].rearrange("p j d -> p (j d)"), src, ACT.Copy, scale=1.0 / W_SCALE).then_inc(side_hi, 1)
                    return
                dst, scale = (q_st[par], QSCALE / W_SCALE) if name[0] == "q" else (k_hl[par], 1.0 / W_SCALE)
                act.activation(dst[0:64, 2 * c, :], src[0:64, :], ACT.Copy, scale=scale)
                act.activation(dst[0:64, 2 * c + 1, :], src[64:128, :], ACT.Copy, scale=scale).then_inc(side_hi, 1)

            def side(step, b, par):
                name, _, n, _, m = step
                if name[0] in "qkv":
                    proj_high(name, par, n, m)
                else:
                    side_high(name, b, n, m)

            ctx_high(0)
            for st in FIRST:
                side(st, 0, 0)

            def batch(b, par):
                steps = {s[1]: s for s in steps_of(b)}
                for u in range(UNITS):
                    g, t = b * UNITS + u, u % 2
                    act.wait_ge(max_done, g + 1)
                    wait(act, pT_mm, g - 1)
                    if u % HEADS == 0:
                        wait(act, on_done, b * NT_TOK + u // HEADS - 1)
                    act.activation(prob[t], bank_s[t], ACT.Exp, bias=neg_max[:, t:t + 1],
                                   accum_out=p_sum[:, (u // HEADS) % 2, u % HEADS:u % HEADS + 1]).then_inc(exp_done, 1)
                    act.wait_ge(pT_mm, g + 1)
                    wait(act, pv_mm, g - 1)
                    act.activation(pT_hi[t], bank_t[t], ACT.Copy).then_inc(pT_hi_done, 1)
                    if u in steps:
                        name = steps[u][0]
                        side(steps[u], b - 1 if name in POST else b + 1, 1 - par)
                    if u == 3 and not (isinstance(b, int) and b == B - 1):
                        ctx_high(b + 1)
                    if u == 14 and not (isinstance(b, int) and b == 0):
                        gap(b - 1)

            def gap(b):
                act.wait_ge(gap_done, b + 1)
                act.activation(top[:, 5, :], top[:, 4, :], ACT.Exp).then_inc(gap_exp, 1)

            over_batches(act, batch)
            for n in range(PIECES):
                if n == 0:
                    act.wait_ge(pv_mm, B * UNITS)
                if n < 2 * len(POST) and n % 2 == 0 and n // 2 < 6:
                    side(LAST[n // 2], B - 1, (B - 1) % 2)
                act.wait_ge(stage_in[n % 2], 16 * (PIECES // 2 + n // 2 + 1))
                act.activation(stage[n % 2][:, :], stage[n % 2][:, :], ACT.Copy, scale=W_SCALE).then_inc(stage_scaled, 1)
                act.wait_ge(stage_scaled, PIECES + n + 1)
                act.activation(w2_hi[:, n * H:(n + 1) * H], stage[n % 2][:, :], ACT.Copy).then_inc(stage_hi, 1)
            gap(B - 1)

            act.wait_ge(tables, 2)

            def rows_high(j):
                act.wait_ge(z_aff_done, j + 1)
                act.activation(z_hi[:, :, :], z_aff[:, :, :], ACT.Copy).then_inc(z_hi_done, 1)

            def gelus(j):
                e = act.value_load(tile_expert[0:1, j:j + 1] if isinstance(j, int) else tile_expert[0:1, bass.ds(j, 1)], min_val=0, max_val=E - 1)
                for m in range(HC // 2):
                    act.wait_ge(h_mm, j * 4 + m + 1)
                    wait(act, h_lo_done, (j - 1) * 4 + m + 1)
                    for i in range(2):
                        hc = 2 * m + i
                        last = act.activation(hid[:, m, i * TILE:(i + 1) * TILE], bank_h[m][:, i * TILE:(i + 1) * TILE], ACT.Gelu,
                                              bias=b1_s[:, bass.ds(e * HC + hc, 1)], scale=1.0 / W_SCALE)
                    last.then_inc(gelu_done, 1)

            rows_high(0)
            gelus(0)
            rows_high(1)

            def tile(j):
                gelus(j + 1)
                rows_high(j + 2)

            with act.Fori(0, NT - 2) as i:
                tile(i)
            gelus(NT - 1)

        @block.tensor
        def _(pe):
            def products(dst, pairs, start=True, stop=True):
                for i, (a, b_) in enumerate(pairs):
                    last = pe.matmul(dst, a, b_, start=start and i == 0, stop=stop and i == len(pairs) - 1)
                return last

            def three(a_hi, a_lo, b_hi, b_lo):
                return [(a_hi, b_hi), (a_hi, b_lo), (a_lo, b_hi)]

            def side(step, b, par):
                name, _, n, hi, m = step
                dst, c = bank_m[m], int(name[-1]) if name[-1].isdigit() else 0
                wait(pe, side_done, n - 1)
                kind = name.rstrip("01")
                if kind in ("xT", "oT", "zT"):
                    if kind == "xT":
                        pe.wait_ge(ln_done, b + 1)
                        src = xn
                    elif kind == "oT":
                        pe.wait_ge(on_done, (b + 1) * NT_TOK)
                        src = o_n[par]
                    else:
                        pe.wait_ge(z_done, b + 1)
                        src = rows_w
                    for j in range(NT_TOK):
                        last = pe.transpose(dst[:, j * P:(j + 1) * P], src[:, j, c * P:(c + 1) * P], ident[:, :])
                elif kind in ("q", "k"):
                    if name == "q0":
                        pe.wait_ge(side_done, n)
                    if name == "k0":
                        pe.wait_ge(ctx_lo_done, b + 1)
                    if kind == "q":
                        w, a, rows = (wq_hi, wq_lo), (xT_hi, xT_lo), P
                    else:
                        w, a, rows = (wk_hi, wk_lo), (ctx_hi, ctx_lo), KVP
                    pairs = []
                    for k in range(2):
                        cols = slice(c * P, (c + 1) * P)
                        pairs += three(w[0][:, k, cols], w[1][:, k, cols], a[0][0:rows, k, :], a[1][0:rows, k, :])
                    last = products(dst, pairs)
                elif kind == "v":
                    for i in range(2):
                        toks = slice((2 * c + i) * P, (2 * c + i + 1) * P)
                        pairs = []
                        for k in range(2):
                            pairs += three(ctx_hi[0:KVP, k, toks], ctx_lo[0:KVP, k, toks], wv_hi[:, k, :], wv_lo[:, k, :])
                        last = products(dst[:, i * D:(i + 1) * D], pairs)
                elif kind == "out":
                    if name == "out0":
                        pe.wait_ge(side_done, n)
                    for i in range(2):
                        toks = slice((2 * c + i) * P, (2 * c + i + 1) * P)
                        pairs = []
                        for k in range(DC):
                            pairs += three(oT_hi[:, k, toks], oT_lo[:, k, toks], wo_hi[:, k, :], wo_lo[:, k, :])
                        last = products(dst[:, i * D:(i + 1) * D], pairs)
                elif kind == "logits":
                    pe.wait_ge(side_done, n)
                    for j in range(NT_TOK):
                        toks = slice(j * P, (j + 1) * P)
                        pairs = []
                        for k in range(DC):
                            pairs += three(zrT_hi[:, k, toks], zrT_lo[:, k, toks], rw_hi[:, k, :], rw_lo[:, k, :])
                        last = products(dst[:, j * E:(j + 1) * E], pairs)
                else:
                    pe.wait_ge(gap_done, b + 1)
                    for j in range(NT_TOK + 1):
                        pairs = [(ones[:, :], hot16[:, i, :]) for i in range(j)]
                        if j < NT_TOK:
                            pairs.append((before[:, :], hot16[:, j, :]))
                        last = products(dst[:, j * E:(j + 1) * E], pairs)
                last.then_inc(side_mm, 1)

            def scores(g, u, par):
                t, h, j = u % 2, u % HEADS, u // HEADS
                wait(pe, exp_done, g - 1)
                q = q_st[par][:, h, j * P:(j + 1) * P]
                products(bank_s[t], [(q, k_hl[par][:, h, :]), (q, k_lh[par][:, h, :])]).then_inc(score_mm, 1)

            def turn(g, u):
                t = u % 2
                pe.wait_ge(exp_done, g + 1)
                wait(pe, pT_lo_done, g - 1)
                for k in range(S // P):
                    last = pe.transpose(bank_t[t][:, k * P:(k + 1) * P], prob[t][:, k * P:(k + 1) * P], ident[:, :])
                last.then_inc(pT_mm, 1)

            def weigh(g, u, par, b):
                t, h, j = u % 2, u % HEADS, u // HEADS
                if h == 0:
                    wait(pe, on_done, b * NT_TOK + j - 1)
                pe.wait_ge(pT_lo_done, g + 1)
                cols, pairs = slice(h * HD, (h + 1) * HD), []
                for k in range(S // P):
                    keys = slice(k * P, (k + 1) * P)
                    pairs += three(pT_hi[t][:, keys], pT_lo[t][:, keys], v_hi[par][:, k, cols], v_lo[par][:, k, cols])
                products(bank_o[j % 2][:, cols], pairs).then_inc(pv_mm, 1)

            pe.wait_ge(const_pool, 11)
            pe.wait_ge(const_dve, 1)
            for k in range(DC):
                last = pe.matmul(bank_s[0][:, 0:E], rlb_bc[:, k, :], rw_raw[:, k, :], start=k == 0, stop=k == DC - 1)
            last.then_inc(rbias_mm, 1)
            pe.wait_ge(wqkvo_lo, 4)
            for st in FIRST:
                side(st, 0, 0)
            pe.wait_ge(rbias_done, 1)
            pe.wait_ge(side_done, 8)
            scores(0, 0, 0)

            def batch(b, par):
                steps = {s[1]: s for s in steps_of(b)}
                for u in range(UNITS):
                    g = b * UNITS + u
                    last_batch = isinstance(b, int) and b == B - 1
                    if u < UNITS - 1:
                        scores(g + 1, u + 1, par)
                    elif not last_batch:
                        k1 = [s for s in steps_of(b) if s[0] == "k1"][0]
                        pe.wait_ge(side_done, k1[2] + 1)
                        scores(g + 1, 0, 1 - par)
                    if u > 0:
                        weigh(g - 1, u - 1, par, b)
                    elif not (isinstance(b, int) and b == 0):
                        weigh(g - 1, UNITS - 1, 1 - par, b - 1)
                    turn(g, u)
                    if u in steps:
                        name = steps[u][0]
                        side(steps[u], b - 1 if name in POST else b + 1, 1 - par)

            over_batches(pe, batch)
            weigh(B * UNITS - 1, UNITS - 1, (B - 1) % 2, B - 1)
            for st in LAST:
                side(st, B - 1, (B - 1) % 2)

            def expert_of(j):
                return pe.value_load(tile_expert[0:1, j:j + 1] if isinstance(j, int) else tile_expert[0:1, bass.ds(j, 1)], min_val=0, max_val=E - 1)

            def rows_turn(j, par):
                pe.wait_ge(rows_in[par], (j // 2 + 1) * 16 if isinstance(j, int) else j * 8 + 16 - 8 * par)
                wait(pe, z_aff_done, j)
                for c in range(DC):
                    for s in range(2):
                        last = pe.transpose(bank_z[:, c * TILE + s * P:c * TILE + (s + 1) * P], rows_r[par][:, s, c * P:(c + 1) * P], ident[:, :])
                last.then_inc(zT_mm, 1)

            def hidden(j, e):
                pe.wait_ge(z_lo_done, j + 1)
                for m in range(HC // 2):
                    wait(pe, gelu_done, (j - 1) * 4 + m + 1)
                    for i in range(2):
                        pairs = []
                        for c in range(DC):
                            at = e * (DC * H) + c * H + (2 * m + i) * P
                            pairs += three(w1_hi[:, bass.ds(at, P)], w1_lo[:, bass.ds(at, P)], z_hi[:, c, :], z_lo[:, c, :])
                        last = products(bank_h[m][:, i * TILE:(i + 1) * TILE], pairs)
                    last.then_inc(h_mm, 1)

            def back(j, e, par):
                wait(pe, y_done, j - 1)
                pe.wait_ge(h_lo_done, j * 4 + 4)
                for s in range(2):
                    pairs = []
                    for hc in range(HC):
                        rows = slice(hc * TILE + s * P, hc * TILE + (s + 1) * P)
                        at = e * (HC * D) + hc * D
                        pairs += three(h_hi[par][:, rows], h_lo[par][:, rows], w2_hi[:, bass.ds(at, D)], w2_lo[:, bass.ds(at, D)])
                    last = products(bank_y[par][:, s * D:(s + 1) * D], pairs)
                last.then_inc(y_mm, 1)

            pe.wait_ge(side_done, 16 * B)
            pe.wait_ge(tables, 2)
            pe.wait_ge(stage_lo, 2 * PIECES)
            rows_turn(0, 0)
            hidden(0, expert_of(0))
            rows_turn(1, 1)

            def tile(j, par):
                hidden(j + 1, expert_of(j + 1))
                rows_turn(j + 2, par)
                back(j, expert_of(j), par)

            over_tiles(pe, tile)
            hidden(NT - 1, expert_of(NT - 1))
            back(NT - 2, expert_of(NT - 2), (NT - 2) % 2)
            back(NT - 1, expert_of(NT - 1), (NT - 1) % 2)

        @block.vector
        def _(v):
            v.memset(ones[:, :], 1.0).then_inc(dve, 1)
            v.memset(one8[:, :], 1.0).then_inc(dve, 1)
            v.wait_ge(const_pool, 9)
            v.tensor_copy(code[:, :, :], code_i[:, :, :]).then_inc(dve, 1)
            v.tensor_copy(region_f[:, :], region_i[:, :]).then_inc(dve, 1)
            v.tensor_copy(base[:, :], region_i[:, :]).then_inc(dve, 1)
            v.tensor_copy(tok_f[:, :], tok_i[:, :]).then_inc(dve, 1)
            v.tensor_copy(tile_f[:, :], tile_i[:, :]).then_inc(dve, 1)
            v.tensor_copy(pad_rows[:, :, D + COL_TOKEN], pad_i[:, :]).then_inc(pads_ready, 1)
            v.wait_ge(small_in, 16 * SMALL_LOADS)
            for k in range(DC):
                v.tensor_copy(rlb_bc[:, k, :], rlb_s[:, k:k + 1].to_broadcast([P, P])).then_inc(dve, 1)
                v.tensor_scalar(rw_sc[:, k, :], rw_raw[:, k, :], rls_s[:, k:k + 1], W_SCALE, ALU.mult, ALU.mult).then_inc(dve, 1)
            v.wait_ge(dve, 11)
            v.tensor_copy(rw_hi[:, :, :], rw_sc[:, :, :]).then_inc(dve, 1)
            v.wait_ge(dve, 12)
            v.tensor_tensor(rw_lo[:, :, :], rw_sc[:, :, :], rw_hi[:, :, :], ALU.subtract).then_inc(const_dve, 1)
            v.wait_ge(gates_tanh, 2)
            v.tensor_scalar(gxw[:, :], gx[:, :], 1.0 / W_SCALE, None, ALU.mult).then_inc(dve, 1)
            v.tensor_scalar(tanh_bo[:, :], tanh_bo[:, :], gx[:, 0:1], None, ALU.mult).then_inc(gates_done, 1)

            def x_stats(b):
                v.wait_ge(x_loaded, 16 * (b + 1))
                wait(v, ln_done, b)
                for j in range(NT_TOK):
                    last = v.bn_stats(stats[:, 0, j, :], x_in[:, j, :])
                last.then_inc(x_bn, 1)
                v.wait_ge(x_bn, b + 1)
                settle(v)
                for j in range(NT_TOK):
                    last = v.bn_aggr(mv[:, 0, j, :], stats[:, 0, j, :])
                last.then_inc(ln_stats, 1)

            def z_statistics(b, n):
                v.wait_ge(side_done, n + 1)
                for j in range(NT_TOK):
                    last = v.bn_stats(stats[:, 1, j, :], x2[:, j, :])
                last.then_inc(z_bn, 1)
                v.wait_ge(z_bn, b + 1)
                settle(v)
                for j in range(NT_TOK):
                    last = v.bn_aggr(mv[:, 1, j, :], stats[:, 1, j, :])
                last.then_inc(z_stats, 1)

            v.wait_ge(dve, 13)
            x_stats(0)
            for i, (hi, lo, src) in enumerate([
                    (wq_hi, wq_lo, stage[0][:, 0:512]), (wo_hi, wo_lo, stage[0][:, 512:1024]),
                    (wk_hi, wk_lo, stage[1][0:KVP, 0:512]), (wv_hi, wv_lo, stage[1][0:KVP, 512:1024])]):
                v.wait_ge(wqkvo_in[i // 2], 32)
                v.tensor_scalar(hi[:, :, :].rearrange("p c n -> p (c n)"), src, W_SCALE, None, ALU.mult).then_inc(wqkvo_hi, 1)
                v.wait_ge(wqkvo_hi, i + 1)
                v.scalar_tensor_tensor(out=lo[:, :, :].rearrange("p c n -> p (c n)"), in0=src, scalar=W_SCALE,
                                       in1=hi[:, :, :].rearrange("p c n -> p (c n)"), op0=ALU.mult, op1=ALU.subtract).then_inc(wqkvo_lo, 1)
            v.wait_ge(rbias_mm, 1)
            v.tensor_tensor(rbias[:, :], bank_s[0][:, 0:E], rbias[:, :], ALU.add).then_inc(rbias_done, 1)

            CHAIN = 19

            def chained(c, ins):
                ins.then_inc(chain, 1)
                v.wait_ge(chain, c)

            def route(b, n, m):
                c = b * CHAIN
                v.wait_ge(side_mm, n + 1)
                shape = [P, NT_TOK, E]
                v.scalar_tensor_tensor(out=logit[:, :, :], in0=bank_m[m][:, 0:NT_TOK * E].rearrange("p (j e) -> p j e", j=NT_TOK),
                                       scalar=1.0 / W_SCALE, in1=rbias[:, :].unsqueeze(1).to_broadcast(shape),
                                       op0=ALU.mult, op1=ALU.add).then_inc(side_done, 1)
                v.wait_ge(side_done, n + 1)
                for k, (src, hot) in enumerate([(logit, hot1), (logit2, hot2)]):
                    at = c + k * 5
                    chained(at + 1, v.tensor_reduce(top[:, 2 * k, :], src[:, :, :], AX.X, ALU.max))
                    chained(at + 2, v.tensor_tensor(tmp8[:, :, :], src[:, :, :], top[:, 2 * k, :].unsqueeze(2).to_broadcast(shape), ALU.is_equal))
                    chained(at + 3, v.tensor_tensor(tmp8[:, :, :], tmp8[:, :, :], code[:, :, :], ALU.mult))
                    chained(at + 4, v.tensor_reduce(top[:, 2 * k + 1, :], tmp8[:, :, :], AX.X, ALU.max))
                    chained(at + 5, v.tensor_tensor(hot[:, :, :], code[:, :, :], top[:, 2 * k + 1, :].unsqueeze(2).to_broadcast(shape), ALU.is_equal))
                    if k == 0:
                        v.scalar_tensor_tensor(out=logit2[:, :, :], in0=hot1[:, :, :], scalar=FAR_BELOW, in1=logit[:, :, :],
                                               op0=ALU.mult, op1=ALU.add).then_inc(masked, 1)
                        v.wait_ge(masked, b + 1)
                v.tensor_tensor(top[:, 4, :], top[:, 2, :], top[:, 0, :], ALU.subtract).then_inc(gap_sub, 1)
                v.wait_ge(gap_sub, b + 1)
                v.tensor_tensor(hot16[:, :, :], hot1[:, :, :], hot2[:, :, :], ALU.add).then_inc(gap_done, 1)

            def slots(b, n, m):
                c = b * CHAIN + 10
                shape = [P, NT_TOK, E]
                v.wait_ge(z_done, b + 1)
                v.wait_ge(gap_exp, b + 1)
                chained(c + 1, v.tensor_scalar(top[:, 6, :], top[:, 5, :], 1.0, None, ALU.add))
                chained(c + 2, v.reciprocal(top[:, 6, :], top[:, 6, :]))
                chained(c + 3, v.tensor_scalar(top[:, 6, :], top[:, 6, :], gf[:, 0:1], None, ALU.mult))
                chained(c + 4, v.tensor_tensor(rows_w[:, :, D + COL_G2], top[:, 6, :], top[:, 5, :], ALU.mult))
                v.tensor_tensor(rows_w[:, :, D + COL_DG], top[:, 6, :], rows_w[:, :, D + COL_G2], ALU.subtract)
                v.tensor_copy(rows_w[:, :, D + COL_E1], top[:, 1, :])
                v.tensor_copy(rows_w[:, :, D + COL_TOKEN], tok_f[:, b * NT_TOK:(b + 1) * NT_TOK] if isinstance(b, int) else tok_f[:, bass.ds(b * NT_TOK, NT_TOK)])
                v.wait_ge(side_mm, n + 1)
                chained(c + 5, v.tensor_tensor(place[:, :, :], bank_m[m][:, 0:NT_TOK * E].rearrange("p (j e) -> p j e", j=NT_TOK),
                                               base[:, :].unsqueeze(1).to_broadcast(shape), ALU.add))
                v.tensor_tensor(base[:, :], bank_m[m][:, NT_TOK * E:(NT_TOK + 1) * E], base[:, :], ALU.add).then_inc(side_done, 1)
                chained(c + 6, v.tensor_tensor(tmp8[:, :, :], hot1[:, :, :], place[:, :, :], ALU.mult))
                chained(c + 7, v.tensor_reduce(slot_f[:, 0, :], tmp8[:, :, :], AX.X, ALU.add))
                chained(c + 8, v.tensor_tensor(tmp8[:, :, :], hot2[:, :, :], place[:, :, :], ALU.mult))
                chained(c + 9, v.tensor_reduce(slot_f[:, 1, :], tmp8[:, :, :], AX.X, ALU.add))
                v.tensor_copy(slot_i[:, :, :], slot_f[:, :, :]).then_inc(rows_ready, 1)

            def side(step, b, par):
                name, _, n, hi, m = step
                src, c = bank_m[m], int(name[-1]) if name[-1].isdigit() else 0
                kind = name.rstrip("01")
                if name == "logits":
                    return route(b, n, m)
                if name == "prefix":
                    return slots(b, n, m)
                if kind == "out":
                    v.wait_ge(side_mm, n + 1)
                    v.wait_ge(res_ready, b + 1)
                    half_of = x2[:, 2 * c:2 * c + 2, :].rearrange("p j d -> p (j d)")
                    v.scalar_tensor_tensor(out=half_of, in0=src, scalar=gxw[:, 0:1], in1=half_of, op0=ALU.mult, op1=ALU.add).then_inc(side_done, 1)
                    return
                v.wait_ge(side_hi, hi + 1)
                if kind in ("xT", "oT", "zT"):
                    h, l = {"xT": (xT_hi, xT_lo), "oT": (oT_hi, oT_lo), "zT": (zrT_hi, zrT_lo)}[kind]
                    v.tensor_tensor(l[:, c, :], src, h[:, c, :], ALU.subtract).then_inc(side_done, 1)
                elif kind == "v":
                    h, l = (t[par][:, 2 * c:2 * c + 2, :].rearrange("p j d -> p (j d)") for t in (v_hi, v_lo))
                    v.scalar_tensor_tensor(out=l, in0=src, scalar=1.0 / W_SCALE, in1=h, op0=ALU.mult, op1=ALU.subtract).then_inc(side_done, 1)
                elif kind == "q":
                    for i in range(2):
                        last = v.scalar_tensor_tensor(out=q_st[par][64:128, 2 * c + i, :], in0=src[64 * i:64 * i + 64, :], scalar=QSCALE / W_SCALE,
                                                      in1=q_st[par][0:64, 2 * c + i, :], op0=ALU.mult, op1=ALU.subtract)
                    last.then_inc(side_done, 1)
                else:
                    for i in range(2):
                        h = 2 * c + i
                        v.tensor_copy(k_lh[par][64:128, h, :], k_hl[par][0:64, h, :])
                        v.scalar_tensor_tensor(out=k_hl[par][64:128, h, :], in0=src[64 * i:64 * i + 64, :], scalar=1.0 / W_SCALE,
                                               in1=k_hl[par][0:64, h, :], op0=ALU.mult, op1=ALU.subtract)
                        last = v.scalar_tensor_tensor(out=k_lh[par][0:64, h, :], in0=src[64 * i:64 * i + 64, :], scalar=1.0 / W_SCALE,
                                                      in1=k_hl[par][0:64, h, :], op0=ALU.mult, op1=ALU.subtract)
                    last.then_inc(side_done, 1)

            for st in FIRST:
                side(st, 0, 0)

            def batch(b, par):
                steps = {s[1]: s for s in steps_of(b)}
                first, final = isinstance(b, int) and b == 0, isinstance(b, int) and b == B - 1
                for u in range(UNITS):
                    g, t = b * UNITS + u, u % 2
                    if u == 0:
                        row_max(g, 0)
                    if u < UNITS - 1:
                        row_max(g + 1, 1 - t)
                    v.wait_ge(pT_hi_done, g + 1)
                    v.tensor_tensor(pT_lo[t], bank_t[t], pT_hi[t], ALU.subtract).then_inc(pT_lo_done, 1)
                    if u % HEADS == 0 and not (first and u == 0):
                        if u == 0:
                            normalise(b - 1, NT_TOK - 1, 1 - par)
                        else:
                            normalise(b, u // HEADS - 1, par)
                    if u == 0 and not final:
                        x_stats(b + 1)
                    if u in steps:
                        name = steps[u][0]
                        side(steps[u], b - 1 if name in POST else b + 1, 1 - par)
                        if name == "out1":
                            z_statistics(b - 1, steps[u][2])
                    if u in (5, 9):
                        s = (u - 5) // 4
                        n = b * 2 + s
                        v.wait_ge(stage_in[s], b * 16 + 16)
                        v.tensor_scalar(stage[s][:, :], stage[s][:, :], W_SCALE, None, ALU.mult).then_inc(stage_scaled, 1)
                        v.wait_ge(stage_scaled, n + 1)
                        v.tensor_copy(w1_hi[:, n * H:(n + 1) * H] if isinstance(n, int) else w1_hi[:, bass.ds(n * H, H)],
                                      stage[s][:, :]).then_inc(stage_hi, 1)

            def row_max(g, t):
                v.wait_ge(score_mm, g + 1)
                wait(v, exp_done, g - 1)
                v.tensor_reduce(neg_max[:, t:t + 1], bank_s[t], AX.X, ALU.max, negate=True).then_inc(max_done, 1)

            def normalise(b, j, par):
                n = b * NT_TOK + j
                v.wait_ge(pv_mm, (n + 1) * HEADS)
                wait(v, on_done, n)
                v.reciprocal(p_inv[:, :], p_sum[:, j % 2, :]).then_inc(inv_done, 1)
                v.wait_ge(inv_done, n + 1)
                v.tensor_tensor(o_n[par][:, j, :].rearrange("p (h d) -> p h d", h=HEADS),
                                bank_o[j % 2][:, 0:D].rearrange("p (h d) -> p h d", h=HEADS),
                                p_inv[:, :].unsqueeze(2).to_broadcast([P, HEADS, HD]), ALU.mult).then_inc(on_done, 1)

            over_batches(v, batch)
            normalise(B - 1, NT_TOK - 1, (B - 1) % 2)
            for st in LAST:
                side(st, B - 1, (B - 1) % 2)
                if st[0] == "out1":
                    z_statistics(B - 1, st[2])

            t0 = B * CHAIN
            links = iter(range(t0 + 1, t0 + 100))
            v.wait_ge(side_done, 16 * B)
            v.tensor_copy(pad_at[:, :], base[:, :]).then_inc(tables, 1)
            chained(next(links), v.tensor_tensor(cnt_f[:, :], base[:, :], region_f[:, :], ALU.subtract))
            chained(next(links), v.tensor_scalar(cnt_i[:, :], cnt_f[:, :], float(TILE - 1), None, ALU.add))
            chained(next(links), v.tensor_scalar(cnt_i[:, :], cnt_i[:, :], TILE.bit_length() - 1, None, ALU.arith_shift_right))
            chained(next(links), v.tensor_copy(cnt_f[:, :], cnt_i[:, :]))
            chained(next(links), v.tensor_tensor_scan(cum[:, :], one8[:, :], cnt_f[:, :], 0.0, ALU.mult, ALU.add))
            shape = [P, NT, E]
            chained(next(links), v.tensor_tensor(past[:, :, :], tile_f[:, :].unsqueeze(2).to_broadcast(shape),
                                                 cum[:, :].unsqueeze(1).to_broadcast(shape), ALU.is_ge))
            chained(next(links), v.tensor_tensor(past_n[:, :, :], past[:, :, :], cnt_f[:, :].unsqueeze(1).to_broadcast(shape), ALU.mult))
            chained(next(links), v.tensor_reduce(tab[:, 0, :], past[:, :, :], AX.X, ALU.add))
            chained(next(links), v.tensor_reduce(tab[:, 1, :], past_n[:, :, :], AX.X, ALU.add))
            chained(next(links), v.tensor_tensor(tab[:, 1, :], tile_f[:, :], tab[:, 1, :], ALU.subtract))
            chained(next(links), v.tensor_scalar(tab[:, 2, :], tab[:, 0, :], float(E), float(TILE), ALU.is_lt, ALU.mult))
            chained(next(links), v.tensor_tensor(tab[:, 1, :], tab[:, 1, :], tab[:, 2, :], ALU.mult))
            chained(next(links), v.tensor_scalar(tile_expert[:, :], tab[:, 0, :], float(E - 1), None, ALU.min))
            v.scalar_tensor_tensor(out=tile_row[:, :], in0=tab[:, 0, :], scalar=float(REGION), in1=tab[:, 1, :],
                                   op0=ALU.mult, op1=ALU.add).then_inc(tables, 1)
            v.wait_ge(tables, 2)

            def expert_of(j):
                return v.value_load(tile_expert[0:1, j:j + 1] if isinstance(j, int) else tile_expert[0:1, bass.ds(j, 1)], min_val=0, max_val=E - 1)

            def rows_split(j, par, e):
                v.wait_ge(zT_mm, j + 1)
                wait(v, z_hi_done, j)
                for c in range(DC):
                    col = bass.ds(e * DC + c, 1)
                    last = v.tensor_scalar(z_aff[:, c, :], bank_z[:, c * TILE:(c + 1) * TILE], els_s[:, col], elb_s[:, col], ALU.mult, ALU.add)
                last.then_inc(z_aff_done, 1)
                v.tensor_copy(extras[:, j if isinstance(j, int) else bass.ds(j, 1), :, :] if isinstance(j, int) else
                              extras[:, bass.ds(j, 1), :, :].rearrange("p a s n -> p (a s) n"), rows_r[par][:, :, D:ROW])
                v.wait_ge(z_hi_done, j + 1)
                v.tensor_tensor(z_lo[:, :, :], z_aff[:, :, :], z_hi[:, :, :], ALU.subtract).then_inc(z_lo_done, 1)

            def split_hidden(j, par):
                wait(v, y_mm, j - 1)
                for m in range(HC // 2):
                    cols = slice(m * 2 * TILE, (m + 1) * 2 * TILE)
                    v.wait_ge(gelu_done, j * 4 + m + 1)
                    v.tensor_copy(h_hi[par][:, cols], hid[:, m, :]).then_inc(h_hi_done, 1)
                    v.wait_ge(h_hi_done, j * 4 + m + 1)
                    v.tensor_tensor(h_lo[par][:, cols], hid[:, m, :], h_hi[par][:, cols], ALU.subtract).then_inc(h_lo_done, 1)

            def finish_rows(j, par, e):
                mine = extras[:, j, :, :] if isinstance(j, int) else extras[:, bass.ds(j, 1), :, :].rearrange("p a s n -> p (a s) n")
                wait(v, y_added, 32 * (j - 1))
                wait(v, y_done, j)
                v.tensor_copy(y_idx[par][:, :], mine[:, :, COL_TOKEN])
                v.scalar_tensor_tensor(out=gate[:, :], in0=mine[:, :, COL_E1], scalar=code[:, 0, bass.ds(e, 1)], in1=mine[:, :, COL_DG],
                                       op0=ALU.is_equal, op1=ALU.mult).then_inc(gate_step, 1)
                v.wait_ge(gate_step, j * 3 + 1)
                v.tensor_tensor(gate[:, :], gate[:, :], mine[:, :, COL_G2], ALU.add).then_inc(gate_step, 1)
                v.wait_ge(y_mm, j + 1)
                v.scalar_tensor_tensor(out=y_out[par][:, :, :], in0=bank_y[par][:, :].rearrange("p (s d) -> p s d", s=2), scalar=1.0 / W_SCALE,
                                       in1=b2_all[:, bass.ds(e, 1), :].to_broadcast([P, 2, D]), op0=ALU.mult, op1=ALU.add).then_inc(gate_step, 1)
                v.wait_ge(gate_step, j * 3 + 3)
                for s in range(2):
                    last = v.tensor_scalar(y_out[par][:, s, :], y_out[par][:, s, :], gate[:, s:s + 1], None, ALU.mult)
                last.then_inc(y_done, 1)

            rows_split(0, 0, expert_of(0))
            split_hidden(0, 0)
            rows_split(1, 1, expert_of(1))

            def tile(j, par):
                split_hidden(j + 1, 1 - par)
                rows_split(j + 2, par, expert_of(j + 2))
                finish_rows(j, par, expert_of(j))

            over_tiles(v, tile)
            split_hidden(NT - 1, (NT - 1) % 2)
            finish_rows(NT - 2, (NT - 2) % 2, expert_of(NT - 2))
            finish_rows(NT - 1, (NT - 1) % 2, expert_of(NT - 1))


_OUT_SHAPE = (8, 512, 256)


def kernel(**inputs):
    import numpy as np
    import concourse.bacc as bacc
    from concourse.bass_utils import run_bass_kernel_spmd

    def a(name):
        return np.asarray(inputs[name])

    E = a("L0_ffn_w1").shape[0]
    arrays = {
        "x": a("x"),
        "ctxT": a("ctx_768").transpose(0, 2, 1),
        "g_xattn": a("g_xattn"),
        "g_ffn": a("g_ffn"),
        "WqT": a("L0_xattn_Wq").T,
        "WkT": a("L0_xattn_Wk").T,
        "WvT": a("L0_xattn_Wv").T,
        "WoT": a("L0_xattn_Wo").T,
        "bo": a("L0_xattn_bo"),
        "rls": a("L0_ffn_router_ln_scale").reshape(-1, 128).T,
        "rlb": a("L0_ffn_router_ln_bias").reshape(-1, 128).T,
        "rwT": a("L0_ffn_router_w").T,
        "rb": a("L0_ffn_router_b"),
        "els": a("L0_ffn_expert_ln_scale").reshape(-1, 128).T,
        "elb": a("L0_ffn_expert_ln_bias").reshape(-1, 128).T,
        "w1T": a("L0_ffn_w1").transpose(0, 2, 1),
        "b1": a("L0_ffn_b1").reshape(-1, 128).T,
        "w2T": a("L0_ffn_w2").transpose(0, 2, 1),
        "b2": a("L0_ffn_b2"),
    }
    nc = bacc.Bacc("TRN2", target_bir_lowering=False, num_devices=1)
    maps, args = {}, []
    for name, value in arrays.items():
        value = np.ascontiguousarray(value)
        maps[f"in_{name}"] = value
        args.append(nc.dram_tensor(f"in_{name}", value.shape, mybir.dt.from_np(value.dtype), kind="ExternalInput").ap())
    out = nc.dram_tensor("out", _OUT_SHAPE, F32, kind="ExternalOutput").ap()
    build(nc, *args, out)
    r = run_bass_kernel_spmd(nc, [maps], core_ids=[0])
    return r.results[0]["out"]
```

```python
from contextlib import ExitStack

import concourse.bass as bass
from concourse import mybir

ALU = mybir.AluOpType
ACT = mybir.ActivationFunctionType
AX = mybir.AxisListType
F32 = mybir.dt.float32
F16 = mybir.dt.float16
I32 = mybir.dt.int32

P = 128
W_SCALE = 64.0
LN_EPS, LN2_EPS = 1e-5, 1e-6
FAR_BELOW = -3.0e38
TILE = 256
ROW_EXTRA = 4
COL_TOKEN, COL_G2, COL_DG, COL_E1 = range(4)


def build(nc, x, ctxT, g_xattn, g_ffn, WqT, WkT, WvT, WoT, bo, rls, rlb, rwT, rb, els, elb, w1T, b1, w2T, b2, out):
    B, S, D = x.shape
    DKV = ctxT.shape[1]
    E, _, H = w1T.shape
    HEADS, HD = 4, D // 4
    T = B * S
    NT_TOK = S // P
    DC = D // P
    KVP = DKV // 2
    HC = H // P
    NT = (2 * T) // TILE + E - 1
    REGION = T + TILE
    ROW = D + ROW_EXTRA
    UNITS = NT_TOK * HEADS
    QSCALE = float(HD) ** -0.5
    assert D == 256 and S == 512 and HD == 64 and H == 1024 and UNITS == 16 and HEADS == 4

    x_v = x.rearrange("b (j p) d -> b p j d", p=P)
    out_v = out.rearrange("b s d -> (b s) d")
    ctx_v = ctxT.rearrange("b (c p) s -> b p c s", p=KVP)
    w1_v = w1T.rearrange("e (c p) h -> (e c) p h", p=P)
    w2_v = w2T.rearrange("e (s c p) d -> (e s) p c d", p=P, s=2)
    rows_dram = nc.dram_tensor("expert_rows", (E * REGION + TILE, ROW), F32, kind="Internal").ap()
    acc_dram = nc.dram_tensor("acc_rows", (T + TILE, D), F32, kind="Internal").ap()
    acc_v = acc_dram[0:T, :].rearrange("(b j p) d -> b p j d", p=P, j=NT_TOK)

    def bc(ap1, n):
        return ap1.rearrange("(a d) -> a d", a=1).to_broadcast([n, ap1.shape[0]])

    with ExitStack() as stack:

        def sb(name, shape, dt=F32):
            return stack.enter_context(nc.sbuf_tensor(name, shape, dt))

        def sem(name):
            return stack.enter_context(nc.semaphore(name))

        w1_hi, w1_lo = sb("w1_hi", [P, E * DC * H], F16), sb("w1_lo", [P, E * DC * H], F16)
        arena = sb("arena", [P, E * HC * D])
        arena16 = arena[:, :].bitcast(F16)
        used = [0, 0]

        def take(n_bytes, dt=F32):
            at = used[0]
            used[0] += n_bytes
            assert used[0] <= E * HC * D * 4
            v = arena[:, at // 4:(at + n_bytes) // 4]
            return v if dt is F32 else v.bitcast(dt)

        def heads_of():
            return take(HEADS * S * 2, F16).rearrange("p (h s) -> p h s", h=HEADS)

        def qkv():
            return [heads_of() for _ in range(3)] + [take(NT_TOK * D * 2, F16).rearrange("p (j d) -> p j d", j=NT_TOK) for _ in range(2)]

        x_in = take(NT_TOK * D * 4).rearrange("p (j d) -> p j d", j=NT_TOK)
        ctx_in = take(2 * S * 4).rearrange("p (c s) -> p c s", c=2)
        ctx_hi = take(2 * S * 2, F16).rearrange("p (c s) -> p c s", c=2)
        ctx_lo = take(2 * S * 2, F16).rearrange("p (c s) -> p c s", c=2)
        xT_hi = take(DC * S * 2, F16).rearrange("p (c s) -> p c s", c=DC)
        xT_lo = take(DC * S * 2, F16).rearrange("p (c s) -> p c s", c=DC)
        BEFORE_QKV = used[0]
        qkv_even = qkv()
        used[0] += E * HC * D * 4 - used[0] - 4 * S * 4 - (used[0] - BEFORE_QKV)
        EARLY = used[0]
        qkv_odd = qkv()
        q_st, k_hl, k_lh, v_hi, v_lo = zip(qkv_even, qkv_odd)
        prob = [take(S * 4) for _ in range(2)]
        pT_hi = [take(S * 2, F16) for _ in range(2)]
        pT_lo = [take(S * 2, F16) for _ in range(2)]

        late = sb("late", [P, 6144])
        xn = late[:, 0:1024].rearrange("p (j d) -> p j d", j=NT_TOK)
        o_n = [late[:, 1024 * (1 + i):1024 * (2 + i)].rearrange("p (j d) -> p j d", j=NT_TOK) for i in range(2)]
        oT_hi = late[:, 3072:3584].bitcast(F16).rearrange("p (c s) -> p c s", c=DC)
        oT_lo = late[:, 3584:4096].bitcast(F16).rearrange("p (c s) -> p c s", c=DC)
        zrT_hi = late[:, 4096:4608].bitcast(F16).rearrange("p (c s) -> p c s", c=DC)
        zrT_lo = late[:, 4608:5120].bitcast(F16).rearrange("p (c s) -> p c s", c=DC)
        x2 = late[:, 5120:6144].rearrange("p (j d) -> p j d", j=NT_TOK)
        hid = late[:, 0:2048].rearrange("p (m n) -> p m n", n=2 * TILE)
        h_hi = [late[:, 2048 + 1024 * i:3072 + 1024 * i].bitcast(F16) for i in range(2)]
        h_lo = [late[:, 4096 + 1024 * i:5120 + 1024 * i].bitcast(F16) for i in range(2)]

        stage = [sb(f"stage{i}", [P, H]) for i in range(2)]
        wq_hi, wq_lo = sb("wq_hi", [P, DC, D], F16), sb("wq_lo", [P, DC, D], F16)
        wo_hi, wo_lo = sb("wo_hi", [P, DC, D], F16), sb("wo_lo", [P, DC, D], F16)
        wk_hi, wk_lo = sb("wk_hi", [KVP, 2, D], F16), sb("wk_lo", [KVP, 2, D], F16)
        wv_hi, wv_lo = sb("wv_hi", [KVP, 2, D], F16), sb("wv_lo", [KVP, 2, D], F16)
        rows_w = sb("rows_w", [P, NT_TOK, ROW])
        rows_r = [sb(f"rows_r{i}", [P, 2, ROW]) for i in range(2)]
        turned = [t[:, :, :].rearrange("p s n -> p (s n)")[:, 0:S] for t in rows_r]
        z_aff = sb("z_aff", [P, DC, TILE])
        z_hi, z_lo = sb("z_hi", [P, DC, TILE], F16), sb("z_lo", [P, DC, TILE], F16)
        y_out = [sb(f"y_out{i}", [P, 2, D]) for i in range(2)]
        y_idx = [sb(f"y_idx{i}", [P, 2], I32) for i in range(2)]
        b2_all = sb("b2_all", [P, E, D])
        tanh_bo = sb("tanh_bo", [P, D])
        extras = sb("extras", [P, NT, 2, ROW_EXTRA])
        gate = sb("gate", [P, 2])
        els_s, elb_s = sb("els_s", [P, E * DC]), sb("elb_s", [P, E * DC])
        b1_s = sb("b1_s", [P, E * HC])
        ident = sb("ident", [P, P])
        before = sb("before", [P, P], F16)
        ones = sb("ones", [P, P], F16)
        rlb_bc = sb("rlb_bc", [P, DC, P])
        rls_s, rlb_s = sb("rls_s", [P, DC]), sb("rlb_s", [P, DC])
        rw_raw, rw_sc = sb("rw_raw", [P, DC, E]), sb("rw_sc", [P, DC, E])
        rw_hi, rw_lo = sb("rw_hi", [P, DC, E], F16), sb("rw_lo", [P, DC, E], F16)
        rbias = sb("rbias", [P, E])
        gx, gf, gxw = sb("gx", [P, 1]), sb("gf", [P, 1]), sb("gxw", [P, 1])
        stats = sb("stats", [P, 2, NT_TOK, 6])
        mv = sb("mv", [P, 2, NT_TOK, 2])
        rs = sb("rs", [P, 8, NT_TOK])
        half = sb("half", [P, NT_TOK])
        neg_max = sb("neg_max", [P, 2])
        p_sum, p_inv = sb("p_sum", [P, 2, HEADS]), sb("p_inv", [P, HEADS])
        code = sb("code", [P, NT_TOK, E])
        code_i = sb("code_i", [P, NT_TOK, E], I32)
        region_i, region_f = sb("region_i", [P, E], I32), sb("region_f", [P, E])
        base = sb("base", [P, E])
        tok_i, tok_f = sb("tok_i", [P, T // P], I32), sb("tok_f", [P, T // P])
        pad_i = sb("pad_i", [P, 2], I32)
        pad_rows = sb("pad_rows", [P, 2, ROW])
        logit, logit2 = sb("logit", [P, NT_TOK, E]), sb("logit2", [P, NT_TOK, E])
        hot1, hot2 = sb("hot1", [P, NT_TOK, E]), sb("hot2", [P, NT_TOK, E])
        hot16 = sb("hot16", [P, NT_TOK, E], F16)
        tmp8 = sb("tmp8", [P, NT_TOK, E])
        top = sb("top", [P, 8, NT_TOK])
        place = sb("place", [P, NT_TOK, E])
        slot_f, slot_i = sb("slot_f", [P, 2, NT_TOK]), sb("slot_i", [P, 2, NT_TOK], I32)
        tile_i, tile_f = sb("tile_i", [P, NT], I32), sb("tile_f", [P, NT])
        cnt_i, cnt_f = sb("cnt_i", [P, E], I32), sb("cnt_f", [P, E])
        cum, one8 = sb("cum", [P, E]), sb("one8", [P, E])
        past, past_n = sb("past", [P, NT, E]), sb("past_n", [P, NT, E])
        tab = sb("tab", [P, 4, NT])
        tile_expert, tile_row = sb("tile_expert", [P, NT], I32), sb("tile_row", [P, NT], I32)
        pad_at = sb("pad_at", [P, E], I32)

        psum = stack.enter_context(nc.psum_tensor("psum", [P, 8, 512], F32))
        bank_s = [psum[:, i, :] for i in (0, 1)]
        bank_t = [psum[:, i, :] for i in (2, 3)]
        bank_o = [psum[:, i, :] for i in (4, 5)]
        bank_m = [psum[:, i, :] for i in (6, 7)]
        bank_h = [psum[:, i, :] for i in (0, 1, 2, 3)]
        bank_y = [psum[:, i, :] for i in (4, 5)]
        bank_z = psum[:, 6, :]

        small_in = sem("small_in")
        wqkvo_in = [sem(f"wqkvo_in{i}") for i in range(2)]
        x_loaded, ctx_loaded, xres_loaded = sem("x_loaded"), sem("ctx_loaded"), sem("xres_loaded")
        stage_in = [sem(f"stage_in{i}") for i in range(2)]
        const_pool, const_dve = sem("const_pool"), sem("const_dve")
        gates_done, gates_tanh, rbias_mm, rbias_done = sem("gates_done"), sem("gates_tanh"), sem("rbias_mm"), sem("rbias_done")
        wqkvo_hi, wqkvo_lo = sem("wqkvo_hi"), sem("wqkvo_lo")
        ln_stats, ln_done, ln_step = sem("ln_stats"), sem("ln_done"), sem("ln_step")
        ctx_hi_done, ctx_lo_done = sem("ctx_hi_done"), sem("ctx_lo_done")
        res_ready = sem("res_ready")
        side_mm, side_hi, side_done = sem("side_mm"), sem("side_hi"), sem("side_done")
        turned_hi, turned_copied, turned_lo = sem("turned_hi"), sem("turned_copied"), sem("turned_lo")
        score_mm, max_done, exp_done = sem("score_mm"), sem("max_done"), sem("exp_done")
        pT_mm, pT_hi_done, pT_lo_done, pv_mm = sem("pT_mm"), sem("pT_hi_done"), sem("pT_lo_done"), sem("pv_mm")
        on_done, k_swapped = sem("on_done"), sem("k_swapped")
        x_scale_ready, z_scale_ready = sem("x_scale_ready"), sem("z_scale_ready")
        x2_stored = sem("x2_stored")
        z_stats = sem("z_stats")
        z_done, z_step = sem("z_done"), sem("z_step")
        dve, chain = sem("dve"), sem("chain")
        masked, gap_sub, inv_done, gate_step = sem("masked"), sem("gap_sub"), sem("inv_done"), sem("gate_step")
        x_bn, z_bn = sem("x_bn"), sem("z_bn")
        gap_done, gap_exp = sem("gap_done"), sem("gap_exp")
        rows_ready, rows_sent = sem("rows_ready"), sem("rows_sent")
        stage_scaled, stage_hi, stage_lo = sem("stage_scaled"), sem("stage_hi"), sem("stage_lo")
        w2_hi_done, w2_lo_done = sem("w2_hi_done"), sem("w2_lo_done")
        pads_ready, pads_sent, tables = sem("pads_ready"), sem("pads_sent"), sem("tables")
        rows_in = [sem(f"rows_in{i}") for i in range(2)]
        zT_mm, z_aff_done, z_hi_done, z_lo_done = sem("zT_mm"), sem("z_aff_done"), sem("z_hi_done"), sem("z_lo_done")
        h_mm, gelu_done, h_hi_done, h_lo_done = sem("h_mm"), sem("gelu_done"), sem("h_hi_done"), sem("h_lo_done")
        y_mm, y_done, y_added = sem("y_mm"), sem("y_done"), sem("y_added")
        out_stored = sem("out_stored")
        settled = sem("settled")

        PRE = ["k0", "k1", "xT0", "xT1", "v0", "q0", "q1", "v1"]
        POST = ["oT0", "oT1", "out0", "out1", "zT0", "zT1", "logits", "prefix"]
        UNIT_OF = {"oT0": 1, "oT1": 2, "out0": 3, "out1": 4, "k0": 6, "k1": 7, "xT0": 8, "xT1": 8.5, "v0": 9,
                   "q0": 10, "zT0": 10.5, "zT1": 11, "q1": 12, "logits": 13, "v1": 14, "prefix": 15}
        BOTH = list(UNIT_OF)
        NEEDS = {"q0": "xT1", "logits": "zT1", "out0": "oT1"}
        TURNED = ("xT", "zT")

        class Step:

            def __init__(self, name, bank, n, k, hi, bank_before, needs):
                self.name, self.unit, self.bank, self.n, self.k, self.hi = name, UNIT_OF[name], bank, n, k, hi
                self.kind, self.half = name.rstrip("01"), int(name[-1]) if name[-1].isdigit() else 0
                self.bank_before, self.needs = bank_before, needs

        def numbered(names, n0, turned0, own0, hi0):
            steps, turned, own, hi, at = [], turned0, own0, hi0, {}
            for i, name in enumerate(names):
                is_turned = name.rstrip("01") in TURNED
                before = steps[i - 2] if i > 1 else None
                bank_before = (before.kind in TURNED, before.k + 1) if before else (False, own0 - 1 + i)
                at[name] = (is_turned, (turned if is_turned else own) + 1)
                steps.append(Step(name, i % 2, n0 + i, turned if is_turned else own, hi, bank_before, at.get(NEEDS.get(name))))
                turned += is_turned
                own += not is_turned
                hi += name.rstrip("01") in ("oT", "q", "k", "v")
            return steps

        FIRST = numbered(PRE, 0, 0, 0, 0)
        LAST = numbered(POST, 16 * B - 8, 4 * B - 2, 12 * B - 6, 8 * B - 2)

        def steps_of(b):
            if isinstance(b, int) and b == 0:
                return numbered(PRE, 8, 2, 6, 6)
            names = POST if isinstance(b, int) and b == B - 1 else BOTH
            return numbered(names, b * 16, b * 4, b * 12, b * 8 + 4)

        def own_of(b, name):
            return [s.k for s in steps_of(b) if s.name == name][0] + 1

        def wait(eng, s, n):
            if not isinstance(n, int) or n > 0:
                eng.wait_ge(s, n)

        def settle(eng):
            eng.sem_inc(settled, 1)

        def over_batches(eng, body):
            body(0, 0)
            with eng.Fori(0, (B - 2) // 2) as i:
                body(i * 2 + 1, 1)
                body(i * 2 + 2, 0)
            body(B - 1, (B - 1) % 2)

        def over_tiles(eng, body):
            body(0, 0)
            with eng.Fori(0, (NT - 3) // 2) as i:
                body(i * 2 + 1, 1)
                body(i * 2 + 2, 0)

        PIECES = E * DC
        PIECE_BYTES = E * HC * D * 4 // PIECES
        AFTER_PRE, AFTER_EVEN = BEFORE_QKV // PIECE_BYTES, EARLY // PIECE_BYTES
        assert B % 2 == 0 and PIECES == 2 * B

        W1_UNITS = {False: (5, 13), True: (0, 1)}
        W2_FIRST_UNIT = 5

        def w2_piece(n, low):
            at = (n // 2) * 2 * HC * D + low * HC * D + (n % 2) * H
            return arena16[:, at:at + H]

        SMALL_LOADS = 11
        block = stack.enter_context(nc.Block())

        @block.sync
        def _(sp):
            sp.dma_start(x_in, x_v[0]).then_inc(x_loaded, 16)
            sp.dma_start(ctx_in[0:KVP], ctx_v[0]).then_inc(ctx_loaded, 16)
            sp.dma_start(stage[0][:, 0:512].rearrange("p (c n) -> p c n", c=DC), WqT.rearrange("(c p) n -> p c n", p=P)).then_inc(wqkvo_in[0], 16)
            sp.dma_start(stage[0][:, 512:1024].rearrange("p (c n) -> p c n", c=DC), WoT.rearrange("(c p) n -> p c n", p=P)).then_inc(wqkvo_in[0], 16)
            sp.dma_start(stage[1][0:KVP, 0:512].rearrange("p (c n) -> p c n", c=2), WkT.rearrange("(c p) n -> p c n", p=KVP)).then_inc(wqkvo_in[1], 16)
            sp.dma_start(stage[1][0:KVP, 512:1024].rearrange("p (c n) -> p c n", c=2), WvT.rearrange("(c p) n -> p c n", p=KVP)).then_inc(wqkvo_in[1], 16)
            sp.dma_start(gx[:, :], bc(g_xattn, P)).then_inc(small_in, 16)
            sp.dma_start(gf[:, :], bc(g_ffn, P)).then_inc(small_in, 16)
            sp.dma_start(tanh_bo[:, :], bc(bo, P)).then_inc(small_in, 16)
            sp.dma_start(rbias[:, :], bc(rb, P)).then_inc(small_in, 16)
            sp.dma_start(rls_s[:, :], rls).then_inc(small_in, 16)
            sp.dma_start(rlb_s[:, :], rlb).then_inc(small_in, 16)
            sp.dma_start(rw_raw[:, :, :], rwT.rearrange("(c p) e -> p c e", p=P)).then_inc(small_in, 16)
            sp.dma_start(els_s[:, :], els).then_inc(small_in, 16)
            sp.dma_start(elb_s[:, :], elb).then_inc(small_in, 16)
            sp.dma_start(b1_s[:, :], b1).then_inc(small_in, 16)
            sp.dma_start(b2_all[:, :, :].rearrange("p e d -> p (e d)"), bc(b2.rearrange("e d -> (e d)"), P)).then_inc(small_in, 16)
            sp.dma_start(x2, x_v[0]).then_inc(xres_loaded, 16)
            sp.wait_ge(side_done, 2)
            sp.dma_start(k_lh[0][0:64], k_hl[0][64:128]).then_inc(k_swapped, 16)
            sp.dma_start(k_lh[0][64:128], k_hl[0][0:64]).then_inc(k_swapped, 16)
            sp.wait_ge(pads_ready, 1)
            sp.dma_start(rows_dram[E * REGION:E * REGION + TILE, :].rearrange("(s p) n -> p s n", p=P), pad_rows[:, :, :]).then_inc(pads_sent, 16)
            sp.dma_start(acc_dram[T:T + TILE, :].rearrange("(s p) n -> p s n", p=P), pad_rows[:, :, 0:D]).then_inc(pads_sent, 16)

            def batch(b, par):
                if not (isinstance(b, int) and b == B - 1):
                    wait(sp, ln_done, b + 1)
                    settle(sp)
                    sp.dma_start(x_in, x_v[b + 1] if isinstance(b, int) else x_v[bass.ds(b + 1, 1)].rearrange("a p j d -> (a p) j d")).then_inc(x_loaded, 16)
                    sp.wait_ge(ctx_hi_done, b + 1)
                    sp.wait_ge(ctx_lo_done, b + 1)
                    settle(sp)
                    sp.dma_start(ctx_in[0:KVP], ctx_v[b + 1] if isinstance(b, int) else ctx_v[bass.ds(b + 1, 1)].rearrange("a p c s -> (a p) c s")).then_inc(ctx_loaded, 16)
                for s in range(2):
                    n = b * 2 + s
                    if isinstance(b, int) and b == 0:
                        sp.wait_ge(wqkvo_lo, 4)
                    else:
                        sp.wait_ge(stage_lo, n - 1)
                        settle(sp)
                    sp.dma_start(stage[s][:, :], w1_v[n] if isinstance(b, int) else w1_v[bass.ds(n, 1)].rearrange("a p h -> (a p) h")).then_inc(stage_in[s], 16)
                if not (isinstance(b, int) and b == B - 1):
                    swap_k(b + 1, 1 - par, own_of(b, "k1"))
                final = isinstance(b, int) and b == B - 1
                if final:
                    load_w2(0)
                    load_w2(1)
                if not (isinstance(b, int) and b == 0):
                    store_x2(b - 1)
                if final:
                    for n in range(2, 5):
                        load_w2(n)
                if not (isinstance(b, int) and b == 0):
                    sp.wait_ge(z_done, b)
                    settle(sp)
                    sp.wait_ge(x2_stored, 16 * b)
                    settle(sp)
                    sp.dma_start(x2, x_v[b] if isinstance(b, int) else x_v[bass.ds(b, 1)].rearrange("a p j d -> (a p) j d")).then_inc(xres_loaded, 16)

            def load_w2(n):
                if n < 2:
                    sp.wait_ge(stage_lo, PIECES - 1 + n)
                else:
                    sp.wait_ge(w2_lo_done, n - 1)
                sp.dma_start(stage[n % 2][:, :].rearrange("p (c d) -> p c d", d=D), w2_v[n]).then_inc(stage_in[n % 2], 16)

            def swap_k(b, par, n):
                sp.wait_ge(side_done, n)
                settle(sp)
                sp.dma_start(k_lh[par][0:64], k_hl[par][64:128]).then_inc(k_swapped, 16)
                sp.dma_start(k_lh[par][64:128], k_hl[par][0:64]).then_inc(k_swapped, 16)

            def store_x2(b):
                sp.wait_ge(z_stats, b + 1)
                settle(sp)
                sp.dma_start(acc_v[b] if isinstance(b, int) else acc_v[bass.ds(b, 1)].rearrange("a p j d -> (a p) j d"), x2).then_inc(x2_stored, 16)

            over_batches(sp, batch)
            for n in range(5, AFTER_EVEN + 2):
                load_w2(n)
            store_x2(B - 1)
            for n in range(AFTER_EVEN + 2, PIECES):
                load_w2(n)
            sp.wait_ge(tables, 2)
            for e in range(E):
                at = sp.value_load(pad_at[0:1, e:e + 1], min_val=e * REGION, max_val=e * REGION + T)
                sp.dma_start(rows_dram[bass.ds(at, TILE), :].rearrange("(s p) n -> p s n", p=P), pad_rows[:, :, :]).then_inc(pads_sent, 16)
            sp.wait_ge(pads_sent, 16 * (2 + E))
            sp.wait_ge(rows_sent, 16 * 2 * NT_TOK * B)

            def load_rows(j, par):
                at = sp.value_load(tile_row[0:1, j:j + 1] if isinstance(j, int) else tile_row[0:1, bass.ds(j, 1)], min_val=0, max_val=E * REGION)
                sp.dma_start(rows_r[par][:, :, :], rows_dram[bass.ds(at, TILE), :].rearrange("(s p) n -> p s n", p=P)).then_inc(rows_in[par], 16)

            load_rows(0, 0)
            load_rows(1, 1)

            def more_rows(j, par):
                sp.wait_ge(zT_mm, j + 1)
                sp.wait_ge(z_lo_done, j + 1)
                settle(sp)
                load_rows(j + 2, par)

            over_tiles(sp, more_rows)
            sp.wait_ge(x2_stored, 16 * B)
            sp.wait_ge(y_added, 16 * 2 * NT)
            sp.dma_start(out_v, acc_dram[0:T, :]).then_inc(out_stored, 16)
            sp.wait_ge(out_stored, 16)

        @block.gpsimd
        def _(pool):
            pool.memset(ident[:, :], 0.0).then_inc(const_pool, 1)
            pool.memset(before[:, :], 1.0).then_inc(const_pool, 1)
            pool.memset(pad_rows[:, :, :], 0.0).then_inc(const_pool, 1)
            pool.memset(half[:, :], -0.5).then_inc(const_pool, 1)
            pool.iota(code_i[:, :, :], pattern=[[0, NT_TOK], [-1, E]], base=E, channel_multiplier=0).then_inc(const_pool, 1)
            pool.iota(region_i[:, :], pattern=[[REGION, E]], base=0, channel_multiplier=0).then_inc(const_pool, 1)
            pool.iota(tok_i[:, :], pattern=[[P, T // P]], base=0, channel_multiplier=1).then_inc(const_pool, 1)
            pool.iota(tile_i[:, :], pattern=[[1, NT]], base=0, channel_multiplier=0).then_inc(const_pool, 1)
            pool.iota(pad_i[:, :], pattern=[[P, 2]], base=T, channel_multiplier=1).then_inc(const_pool, 1)
            pool.wait_ge(const_pool, 9)
            pool.affine_select(out=ident[:, :], in_=ident[:, :], compare_op=ALU.not_equal, fill=1.0, base=0,
                               pattern=[[-1, P]], channel_multiplier=1).then_inc(const_pool, 1)
            pool.affine_select(out=before[:, :], in_=before[:, :], compare_op=ALU.is_gt, fill=0.0, base=0,
                               pattern=[[1, P]], channel_multiplier=-1).then_inc(const_pool, 1)

            def link(s, count, ins):
                ins.then_inc(s, 1)
                pool.wait_ge(s, count)
                settle(pool)

            Z_STEPS = 6

            def scale_of_x(b):
                pool.wait_ge(ln_stats, b + 1)
                settle(pool)
                link(ln_step, b + 1, pool.tensor_scalar(rs[:, 0, :], mv[:, 0, :, 1], LN_EPS, None, ALU.add))
                pool.tensor_tensor(rs[:, 1, :], rs[:, 0, :], half[:, :], ALU.pow).then_inc(x_scale_ready, 1)

            def ctx_low(b):
                pool.wait_ge(ctx_hi_done, b + 1)
                pool.tensor_tensor(ctx_lo[0:KVP], ctx_in[0:KVP], ctx_hi[0:KVP], ALU.subtract).then_inc(ctx_lo_done, 1)

            def residual(b):
                pool.wait_ge(xres_loaded, 16 * (b + 1))
                pool.tensor_tensor(x2, x2, tanh_bo[:, :].unsqueeze(1).to_broadcast([P, NT_TOK, D]), ALU.add).then_inc(res_ready, 1)

            def scale_of_z(b):
                pool.wait_ge(z_stats, b + 1)
                settle(pool)
                c = b * Z_STEPS
                var = mv[:, 1, :, 1]
                link(z_step, c + 1, pool.tensor_scalar(rs[:, 2, :], var, LN_EPS, None, ALU.add))
                link(z_step, c + 2, pool.tensor_tensor(rs[:, 3, :], rs[:, 2, :], half[:, :], ALU.pow))
                link(z_step, c + 3, pool.tensor_tensor(rs[:, 4, :], rs[:, 3, :], rs[:, 3, :], ALU.mult))
                link(z_step, c + 4, pool.tensor_tensor(rs[:, 5, :], rs[:, 4, :], var, ALU.mult))
                link(z_step, c + 5, pool.tensor_scalar(rs[:, 5, :], rs[:, 5, :], LN2_EPS, None, ALU.add))
                link(z_step, c + 6, pool.tensor_tensor(rs[:, 6, :], rs[:, 5, :], half[:, :], ALU.pow))
                pool.tensor_tensor(rs[:, 7, :], rs[:, 3, :], rs[:, 6, :], ALU.mult).then_inc(z_scale_ready, 1)

            def w1_low(n, s):
                cols = slice(n * H, (n + 1) * H) if isinstance(n, int) else bass.ds(n * H, H)
                pool.wait_ge(stage_hi, n + 1)
                pool.tensor_tensor(w1_lo[:, cols], stage[s][:, :], w1_hi[:, cols], ALU.subtract).then_inc(stage_lo, 1)

            def scatter(b):
                pool.wait_ge(rows_ready, b + 1)
                settle(pool)
                for k in range(2):
                    for j in range(NT_TOK):
                        pool.indirect_dma_start(rows_dram[:, :], bass.IndirectOffsetOnAxis(ap=slot_i[:, k, j:j + 1], axis=0),
                                                rows_w[:, j, :], None).then_inc(rows_sent, 16)
                pool.wait_ge(rows_sent, (b + 1) * 2 * NT_TOK * 16)

            def turned_low(step):
                dst_hi, dst_lo = {"xT": (xT_hi, xT_lo), "zT": (zrT_hi, zrT_lo)}[step.kind]
                pool.wait_ge(turned_hi, step.k + 1)
                pool.wait_ge(turned_copied, step.k + 1)
                pool.tensor_tensor(dst_lo[:, step.half, :], turned[step.half], dst_hi[:, step.half, :], ALU.subtract).then_inc(turned_lo, 1)

            pool.wait_ge(gates_done, 1)
            ctx_low(0)
            scale_of_x(0)
            for step in FIRST:
                if step.kind in TURNED:
                    turned_low(step)
            residual(0)

            def batch(b, par):
                first, final = isinstance(b, int) and b == 0, isinstance(b, int) and b == B - 1
                if not final:
                    ctx_low(b + 1)
                    scale_of_x(b + 1)
                if final:
                    w1_low(b * 2, 0)
                    w1_low(b * 2 + 1, 1)
                if not first:
                    scale_of_z(b - 1)
                if not final:
                    w1_low(b * 2, 0)
                for step in steps_of(b):
                    if step.kind in TURNED:
                        turned_low(step)
                if not first:
                    residual(b)
                if not final:
                    w1_low(b * 2 + 1, 1)
                if not first:
                    scatter(b - 1)

            over_batches(pool, batch)
            scale_of_z(B - 1)
            for step in LAST:
                if step.kind in TURNED:
                    turned_low(step)
            scatter(B - 1)
            pool.wait_ge(x2_stored, 16 * B)

            def add_rows(j, par):
                pool.wait_ge(y_done, j + 1)
                if not isinstance(j, int) or j > 0:
                    pool.wait_ge(y_added, 32 * j)
                settle(pool)
                for s in range(2):
                    pool.indirect_dma_start(acc_dram[:, :], bass.IndirectOffsetOnAxis(ap=y_idx[par][:, s:s + 1], axis=0),
                                            y_out[par][:, s, :], None, compute_op=ALU.add).then_inc(y_added, 16)

            add_rows(0, 0)
            with pool.Fori(0, (NT - 1) // 2) as i:
                add_rows(i * 2 + 1, 1)
                add_rows(i * 2 + 2, 0)
            pool.wait_ge(y_added, 32 * NT)

        @block.scalar
        def _(act):
            act.wait_ge(small_in, 16 * SMALL_LOADS)
            act.activation(gx[:, :], gx[:, :], ACT.Tanh).then_inc(gates_tanh, 1)
            act.activation(gf[:, :], gf[:, :], ACT.Tanh).then_inc(gates_tanh, 1)

            def ctx_high(b):
                act.wait_ge(ctx_loaded, 16 * (b + 1))
                if not (isinstance(b, int) and b == 0):
                    act.wait_ge(side_mm, (b - 1) * 16 if not isinstance(b, int) else max((b - 1) * 16, 8))
                act.activation(ctx_hi[0:KVP], ctx_in[0:KVP], ACT.Copy).then_inc(ctx_hi_done, 1)

            def side(step, b, par):
                if step.kind in ("out", "logits", "prefix"):
                    return
                act.wait_ge(side_mm, step.n + 1)
                c, src = step.half, bank_m[step.bank]
                if step.kind in TURNED:
                    act.activation({"xT": xT_hi, "zT": zrT_hi}[step.kind][:, c, :], src, ACT.Copy).then_inc(turned_hi, 1)
                    wait(act, turned_lo, step.k - 1)
                    act.activation(turned[step.half], src, ACT.Copy).then_inc(turned_copied, 1)
                elif step.kind == "oT":
                    act.activation(oT_hi[:, c, :], src, ACT.Copy).then_inc(side_hi, 1)
                elif step.kind == "v":
                    act.activation(v_hi[par][:, 2 * c:2 * c + 2, :].rearrange("p j d -> p (j d)"), src, ACT.Copy, scale=1.0 / W_SCALE).then_inc(side_hi, 1)
                else:
                    dst, scale = (q_st[par], QSCALE / W_SCALE) if step.kind == "q" else (k_hl[par], 1.0 / W_SCALE)
                    act.activation(dst[0:64, 2 * c, :], src[0:64, :], ACT.Copy, scale=scale)
                    act.activation(dst[0:64, 2 * c + 1, :], src[64:128, :], ACT.Copy, scale=scale).then_inc(side_hi, 1)

            ctx_high(0)
            for st in FIRST:
                side(st, 0, 0)

            def w2_high(n):
                if n == 0:
                    act.wait_ge(ln_done, B)
                    act.wait_ge(ctx_lo_done, B)
                    act.wait_ge(side_mm, 16 * (B - 1))
                elif n == AFTER_PRE:
                    act.wait_ge(pv_mm, (B - 1) * UNITS)
                elif n == AFTER_EVEN:
                    act.wait_ge(pv_mm, B * UNITS)
                act.wait_ge(stage_in[n % 2], 16 * (PIECES // 2 + n // 2 + 1))
                act.activation(w2_piece(n, 0), stage[n % 2][:, :], ACT.Copy, scale=W_SCALE).then_inc(w2_hi_done, 1)

            def exponentials(b, u):
                g, t, j = b * UNITS + u, u % 2, u // HEADS
                act.wait_ge(max_done, g + 1)
                wait(act, pT_mm, g - 1)
                if u % HEADS == 0:
                    wait(act, on_done, b * NT_TOK + j - 1)
                act.activation(prob[t], bank_s[t], ACT.Exp, bias=neg_max[:, t:t + 1],
                               accum_out=p_sum[:, j % 2, u % HEADS:u % HEADS + 1]).then_inc(exp_done, 1)

            def batch(b, par):
                first, final = isinstance(b, int) and b == 0, isinstance(b, int) and b == B - 1
                for u in range(UNITS):
                    g, t = b * UNITS + u, u % 2
                    if u < UNITS - 1:
                        exponentials(b, u + 1)
                    elif not final:
                        exponentials(b + 1, 0)
                    act.wait_ge(pT_mm, g + 1)
                    wait(act, pv_mm, g - 1)
                    act.activation(pT_hi[t], bank_t[t], ACT.Copy).then_inc(pT_hi_done, 1)
                    for step in steps_of(b):
                        if int(step.unit) == u:
                            side(step, b - 1 if step.name in POST else b + 1, 1 - par)
                    if u == 0 and not final:
                        ctx_high(b + 1)
                    if u in W1_UNITS[final]:
                        s = W1_UNITS[final].index(u)
                        n = b * 2 + s
                        act.wait_ge(stage_in[s], b * 16 + 16)
                        act.activation(stage[s][:, :], stage[s][:, :], ACT.Copy, scale=W_SCALE).then_inc(stage_scaled, 1)
                        act.wait_ge(stage_scaled, n + 1)
                        act.activation(w1_hi[:, n * H:(n + 1) * H] if isinstance(n, int) else w1_hi[:, bass.ds(n * H, H)],
                                       stage[s][:, :], ACT.Copy).then_inc(stage_hi, 1)
                    if final and 0 <= u - W2_FIRST_UNIT < AFTER_EVEN:
                        w2_high(u - W2_FIRST_UNIT)
                    if u == 14 and not first:
                        gap(b - 1)

            def gap(b):
                act.wait_ge(gap_done, b + 1)
                act.activation(top[:, 5, :], top[:, 4, :], ACT.Exp).then_inc(gap_exp, 1)

            exponentials(0, 0)
            over_batches(act, batch)
            for i, step in enumerate(LAST):
                side(step, B - 1, (B - 1) % 2)
                if step.name in ("oT1", "zT1"):
                    for n in range(2):
                        w2_high(AFTER_EVEN + n + (0 if step.name == "oT1" else 2))
            gap(B - 1)
            for n in range(AFTER_EVEN + 4, PIECES):
                w2_high(n)

            act.wait_ge(tables, 2)

            def rows_high(j):
                act.wait_ge(z_aff_done, j + 1)
                act.activation(z_hi[:, :, :], z_aff[:, :, :], ACT.Copy).then_inc(z_hi_done, 1)

            def gelus(j):
                e = act.value_load(tile_expert[0:1, j:j + 1] if isinstance(j, int) else tile_expert[0:1, bass.ds(j, 1)], min_val=0, max_val=E - 1)
                for m in range(HC // 2):
                    act.wait_ge(h_mm, j * 4 + m + 1)
                    wait(act, h_lo_done, (j - 1) * 4 + m + 1)
                    for i in range(2):
                        hc = 2 * m + i
                        last = act.activation(hid[:, m, i * TILE:(i + 1) * TILE], bank_h[m][:, i * TILE:(i + 1) * TILE], ACT.Gelu,
                                              bias=b1_s[:, bass.ds(e * HC + hc, 1)], scale=1.0 / W_SCALE)
                    last.then_inc(gelu_done, 1)

            rows_high(0)
            gelus(0)
            rows_high(1)

            def tile(j):
                gelus(j + 1)
                rows_high(j + 2)

            with act.Fori(0, NT - 2) as i:
                tile(i)
            gelus(NT - 1)

        @block.tensor
        def _(pe):
            def products(dst, pairs, start=True, stop=True):
                for i, (a, b_) in enumerate(pairs):
                    last = pe.matmul(dst, a, b_, start=start and i == 0, stop=stop and i == len(pairs) - 1)
                return last

            def three(a_hi, a_lo, b_hi, b_lo):
                return [(a_hi, b_hi), (a_hi, b_lo), (a_lo, b_hi)]

            def side(step, b, par):
                dst, c, kind = bank_m[step.bank], step.half, step.kind
                from_turned, count = step.bank_before
                wait(pe, turned_copied if from_turned else side_done, count)
                if step.needs:
                    from_turned, count = step.needs
                    pe.wait_ge(turned_lo if from_turned else side_done, count)
                if kind in ("xT", "oT", "zT"):
                    if kind == "xT":
                        pe.wait_ge(ln_done, b + 1)
                        src = xn
                    elif kind == "oT":
                        pe.wait_ge(on_done, (b + 1) * NT_TOK)
                        src = o_n[par]
                    else:
                        pe.wait_ge(z_done, b + 1)
                        src = rows_w
                    for j in range(NT_TOK):
                        last = pe.transpose(dst[:, j * P:(j + 1) * P], src[:, j, c * P:(c + 1) * P], ident[:, :])
                elif kind in ("q", "k"):
                    if step.name == "k0":
                        pe.wait_ge(ctx_lo_done, b + 1)
                    if kind == "q":
                        w, a, rows = (wq_hi, wq_lo), (xT_hi, xT_lo), P
                    else:
                        w, a, rows = (wk_hi, wk_lo), (ctx_hi, ctx_lo), KVP
                    pairs = []
                    for k in range(2):
                        cols = slice(c * P, (c + 1) * P)
                        pairs += three(w[0][:, k, cols], w[1][:, k, cols], a[0][0:rows, k, :], a[1][0:rows, k, :])
                    last = products(dst, pairs)
                elif kind == "v":
                    for i in range(2):
                        toks = slice((2 * c + i) * P, (2 * c + i + 1) * P)
                        pairs = []
                        for k in range(2):
                            pairs += three(ctx_hi[0:KVP, k, toks], ctx_lo[0:KVP, k, toks], wv_hi[:, k, :], wv_lo[:, k, :])
                        last = products(dst[:, i * D:(i + 1) * D], pairs)
                elif kind == "out":
                    for i in range(2):
                        toks = slice((2 * c + i) * P, (2 * c + i + 1) * P)
                        pairs = []
                        for k in range(DC):
                            pairs += three(oT_hi[:, k, toks], oT_lo[:, k, toks], wo_hi[:, k, :], wo_lo[:, k, :])
                        last = products(dst[:, i * D:(i + 1) * D], pairs)
                elif kind == "logits":
                    for j in range(NT_TOK):
                        toks = slice(j * P, (j + 1) * P)
                        pairs = []
                        for k in range(DC):
                            pairs += three(zrT_hi[:, k, toks], zrT_lo[:, k, toks], rw_hi[:, k, :], rw_lo[:, k, :])
                        last = products(dst[:, j * E:(j + 1) * E], pairs)
                else:
                    pe.wait_ge(gap_done, b + 1)
                    for j in range(NT_TOK + 1):
                        pairs = [(ones[:, :], hot16[:, i, :]) for i in range(j)]
                        if j < NT_TOK:
                            pairs.append((before[:, :], hot16[:, j, :]))
                        last = products(dst[:, j * E:(j + 1) * E], pairs)
                last.then_inc(side_mm, 1)

            def scores(b, u, par):
                g, t, h, j = b * UNITS + u, u % 2, u % HEADS, u // HEADS
                wait(pe, exp_done, g - 1)
                if u == 0:
                    pe.wait_ge(k_swapped, 32 * (b + 1))
                q = q_st[par][:, h, j * P:(j + 1) * P]
                products(bank_s[t], [(q, k_hl[par][:, h, :]), (q, k_lh[par][:, h, :])]).then_inc(score_mm, 1)

            def turn(g, u):
                t = u % 2
                pe.wait_ge(exp_done, g + 1)
                wait(pe, pT_lo_done, g - 1)
                for k in range(S // P):
                    last = pe.transpose(bank_t[t][:, k * P:(k + 1) * P], prob[t][:, k * P:(k + 1) * P], ident[:, :])
                last.then_inc(pT_mm, 1)

            def weigh(g, u, par, b):
                t, h, j = u % 2, u % HEADS, u // HEADS
                if h == 0:
                    wait(pe, on_done, b * NT_TOK + j - 1)
                pe.wait_ge(pT_lo_done, g + 1)
                cols, pairs = slice(h * HD, (h + 1) * HD), []
                for k in range(S // P):
                    keys = slice(k * P, (k + 1) * P)
                    pairs += three(pT_hi[t][:, keys], pT_lo[t][:, keys], v_hi[par][:, k, cols], v_lo[par][:, k, cols])
                products(bank_o[j % 2][:, cols], pairs).then_inc(pv_mm, 1)

            pe.wait_ge(const_pool, 11)
            pe.wait_ge(const_dve, 1)
            for k in range(DC):
                last = pe.matmul(bank_s[0][:, 0:E], rlb_bc[:, k, :], rw_raw[:, k, :], start=k == 0, stop=k == DC - 1)
            last.then_inc(rbias_mm, 1)
            pe.wait_ge(wqkvo_lo, 4)
            for st in FIRST:
                side(st, 0, 0)
            pe.wait_ge(rbias_done, 1)
            pe.wait_ge(side_done, 6)
            scores(0, 0, 0)
            scores(0, 1, 0)

            def batch(b, par):
                first, final = isinstance(b, int) and b == 0, isinstance(b, int) and b == B - 1
                for u in range(UNITS):
                    g = b * UNITS + u
                    turn(g, u)
                    if u < UNITS - 2:
                        scores(b, u + 2, par)
                    elif not final:
                        if u == UNITS - 2:
                            pe.wait_ge(side_done, own_of(b, "q1"))
                        scores(b + 1, u + 2 - UNITS, 1 - par)
                    for step in steps_of(b):
                        if step.unit == u:
                            side(step, b - 1 if step.name in POST else b + 1, 1 - par)
                    if u > 0:
                        weigh(g - 1, u - 1, par, b)
                    elif not first:
                        weigh(g - 1, UNITS - 1, 1 - par, b - 1)
                    for step in steps_of(b):
                        if step.unit == u + 0.5:
                            side(step, b - 1 if step.name in POST else b + 1, 1 - par)

            over_batches(pe, batch)
            weigh(B * UNITS - 1, UNITS - 1, (B - 1) % 2, B - 1)
            for st in LAST:
                side(st, B - 1, (B - 1) % 2)

            def expert_of(j):
                return pe.value_load(tile_expert[0:1, j:j + 1] if isinstance(j, int) else tile_expert[0:1, bass.ds(j, 1)], min_val=0, max_val=E - 1)

            def rows_turn(j, par):
                pe.wait_ge(rows_in[par], (j // 2 + 1) * 16 if isinstance(j, int) else j * 8 + 16 - 8 * par)
                wait(pe, z_aff_done, j)
                for c in range(DC):
                    for s in range(2):
                        last = pe.transpose(bank_z[:, c * TILE + s * P:c * TILE + (s + 1) * P], rows_r[par][:, s, c * P:(c + 1) * P], ident[:, :])
                last.then_inc(zT_mm, 1)

            def hidden(j, e):
                pe.wait_ge(z_lo_done, j + 1)
                for m in range(HC // 2):
                    wait(pe, gelu_done, (j - 1) * 4 + m + 1)
                    for i in range(2):
                        pairs = []
                        for c in range(DC):
                            at = e * (DC * H) + c * H + (2 * m + i) * P
                            pairs += three(w1_hi[:, bass.ds(at, P)], w1_lo[:, bass.ds(at, P)], z_hi[:, c, :], z_lo[:, c, :])
                        last = products(bank_h[m][:, i * TILE:(i + 1) * TILE], pairs)
                    last.then_inc(h_mm, 1)

            def back(j, e, par):
                wait(pe, y_done, j - 1)
                if isinstance(j, int) and j == 0:
                    pe.wait_ge(w2_lo_done, PIECES)
                pe.wait_ge(h_lo_done, j * 4 + 4)
                for s in range(2):
                    pairs = []
                    for hc in range(HC):
                        rows = slice(hc * TILE + s * P, hc * TILE + (s + 1) * P)
                        hi, lo = (bass.ds(e * (2 * HC * D) + low * HC * D + hc * D, D) for low in range(2))
                        pairs += three(h_hi[par][:, rows], h_lo[par][:, rows], arena16[:, hi], arena16[:, lo])
                    last = products(bank_y[par][:, s * D:(s + 1) * D], pairs)
                last.then_inc(y_mm, 1)

            pe.wait_ge(side_done, 12 * B)
            pe.wait_ge(tables, 2)
            pe.wait_ge(stage_lo, PIECES)
            rows_turn(0, 0)
            hidden(0, expert_of(0))
            rows_turn(1, 1)

            def tile(j, par):
                hidden(j + 1, expert_of(j + 1))
                rows_turn(j + 2, par)
                back(j, expert_of(j), par)

            over_tiles(pe, tile)
            hidden(NT - 1, expert_of(NT - 1))
            back(NT - 2, expert_of(NT - 2), (NT - 2) % 2)
            back(NT - 1, expert_of(NT - 1), (NT - 1) % 2)

        @block.vector
        def _(v):
            v.memset(ones[:, :], 1.0).then_inc(dve, 1)
            v.memset(one8[:, :], 1.0).then_inc(dve, 1)
            v.wait_ge(const_pool, 9)
            v.tensor_copy(code[:, :, :], code_i[:, :, :]).then_inc(dve, 1)
            v.tensor_copy(region_f[:, :], region_i[:, :]).then_inc(dve, 1)
            v.tensor_copy(base[:, :], region_i[:, :]).then_inc(dve, 1)
            v.tensor_copy(tok_f[:, :], tok_i[:, :]).then_inc(dve, 1)
            v.tensor_copy(tile_f[:, :], tile_i[:, :]).then_inc(dve, 1)
            v.tensor_copy(pad_rows[:, :, D + COL_TOKEN], pad_i[:, :]).then_inc(pads_ready, 1)
            v.wait_ge(small_in, 16 * SMALL_LOADS)
            for k in range(DC):
                v.tensor_copy(rlb_bc[:, k, :], rlb_s[:, k:k + 1].to_broadcast([P, P])).then_inc(dve, 1)
                v.tensor_scalar(rw_sc[:, k, :], rw_raw[:, k, :], rls_s[:, k:k + 1], W_SCALE, ALU.mult, ALU.mult).then_inc(dve, 1)
            v.wait_ge(dve, 11)
            v.tensor_copy(rw_hi[:, :, :], rw_sc[:, :, :]).then_inc(dve, 1)
            v.wait_ge(dve, 12)
            v.tensor_tensor(rw_lo[:, :, :], rw_sc[:, :, :], rw_hi[:, :, :], ALU.subtract).then_inc(const_dve, 1)
            v.wait_ge(gates_tanh, 2)
            v.tensor_scalar(gxw[:, :], gx[:, :], 1.0 / W_SCALE, None, ALU.mult).then_inc(dve, 1)
            v.tensor_scalar(tanh_bo[:, :], tanh_bo[:, :], gx[:, 0:1], None, ALU.mult).then_inc(gates_done, 1)

            def x_stats(b):
                v.wait_ge(x_loaded, 16 * (b + 1))
                wait(v, ln_done, b)
                for j in range(NT_TOK):
                    last = v.bn_stats(stats[:, 0, j, :], x_in[:, j, :])
                last.then_inc(x_bn, 1)
                v.wait_ge(x_bn, b + 1)
                settle(v)
                for j in range(NT_TOK):
                    last = v.bn_aggr(mv[:, 0, j, :], stats[:, 0, j, :])
                last.then_inc(ln_stats, 1)

            def normalise_x(b):
                v.wait_ge(x_scale_ready, b + 1)
                settle(v)
                for j in range(NT_TOK):
                    last = v.tensor_scalar(xn[:, j, :], x_in[:, j, :], mv[:, 0, j, 0:1], rs[:, 1, j:j + 1], ALU.subtract, ALU.mult)
                last.then_inc(ln_done, 1)

            def normalise_z(b):
                v.wait_ge(z_scale_ready, b + 1)
                settle(v)
                for j in range(NT_TOK):
                    last = v.tensor_scalar(rows_w[:, j, 0:D], x2[:, j, :], mv[:, 1, j, 0:1], rs[:, 7, j:j + 1], ALU.subtract, ALU.mult)
                last.then_inc(z_done, 1)

            def z_statistics(b, n):
                v.wait_ge(side_done, n + 1)
                for j in range(NT_TOK):
                    last = v.bn_stats(stats[:, 1, j, :], x2[:, j, :])
                last.then_inc(z_bn, 1)
                v.wait_ge(z_bn, b + 1)
                settle(v)
                for j in range(NT_TOK):
                    last = v.bn_aggr(mv[:, 1, j, :], stats[:, 1, j, :])
                last.then_inc(z_stats, 1)

            v.wait_ge(dve, 13)
            x_stats(0)
            normalise_x(0)
            for i, (hi, lo, src) in enumerate([
                    (wq_hi, wq_lo, stage[0][:, 0:512]), (wo_hi, wo_lo, stage[0][:, 512:1024]),
                    (wk_hi, wk_lo, stage[1][0:KVP, 0:512]), (wv_hi, wv_lo, stage[1][0:KVP, 512:1024])]):
                v.wait_ge(wqkvo_in[i // 2], 32)
                v.tensor_scalar(hi[:, :, :].rearrange("p c n -> p (c n)"), src, W_SCALE, None, ALU.mult).then_inc(wqkvo_hi, 1)
                v.wait_ge(wqkvo_hi, i + 1)
                v.scalar_tensor_tensor(out=lo[:, :, :].rearrange("p c n -> p (c n)"), in0=src, scalar=W_SCALE,
                                       in1=hi[:, :, :].rearrange("p c n -> p (c n)"), op0=ALU.mult, op1=ALU.subtract).then_inc(wqkvo_lo, 1)
            v.wait_ge(rbias_mm, 1)
            v.tensor_tensor(rbias[:, :], bank_s[0][:, 0:E], rbias[:, :], ALU.add).then_inc(rbias_done, 1)

            CHAIN = 19

            def chained(c, ins):
                ins.then_inc(chain, 1)
                v.wait_ge(chain, c)

            def route(b, step):
                c = b * CHAIN
                v.wait_ge(side_mm, step.n + 1)
                shape = [P, NT_TOK, E]
                v.scalar_tensor_tensor(out=logit[:, :, :], in0=bank_m[step.bank][:, 0:NT_TOK * E].rearrange("p (j e) -> p j e", j=NT_TOK),
                                       scalar=1.0 / W_SCALE, in1=rbias[:, :].unsqueeze(1).to_broadcast(shape),
                                       op0=ALU.mult, op1=ALU.add).then_inc(side_done, 1)
                v.wait_ge(side_done, step.k + 1)
                for k, (src, hot) in enumerate([(logit, hot1), (logit2, hot2)]):
                    at = c + k * 5
                    chained(at + 1, v.tensor_reduce(top[:, 2 * k, :], src[:, :, :], AX.X, ALU.max))
                    chained(at + 2, v.tensor_tensor(tmp8[:, :, :], src[:, :, :], top[:, 2 * k, :].unsqueeze(2).to_broadcast(shape), ALU.is_equal))
                    chained(at + 3, v.tensor_tensor(tmp8[:, :, :], tmp8[:, :, :], code[:, :, :], ALU.mult))
                    chained(at + 4, v.tensor_reduce(top[:, 2 * k + 1, :], tmp8[:, :, :], AX.X, ALU.max))
                    chained(at + 5, v.tensor_tensor(hot[:, :, :], code[:, :, :], top[:, 2 * k + 1, :].unsqueeze(2).to_broadcast(shape), ALU.is_equal))
                    if k == 0:
                        v.scalar_tensor_tensor(out=logit2[:, :, :], in0=hot1[:, :, :], scalar=FAR_BELOW, in1=logit[:, :, :],
                                               op0=ALU.mult, op1=ALU.add).then_inc(masked, 1)
                        v.wait_ge(masked, b + 1)
                v.tensor_tensor(top[:, 4, :], top[:, 2, :], top[:, 0, :], ALU.subtract).then_inc(gap_sub, 1)
                v.wait_ge(gap_sub, b + 1)
                v.tensor_tensor(hot16[:, :, :], hot1[:, :, :], hot2[:, :, :], ALU.add).then_inc(gap_done, 1)

            def slots(b, step):
                c = b * CHAIN + 10
                shape = [P, NT_TOK, E]
                v.wait_ge(z_done, b + 1)
                v.wait_ge(gap_exp, b + 1)
                chained(c + 1, v.tensor_scalar(top[:, 6, :], top[:, 5, :], 1.0, None, ALU.add))
                chained(c + 2, v.reciprocal(top[:, 6, :], top[:, 6, :]))
                chained(c + 3, v.tensor_scalar(top[:, 6, :], top[:, 6, :], gf[:, 0:1], None, ALU.mult))
                chained(c + 4, v.tensor_tensor(rows_w[:, :, D + COL_G2], top[:, 6, :], top[:, 5, :], ALU.mult))
                v.tensor_tensor(rows_w[:, :, D + COL_DG], top[:, 6, :], rows_w[:, :, D + COL_G2], ALU.subtract)
                v.tensor_copy(rows_w[:, :, D + COL_E1], top[:, 1, :])
                v.tensor_copy(rows_w[:, :, D + COL_TOKEN], tok_f[:, b * NT_TOK:(b + 1) * NT_TOK] if isinstance(b, int) else tok_f[:, bass.ds(b * NT_TOK, NT_TOK)])
                v.wait_ge(side_mm, step.n + 1)
                chained(c + 5, v.tensor_tensor(place[:, :, :], bank_m[step.bank][:, 0:NT_TOK * E].rearrange("p (j e) -> p j e", j=NT_TOK),
                                               base[:, :].unsqueeze(1).to_broadcast(shape), ALU.add))
                v.tensor_tensor(base[:, :], bank_m[step.bank][:, NT_TOK * E:(NT_TOK + 1) * E], base[:, :], ALU.add).then_inc(side_done, 1)
                chained(c + 6, v.tensor_tensor(tmp8[:, :, :], hot1[:, :, :], place[:, :, :], ALU.mult))
                chained(c + 7, v.tensor_reduce(slot_f[:, 0, :], tmp8[:, :, :], AX.X, ALU.add))
                chained(c + 8, v.tensor_tensor(tmp8[:, :, :], hot2[:, :, :], place[:, :, :], ALU.mult))
                chained(c + 9, v.tensor_reduce(slot_f[:, 1, :], tmp8[:, :, :], AX.X, ALU.add))
                v.tensor_copy(slot_i[:, :, :], slot_f[:, :, :]).then_inc(rows_ready, 1)

            def side(step, b, par):
                src, c, kind = bank_m[step.bank], step.half, step.kind
                if kind in TURNED:
                    return
                if kind == "logits":
                    return route(b, step)
                if kind == "prefix":
                    return slots(b, step)
                if kind == "out":
                    v.wait_ge(side_mm, step.n + 1)
                    v.wait_ge(res_ready, b + 1)
                    half_of = x2[:, 2 * c:2 * c + 2, :].rearrange("p j d -> p (j d)")
                    v.scalar_tensor_tensor(out=half_of, in0=src, scalar=gxw[:, 0:1], in1=half_of, op0=ALU.mult, op1=ALU.add).then_inc(side_done, 1)
                    return
                v.wait_ge(side_hi, step.hi + 1)
                if kind == "oT":
                    v.tensor_tensor(oT_lo[:, c, :], src, oT_hi[:, c, :], ALU.subtract).then_inc(side_done, 1)
                elif kind == "v":
                    h, l = (t[par][:, 2 * c:2 * c + 2, :].rearrange("p j d -> p (j d)") for t in (v_hi, v_lo))
                    v.scalar_tensor_tensor(out=l, in0=src, scalar=1.0 / W_SCALE, in1=h, op0=ALU.mult, op1=ALU.subtract).then_inc(side_done, 1)
                else:
                    dst, scale = (q_st[par], QSCALE / W_SCALE) if kind == "q" else (k_hl[par], 1.0 / W_SCALE)
                    for i in range(2):
                        last = v.scalar_tensor_tensor(out=dst[64:128, 2 * c + i, :], in0=src[64 * i:64 * i + 64, :], scalar=scale,
                                                      in1=dst[0:64, 2 * c + i, :], op0=ALU.mult, op1=ALU.subtract)
                    last.then_inc(side_done, 1)

            for st in FIRST:
                side(st, 0, 0)

            def batch(b, par):
                first, final = isinstance(b, int) and b == 0, isinstance(b, int) and b == B - 1
                for u in range(UNITS):
                    g, t = b * UNITS + u, u % 2
                    if not (final and u >= UNITS - 2):
                        row_max(g + 2, t)
                    v.wait_ge(pT_hi_done, g + 1)
                    v.tensor_tensor(pT_lo[t], bank_t[t], pT_hi[t], ALU.subtract).then_inc(pT_lo_done, 1)
                    if u % HEADS == 0 and u > 0:
                        normalise(b, u // HEADS - 1, par)
                    elif u == 0 and not first:
                        normalise(b - 1, NT_TOK - 1, 1 - par)
                    if final and 0 <= u - W2_FIRST_UNIT < AFTER_EVEN:
                        w2_low(u - W2_FIRST_UNIT)
                    if u == 0 and not final:
                        x_stats(b + 1)
                    if u == 7 and not final:
                        normalise_x(b + 1)
                    if u == 8 and not first:
                        normalise_z(b - 1)
                    for step in steps_of(b):
                        if int(step.unit) == u:
                            side(step, b - 1 if step.name in POST else b + 1, 1 - par)
                            if step.name == "out1":
                                z_statistics(b - 1, step.k)

            def w2_low(n):
                v.wait_ge(w2_hi_done, n + 1)
                v.scalar_tensor_tensor(out=w2_piece(n, 1), in0=stage[n % 2][:, :], scalar=W_SCALE, in1=w2_piece(n, 0),
                                       op0=ALU.mult, op1=ALU.subtract).then_inc(w2_lo_done, 1)

            def row_max(g, t):
                v.wait_ge(score_mm, g + 1)
                wait(v, exp_done, g - 1)
                v.tensor_reduce(neg_max[:, t:t + 1], bank_s[t], AX.X, ALU.max, negate=True).then_inc(max_done, 1)

            def normalise(b, j, par):
                n = b * NT_TOK + j
                v.wait_ge(pv_mm, (n + 1) * HEADS)
                wait(v, on_done, n)
                v.reciprocal(p_inv[:, :], p_sum[:, j % 2, :]).then_inc(inv_done, 1)
                v.wait_ge(inv_done, n + 1)
                v.tensor_tensor(o_n[par][:, j, :].rearrange("p (h d) -> p h d", h=HEADS),
                                bank_o[j % 2][:, 0:D].rearrange("p (h d) -> p h d", h=HEADS),
                                p_inv[:, :].unsqueeze(2).to_broadcast([P, HEADS, HD]), ALU.mult).then_inc(on_done, 1)

            row_max(0, 0)
            row_max(1, 1)
            over_batches(v, batch)
            normalise(B - 1, NT_TOK - 1, (B - 1) % 2)
            for step in LAST:
                side(step, B - 1, (B - 1) % 2)
                if step.name == "out1":
                    z_statistics(B - 1, step.k)
                    w2_low(AFTER_EVEN)
                    w2_low(AFTER_EVEN + 1)
                    normalise_z(B - 1)
                if step.name == "logits":
                    w2_low(AFTER_EVEN + 2)
                    w2_low(AFTER_EVEN + 3)

            t0 = B * CHAIN
            links = iter(range(t0 + 1, t0 + 100))
            v.wait_ge(side_done, 12 * B)
            v.tensor_copy(pad_at[:, :], base[:, :]).then_inc(tables, 1)
            chained(next(links), v.tensor_tensor(cnt_f[:, :], base[:, :], region_f[:, :], ALU.subtract))
            chained(next(links), v.tensor_scalar(cnt_i[:, :], cnt_f[:, :], float(TILE - 1), None, ALU.add))
            chained(next(links), v.tensor_scalar(cnt_i[:, :], cnt_i[:, :], TILE.bit_length() - 1, None, ALU.arith_shift_right))
            chained(next(links), v.tensor_copy(cnt_f[:, :], cnt_i[:, :]))
            chained(next(links), v.tensor_tensor_scan(cum[:, :], one8[:, :], cnt_f[:, :], 0.0, ALU.mult, ALU.add))
            shape = [P, NT, E]
            chained(next(links), v.tensor_tensor(past[:, :, :], tile_f[:, :].unsqueeze(2).to_broadcast(shape),
                                                 cum[:, :].unsqueeze(1).to_broadcast(shape), ALU.is_ge))
            chained(next(links), v.tensor_tensor(past_n[:, :, :], past[:, :, :], cnt_f[:, :].unsqueeze(1).to_broadcast(shape), ALU.mult))
            chained(next(links), v.tensor_reduce(tab[:, 0, :], past[:, :, :], AX.X, ALU.add))
            chained(next(links), v.tensor_reduce(tab[:, 1, :], past_n[:, :, :], AX.X, ALU.add))
            chained(next(links), v.tensor_tensor(tab[:, 1, :], tile_f[:, :], tab[:, 1, :], ALU.subtract))
            chained(next(links), v.tensor_scalar(tab[:, 2, :], tab[:, 0, :], float(E), float(TILE), ALU.is_lt, ALU.mult))
            chained(next(links), v.tensor_tensor(tab[:, 1, :], tab[:, 1, :], tab[:, 2, :], ALU.mult))
            chained(next(links), v.tensor_scalar(tile_expert[:, :], tab[:, 0, :], float(E - 1), None, ALU.min))
            v.scalar_tensor_tensor(out=tile_row[:, :], in0=tab[:, 0, :], scalar=float(REGION), in1=tab[:, 1, :],
                                   op0=ALU.mult, op1=ALU.add).then_inc(tables, 1)
            v.wait_ge(tables, 2)
            for n in range(AFTER_EVEN + 4, PIECES):
                w2_low(n)

            def expert_of(j):
                return v.value_load(tile_expert[0:1, j:j + 1] if isinstance(j, int) else tile_expert[0:1, bass.ds(j, 1)], min_val=0, max_val=E - 1)

            def rows_split(j, par, e):
                v.wait_ge(zT_mm, j + 1)
                wait(v, z_hi_done, j)
                for c in range(DC):
                    col = bass.ds(e * DC + c, 1)
                    last = v.tensor_scalar(z_aff[:, c, :], bank_z[:, c * TILE:(c + 1) * TILE], els_s[:, col], elb_s[:, col], ALU.mult, ALU.add)
                last.then_inc(z_aff_done, 1)
                v.tensor_copy(extras[:, j if isinstance(j, int) else bass.ds(j, 1), :, :] if isinstance(j, int) else
                              extras[:, bass.ds(j, 1), :, :].rearrange("p a s n -> p (a s) n"), rows_r[par][:, :, D:ROW])
                v.wait_ge(z_hi_done, j + 1)
                v.tensor_tensor(z_lo[:, :, :], z_aff[:, :, :], z_hi[:, :, :], ALU.subtract).then_inc(z_lo_done, 1)

            def split_hidden(j, par):
                wait(v, y_mm, j - 1)
                for m in range(HC // 2):
                    cols = slice(m * 2 * TILE, (m + 1) * 2 * TILE)
                    v.wait_ge(gelu_done, j * 4 + m + 1)
                    v.tensor_copy(h_hi[par][:, cols], hid[:, m, :]).then_inc(h_hi_done, 1)
                    v.wait_ge(h_hi_done, j * 4 + m + 1)
                    v.tensor_tensor(h_lo[par][:, cols], hid[:, m, :], h_hi[par][:, cols], ALU.subtract).then_inc(h_lo_done, 1)

            def finish_rows(j, par, e):
                mine = extras[:, j, :, :] if isinstance(j, int) else extras[:, bass.ds(j, 1), :, :].rearrange("p a s n -> p (a s) n")
                wait(v, y_added, 32 * (j - 1))
                wait(v, y_done, j)
                v.tensor_copy(y_idx[par][:, :], mine[:, :, COL_TOKEN])
                v.scalar_tensor_tensor(out=gate[:, :], in0=mine[:, :, COL_E1], scalar=code[:, 0, bass.ds(e, 1)], in1=mine[:, :, COL_DG],
                                       op0=ALU.is_equal, op1=ALU.mult).then_inc(gate_step, 1)
                v.wait_ge(gate_step, j * 3 + 1)
                v.tensor_tensor(gate[:, :], gate[:, :], mine[:, :, COL_G2], ALU.add).then_inc(gate_step, 1)
                v.wait_ge(y_mm, j + 1)
                v.scalar_tensor_tensor(out=y_out[par][:, :, :], in0=bank_y[par][:, :].rearrange("p (s d) -> p s d", s=2), scalar=1.0 / W_SCALE,
                                       in1=b2_all[:, bass.ds(e, 1), :].to_broadcast([P, 2, D]), op0=ALU.mult, op1=ALU.add).then_inc(gate_step, 1)
                v.wait_ge(gate_step, j * 3 + 3)
                for s in range(2):
                    last = v.tensor_scalar(y_out[par][:, s, :], y_out[par][:, s, :], gate[:, s:s + 1], None, ALU.mult)
                last.then_inc(y_done, 1)

            rows_split(0, 0, expert_of(0))
            split_hidden(0, 0)
            rows_split(1, 1, expert_of(1))

            def tile(j, par):
                split_hidden(j + 1, 1 - par)
                rows_split(j + 2, par, expert_of(j + 2))
                finish_rows(j, par, expert_of(j))

            over_tiles(v, tile)
            split_hidden(NT - 1, (NT - 1) % 2)
            finish_rows(NT - 2, (NT - 2) % 2, expert_of(NT - 2))
            finish_rows(NT - 1, (NT - 1) % 2, expert_of(NT - 1))


_OUT_SHAPE = (8, 512, 256)


def kernel(**inputs):
    import numpy as np
    import concourse.bacc as bacc
    from concourse.bass_utils import run_bass_kernel_spmd

    def a(name):
        return np.asarray(inputs[name])

    E = a("L0_ffn_w1").shape[0]
    arrays = {
        "x": a("x"),
        "ctxT": a("ctx_768").transpose(0, 2, 1),
        "g_xattn": a("g_xattn"),
        "g_ffn": a("g_ffn"),
        "WqT": a("L0_xattn_Wq").T,
        "WkT": a("L0_xattn_Wk").T,
        "WvT": a("L0_xattn_Wv").T,
        "WoT": a("L0_xattn_Wo").T,
        "bo": a("L0_xattn_bo"),
        "rls": a("L0_ffn_router_ln_scale").reshape(-1, 128).T,
        "rlb": a("L0_ffn_router_ln_bias").reshape(-1, 128).T,
        "rwT": a("L0_ffn_router_w").T,
        "rb": a("L0_ffn_router_b"),
        "els": a("L0_ffn_expert_ln_scale").reshape(-1, 128).T,
        "elb": a("L0_ffn_expert_ln_bias").reshape(-1, 128).T,
        "w1T": a("L0_ffn_w1").transpose(0, 2, 1),
        "b1": a("L0_ffn_b1").reshape(-1, 128).T,
        "w2T": a("L0_ffn_w2").transpose(0, 2, 1),
        "b2": a("L0_ffn_b2"),
    }
    nc = bacc.Bacc("TRN2", target_bir_lowering=False, num_devices=1)
    maps, args = {}, []
    for name, value in arrays.items():
        value = np.ascontiguousarray(value)
        maps[f"in_{name}"] = value
        args.append(nc.dram_tensor(f"in_{name}", value.shape, mybir.dt.from_np(value.dtype), kind="ExternalInput").ap())
    out = nc.dram_tensor("out", _OUT_SHAPE, F32, kind="ExternalOutput").ap()
    build(nc, *args, out)
    r = run_bass_kernel_spmd(nc, [maps], core_ids=[0])
    return r.results[0]["out"]
```

```python
from contextlib import ExitStack

import concourse.bass as bass
from concourse import mybir

ALU = mybir.AluOpType
ACT = mybir.ActivationFunctionType
AX = mybir.AxisListType
F32 = mybir.dt.float32
F16 = mybir.dt.float16
I32 = mybir.dt.int32

P = 128
W_SCALE = 64.0
LN_EPS, LN2_EPS = 1e-5, 1e-6
FAR_BELOW = -3.0e38
TILE = 256
SCALAR_HIGH = (1, 2)
EARLY_TILES, SINGLE_TILES = 5, 3
ROW_EXTRA = 4
COL_TOKEN, COL_G2, COL_DG, COL_E1 = range(4)


def build(nc, x, ctxT, g_xattn, g_ffn, WqT, WkT, WvT, WoT, bo, rls, rlb, rwT, rb, els, elb, w1T, b1, w2T, b2, out):
    B, S, D = x.shape
    DKV = ctxT.shape[1]
    E, _, H = w1T.shape
    HEADS, HD = 4, D // 4
    T = B * S
    NT_TOK = S // P
    DC = D // P
    KVP = DKV // 2
    HC = H // P
    NT = (2 * T) // TILE + E - 1
    REGION = T + TILE
    ROW = D + ROW_EXTRA
    UNITS = NT_TOK * HEADS
    QSCALE = float(HD) ** -0.5
    assert D == 256 and S == 512 and HD == 64 and H == 1024 and UNITS == 16 and HEADS == 4

    x_v = x.rearrange("b (j p) d -> b p j d", p=P)
    out_v = out.rearrange("b s d -> (b s) d")
    ctx_v = ctxT.rearrange("b (c p) s -> b p c s", p=KVP)
    w1_v = w1T.rearrange("e (c p) h -> (e c) p h", p=P)
    w2_v = w2T.rearrange("e (s c p) d -> (e s) p c d", p=P, s=2)
    rows_dram = nc.dram_tensor("expert_rows", (E * REGION + TILE, ROW), F32, kind="Internal").ap()
    acc_dram = nc.dram_tensor("acc_rows", (T + TILE, D), F32, kind="Internal").ap()
    acc_v = acc_dram[0:T, :].rearrange("(b j p) d -> b p j d", p=P, j=NT_TOK)

    def bc(ap1, n):
        return ap1.rearrange("(a d) -> a d", a=1).to_broadcast([n, ap1.shape[0]])

    with ExitStack() as stack:

        def sb(name, shape, dt=F32):
            return stack.enter_context(nc.sbuf_tensor(name, shape, dt))

        def sem(name):
            return stack.enter_context(nc.semaphore(name))

        w1_hi, w1_lo = sb("w1_hi", [P, E * DC * H], F16), sb("w1_lo", [P, E * DC * H], F16)
        arena = sb("arena", [P, E * HC * D])
        arena16 = arena[:, :].bitcast(F16)
        used = [0]

        def take(n_bytes, dt=F32):
            at = used[0]
            used[0] += n_bytes
            assert used[0] <= E * HC * D * 4
            v = arena[:, at // 4:(at + n_bytes) // 4]
            return v if dt is F32 else v.bitcast(dt)

        def heads_of():
            return take(HEADS * S * 2, F16).rearrange("p (h s) -> p h s", h=HEADS)

        def qkv():
            return [heads_of() for _ in range(3)] + [take(NT_TOK * D * 2, F16).rearrange("p (j d) -> p j d", j=NT_TOK) for _ in range(2)]

        x_in = take(NT_TOK * D * 4).rearrange("p (j d) -> p j d", j=NT_TOK)
        ctx_in = take(2 * S * 4).rearrange("p (c s) -> p c s", c=2)
        ctx_hi = take(2 * S * 2, F16).rearrange("p (c s) -> p c s", c=2)
        ctx_lo = take(2 * S * 2, F16).rearrange("p (c s) -> p c s", c=2)
        xT_hi = take(DC * S * 2, F16).rearrange("p (c s) -> p c s", c=DC)
        xT_lo = take(DC * S * 2, F16).rearrange("p (c s) -> p c s", c=DC)
        BEFORE_QKV = used[0]
        qkv_even = qkv()
        two_hi, two_lo = ({kind: take(2 * S * 2, F16).rearrange("p (c s) -> p c s", c=2) for kind in "qk"} for _ in range(2))
        EARLY = used[0]
        qkv_odd = qkv()
        q_st, k_hl, k_lh, v_hi, v_lo = zip(qkv_even, qkv_odd)
        prob = [take(S * 4) for _ in range(2)]
        pT_hi = [take(S * 2, F16) for _ in range(2)]
        pT_lo = [take(S * 2, F16) for _ in range(2)]

        late = sb("late", [P, 6144])
        xn = late[:, 0:1024].rearrange("p (j d) -> p j d", j=NT_TOK)
        o_n = [late[:, 1024 * (1 + i):1024 * (2 + i)].rearrange("p (j d) -> p j d", j=NT_TOK) for i in range(2)]
        oT_hi = late[:, 3072:3584].bitcast(F16).rearrange("p (c s) -> p c s", c=DC)
        oT_lo = late[:, 3584:4096].bitcast(F16).rearrange("p (c s) -> p c s", c=DC)
        zrT_hi = late[:, 4096:4608].bitcast(F16).rearrange("p (c s) -> p c s", c=DC)
        zrT_lo = late[:, 4608:5120].bitcast(F16).rearrange("p (c s) -> p c s", c=DC)
        x2 = late[:, 5120:6144].rearrange("p (j d) -> p j d", j=NT_TOK)
        hid = late[:, 0:2048].rearrange("p (m n) -> p m n", n=2 * TILE)
        h_hi = [late[:, 2048 + 2048 * i:3072 + 2048 * i].bitcast(F16) for i in range(2)]
        h_lo = [late[:, 3072 + 2048 * i:4096 + 2048 * i].bitcast(F16) for i in range(2)]

        stage = [sb(f"stage{i}", [P, H]) for i in range(2)]
        wq_hi, wq_lo = sb("wq_hi", [P, DC, D], F16), sb("wq_lo", [P, DC, D], F16)
        wo_hi, wo_lo = sb("wo_hi", [P, DC, D], F16), sb("wo_lo", [P, DC, D], F16)
        wk_hi, wk_lo = sb("wk_hi", [KVP, 2, D], F16), sb("wk_lo", [KVP, 2, D], F16)
        wv_hi, wv_lo = sb("wv_hi", [KVP, 2, D], F16), sb("wv_lo", [KVP, 2, D], F16)
        rows_w = sb("rows_w", [P, NT_TOK, ROW])
        rows_r = [sb(f"rows_r{i}", [P, 2, ROW]) for i in range(2)]
        turned = [t[:, :, :].rearrange("p s n -> p (s n)")[:, 0:S] for t in rows_r]
        z_aff = sb("z_aff", [P, DC, TILE])
        z_hi, z_lo = sb("z_hi", [P, DC, TILE], F16), sb("z_lo", [P, DC, TILE], F16)
        y_out = [sb(f"y_out{i}", [P, 2, D]) for i in range(2)]
        y_idx = [sb(f"y_idx{i}", [P, 2], I32) for i in range(2)]
        b2_all = sb("b2_all", [P, E, D])
        tanh_bo = sb("tanh_bo", [P, D])
        extras = sb("extras", [P, NT, 2, ROW_EXTRA])
        gate = sb("gate", [P, 2])
        els_s, elb_s = sb("els_s", [P, E * DC]), sb("elb_s", [P, E * DC])
        b1_s = sb("b1_s", [P, E * HC])
        ident = sb("ident", [P, P])
        before = sb("before", [P, P], F16)
        ones = sb("ones", [P, P], F16)
        rlb_bc = sb("rlb_bc", [P, DC, P])
        rls_s, rlb_s = sb("rls_s", [P, DC]), sb("rlb_s", [P, DC])
        rw_raw, rw_sc = sb("rw_raw", [P, DC, E]), sb("rw_sc", [P, DC, E])
        rw_hi, rw_lo = sb("rw_hi", [P, DC, E], F16), sb("rw_lo", [P, DC, E], F16)
        rbias = sb("rbias", [P, E])
        gx, gf, gxw = sb("gx", [P, 1]), sb("gf", [P, 1]), sb("gxw", [P, 1])
        stats = sb("stats", [P, 2, NT_TOK, 6])
        mv = sb("mv", [P, 2, NT_TOK, 2])
        rs = sb("rs", [P, 10, NT_TOK])
        half, minus = sb("half", [P, NT_TOK]), sb("minus", [P, NT_TOK])
        neg_max = sb("neg_max", [P, 2])
        p_sum, p_inv = sb("p_sum", [P, 2, HEADS]), sb("p_inv", [P, HEADS])
        code = sb("code", [P, NT_TOK, E])
        code_i = sb("code_i", [P, NT_TOK, E], I32)
        region_i, region_f = sb("region_i", [P, E], I32), sb("region_f", [P, E])
        base = sb("base", [P, E])
        tok_i, tok_f = sb("tok_i", [P, T // P], I32), sb("tok_f", [P, T // P])
        pad_i = sb("pad_i", [P, 2], I32)
        pad_rows = sb("pad_rows", [P, 2, ROW])
        logit, logit2 = sb("logit", [P, NT_TOK, E]), sb("logit2", [P, NT_TOK, E])
        hot1, hot2 = sb("hot1", [P, NT_TOK, E]), sb("hot2", [P, NT_TOK, E])
        hot16 = sb("hot16", [P, NT_TOK, E], F16)
        tmp8, tmp8b = sb("tmp8", [P, NT_TOK, E]), sb("tmp8b", [P, NT_TOK, E])
        top = sb("top", [P, 8, NT_TOK])
        place = sb("place", [P, NT_TOK, E])
        slot_f, slot_i = sb("slot_f", [P, 2, NT_TOK]), sb("slot_i", [P, 2, NT_TOK], I32)
        tile_i, tile_f = sb("tile_i", [P, NT], I32), sb("tile_f", [P, NT])
        cnt_i, cnt_f = sb("cnt_i", [P, E], I32), sb("cnt_f", [P, E])
        cum, one8 = sb("cum", [P, E]), sb("one8", [P, E])
        past, past_n = sb("past", [P, NT, E]), sb("past_n", [P, NT, E])
        tab = sb("tab", [P, 4, NT])
        left, weight = sb("left", [P, E]), sb("weight", [P, E])
        taken, taken_step = sb("taken", [P, E]), sb("taken_step", [P, E])
        tile_expert, tile_row = sb("tile_expert", [P, NT], I32), sb("tile_row", [P, NT], I32)
        pad_at = sb("pad_at", [P, E], I32)

        psum = stack.enter_context(nc.psum_tensor("psum", [P, 8, 512], F32))
        bank_s = [psum[:, i, :] for i in (0, 1)]
        bank_t = [psum[:, i, :] for i in (2, 3)]
        bank_o = [psum[:, i, :] for i in (4, 5)]
        bank_m = [psum[:, i, :] for i in (6, 7)]
        bank_h = [psum[:, i, :] for i in (0, 1, 2, 3)]
        bank_y = [psum[:, i, :] for i in (4, 5)]
        bank_z = psum[:, 6, :]

        small_in, b2_in = sem("small_in"), sem("b2_in")
        proj_in = {name: sem(f"w{name}_in") for name in "kqvo"}
        x_loaded, ctx_loaded, xres_loaded = sem("x_loaded"), sem("ctx_loaded"), sem("xres_loaded")
        stage_in = [sem(f"stage_in{i}") for i in range(2)]
        const_pool, router_ready = sem("const_pool"), sem("router_ready")
        gates_done, gates_tanh, rbias_mm, rbias_done = sem("gates_done"), sem("gates_tanh"), sem("rbias_mm"), sem("rbias_done")
        proj_hi, proj_lo = sem("proj_hi"), sem("proj_lo")
        ln_stats, ln_done, ln_step = sem("ln_stats"), sem("ln_done"), sem("ln_step")
        ctx_hi_done, ctx_lo_done = sem("ctx_hi_done"), sem("ctx_lo_done")
        res_ready = sem("res_ready")
        side_mm, side_hi, side_done = sem("side_mm"), sem("side_hi"), sem("side_done")
        turned_hi, turned_copied, turned_lo = sem("turned_hi"), sem("turned_copied"), sem("turned_lo")
        score_mm, max_done, exp_done = sem("score_mm"), sem("max_done"), sem("exp_done")
        pT_mm, pT_hi_done, pT_lo_done, pv_mm = sem("pT_mm"), sem("pT_hi_done"), sem("pT_lo_done"), sem("pv_mm")
        on_done, q_placed, k_placed = sem("on_done"), sem("q_placed"), sem("k_placed")
        x_scale_ready, z_scale_ready = sem("x_scale_ready"), sem("z_scale_ready")
        x2_stored = sem("x2_stored")
        z_stats = sem("z_stats")
        z_done, z_step = sem("z_done"), sem("z_step")
        dve, chain = sem("dve"), sem("chain")
        masked, gap_sub, inv_done, gate_step = sem("masked"), sem("gap_sub"), sem("inv_done"), sem("gate_step")
        x_bn, z_bn = sem("x_bn"), sem("z_bn")
        gap_done, gap_exp = sem("gap_done"), sem("gap_exp")
        rows_ready, rows_sent = sem("rows_ready"), sem("rows_sent")
        stage_scaled, stage_hi, stage_lo = sem("stage_scaled"), sem("stage_hi"), sem("stage_lo")
        w2_hi_done, w2_lo_done = sem("w2_hi_done"), sem("w2_lo_done")
        pads_ready, pads_sent, tables = sem("pads_ready"), sem("pads_sent"), sem("tables")
        rows_in = [sem(f"rows_in{i}") for i in range(2)]
        zT_mm, z_aff_done, z_hi_done, z_lo_done = sem("zT_mm"), sem("z_aff_done"), sem("z_hi_done"), sem("z_lo_done")
        h_mm, gelu_done, h_hi_done, h_lo_done = sem("h_mm"), sem("gelu_done"), sem("h_hi_done"), sem("h_lo_done")
        plan_step = sem("plan_step")
        y_mm, y_done, y_added = sem("y_mm"), sem("y_done"), sem("y_added")
        out_stored = sem("out_stored")
        settled = sem("settled")

        PRE = ["xT0", "xT1", "k0", "k1", "q0", "q1", "v0", "v1"]
        POST = ["oT0", "oT1", "out0", "out1", "zT0", "zT1", "logits", "prefix"]
        UNIT_OF = {"oT0": 2, "oT1": 2.5, "out0": 3.5, "out1": 4.5, "xT0": 5.5, "xT1": 6, "k0": 7, "k1": 8, "q0": 10,
                   "q1": 10, "zT0": 11, "zT1": 11, "v0": 12.5, "logits": 12.5, "v1": 13.5, "prefix": 15.5}
        BOTH = list(UNIT_OF)
        AT = {"ctx_high": 0, "x_norm": 4, "z_norm": 9, "gap": 14, "w1_scale": (3, 12), "w1_high": (7, 15),
              "x_stats": (0, 1, 2, 3), "z_stats": (5, 5, 6, 6)}
        LATE = ("v1",)
        ROUTE = {(12, 3): (0, 1, 2, 3, 4, 5), (13, 0): (6,), (13, 1): (7,), (13, 3): (8, 9, 10, 11), (14, 2): (12,),
                 (14, 3): (13,), (15, 0): (14,), (15, 1): (15, 16)}
        NEEDS = {"q0": "xT1", "logits": "zT1", "out0": "oT1"}
        TURNED = ("xT", "zT")

        TURNED_STEPS, OWN_STEPS = 4 * B - 2, 12 * B + 2

        class Step:

            def __init__(self, name, turned, bank, n, k, hi, bank_before, needs):
                self.taken = int(UNIT_OF[name]) + (name in LATE)
                self.name, self.unit, self.bank, self.n, self.k, self.hi = name, UNIT_OF[name], bank, n, k, hi
                self.turned = turned
                self.kind, self.half = name.rstrip("01"), int(name[-1]) if name[-1].isdigit() else 0
                self.bank_before, self.needs = bank_before, needs

        def numbered(names, n0, turned0, own0, hi0, kinds=TURNED):
            steps, turned, own, hi, at = [], turned0, own0, hi0, {}
            for i, name in enumerate(names):
                is_turned = name.rstrip("01") in kinds
                before = steps[i - 2] if i > 1 else None
                bank_before = (before.turned, before.k + 1) if before else (False, own0 - 1 + i)
                at[name] = (is_turned, (turned if is_turned else own) + 1)
                steps.append(Step(name, is_turned, i % 2, n0 + i, turned if is_turned else own, hi, bank_before, at.get(NEEDS.get(name))))
                turned += is_turned
                own += not is_turned
                hi += not is_turned and name.rstrip("01") not in ("out", "logits", "prefix")
            return steps

        FIRST = numbered(["k0", "k1", "xT0", "xT1", "q0", "q1", "v0", "v1"], 0, 0, 0, 0)
        LAST = {step.name: step for step in numbered(POST, 16 * B - 8, TURNED_STEPS, OWN_STEPS - 8, 8 * B - 2, ())}

        def steps_of(b):
            if isinstance(b, int) and b == 0:
                return numbered(PRE, 8, 2, 6, 6)
            names = POST if isinstance(b, int) and b == B - 1 else BOTH
            return numbered(names, b * 16, b * 4, b * 12, b * 8 + 4)

        def wait(eng, s, n):
            if not isinstance(n, int) or n > 0:
                eng.wait_ge(s, n)

        def settle(eng):
            eng.sem_inc(settled, 1)

        def over_batches(eng, body):
            body(0, 0)
            with eng.Fori(0, (B - 2) // 2) as i:
                body(i * 2 + 1, 1)
                body(i * 2 + 2, 0)
            body(B - 1, (B - 1) % 2)

        def over_tiles(eng, body):
            assert (NT - 2 - EARLY_TILES) % 2 == 0
            with eng.Fori(0, (NT - 2 - EARLY_TILES) // 2) as i:
                body(i * 2 + EARLY_TILES, EARLY_TILES % 2)
                body(i * 2 + EARLY_TILES + 1, 1 - EARLY_TILES % 2)

        def is_single(j):
            return isinstance(j, int) and j < SINGLE_TILES

        def scalar_takes_high(j):
            return isinstance(j, int) and j in SCALAR_HIGH

        assert (2 * (B - 2) * S - E * (TILE - 1)) // TILE >= EARLY_TILES

        PIECES = E * DC
        PIECE_BYTES = E * HC * D * 4 // PIECES
        AFTER_PRE, AFTER_EVEN = BEFORE_QKV // PIECE_BYTES, EARLY // PIECE_BYTES
        assert B % 2 == 0 and PIECES == 2 * B
        assert (EARLY_TILES, SINGLE_TILES) == (5, 3) and PIECES - AFTER_EVEN == 6

        W2_FIRST_UNIT = 6

        def w2_piece(n, low):
            at = (n // 2) * 2 * HC * D + low * HC * D + (n % 2) * H
            return arena16[:, at:at + H]

        SMALL_LOADS = 10

        def proj_stage(name):
            at = 0 if name in "kq" else 2 * D
            return (stage[1], KVP, slice(at, at + 2 * D)) if name in "kv" else (stage[0], P, slice(at, at + 2 * D))

        def rows_sent_by(b):
            return b * (2 * NT_TOK * 16) + 16

        Q_DMAS, K_DMAS = 16 * 4, 16 * 8
        block = stack.enter_context(nc.Block())

        @block.sync
        def _(sp):
            sp.dma_start(x_in, x_v[0]).then_inc(x_loaded, 16)
            sp.dma_start(ctx_in[0:KVP], ctx_v[0]).then_inc(ctx_loaded, 16)
            for name, w in (("k", WkT), ("q", WqT), ("v", WvT), ("o", WoT)):
                buffer, rows, cols = proj_stage(name)
                sp.dma_start(buffer[0:rows, cols].rearrange("p (c n) -> p c n", c=2), w.rearrange("(c p) n -> p c n", p=rows)).then_inc(proj_in[name], 16)
            sp.dma_start(gx[:, :], bc(g_xattn, P)).then_inc(small_in, 16)
            sp.dma_start(gf[:, :], bc(g_ffn, P)).then_inc(small_in, 16)
            sp.dma_start(tanh_bo[:, :], bc(bo, P)).then_inc(small_in, 16)
            sp.dma_start(rbias[:, :], bc(rb, P)).then_inc(small_in, 16)
            sp.dma_start(rls_s[:, :], rls).then_inc(small_in, 16)
            sp.dma_start(rlb_s[:, :], rlb).then_inc(small_in, 16)
            sp.dma_start(rw_raw[:, :, :], rwT.rearrange("(c p) e -> p c e", p=P)).then_inc(small_in, 16)
            sp.dma_start(els_s[:, :], els).then_inc(small_in, 16)
            sp.dma_start(elb_s[:, :], elb).then_inc(small_in, 16)
            sp.dma_start(b1_s[:, :], b1).then_inc(small_in, 16)
            sp.dma_start(x2, x_v[0]).then_inc(xres_loaded, 16)
            sp.wait_ge(pads_ready, 1)
            sp.dma_start(acc_dram[T:T + TILE, :].rearrange("(s p) n -> p s n", p=P), pad_rows[:, :, 0:D]).then_inc(pads_sent, 16)

            def batch(b, par):
                if not (isinstance(b, int) and b == B - 1):
                    wait(sp, ln_done, b + 1)
                    settle(sp)
                    sp.dma_start(x_in, x_v[b + 1] if isinstance(b, int) else x_v[bass.ds(b + 1, 1)].rearrange("a p j d -> (a p) j d")).then_inc(x_loaded, 16)
                    sp.wait_ge(ctx_hi_done, b + 1)
                    sp.wait_ge(ctx_lo_done, b + 1)
                    settle(sp)
                    sp.dma_start(ctx_in[0:KVP], ctx_v[b + 1] if isinstance(b, int) else ctx_v[bass.ds(b + 1, 1)].rearrange("a p c s -> (a p) c s")).then_inc(ctx_loaded, 16)
                for s in range(2):
                    n = b * 2 + s
                    if isinstance(b, int) and b == 0:
                        sp.wait_ge(proj_lo, 4)
                    else:
                        sp.wait_ge(stage_lo, n - 1)
                        settle(sp)
                    sp.dma_start(stage[s][:, :], w1_v[n] if isinstance(b, int) else w1_v[bass.ds(n, 1)].rearrange("a p h -> (a p) h")).then_inc(stage_in[s], 16)
                final = isinstance(b, int) and b == B - 1
                if final:
                    for n in range(4):
                        load_w2(n)
                if not (isinstance(b, int) and b == 0):
                    store_x2(b - 1)
                if final:
                    load_w2(4)
                if not final:
                    place(steps_of(b), "k", 1 - par)
                if not (isinstance(b, int) and b == 0):
                    sp.wait_ge(z_done, b)
                    settle(sp)
                    sp.wait_ge(x2_stored, 16 * b)
                    settle(sp)
                    sp.dma_start(x2, x_v[b] if isinstance(b, int) else x_v[bass.ds(b, 1)].rearrange("a p j d -> (a p) j d")).then_inc(xres_loaded, 16)
                if not final:
                    place(steps_of(b), "q", 1 - par)

            def load_w2(n):
                if n < 2:
                    sp.wait_ge(stage_lo, PIECES - 1 + n)
                else:
                    sp.wait_ge(w2_lo_done, n - 1)
                sp.dma_start(stage[n % 2][:, :].rearrange("p (c d) -> p c d", d=D), w2_v[n]).then_inc(stage_in[n % 2], 16)

            def place(steps, kind, par):
                sp.wait_ge(side_done, [step.k for step in steps if step.kind == kind][1] + 1)
                settle(sp)
                where = [(q_st, q_placed, (0, HD))] if kind == "q" else [(k_hl, k_placed, (0, HD)), (k_lh, k_placed, (HD, 0))]
                for dst, placed, rows in where:
                    for row, src in zip(rows, (two_hi[kind], two_lo[kind])):
                        for i in range(2):
                            sp.dma_start(dst[par][row:row + HD, i:HEADS:2, :], src[i * HD:(i + 1) * HD, :, :]).then_inc(placed, 16)

            def store_x2(b):
                sp.wait_ge(z_stats, b + 1)
                settle(sp)
                sp.dma_start(acc_v[b] if isinstance(b, int) else acc_v[bass.ds(b, 1)].rearrange("a p j d -> (a p) j d"), x2).then_inc(x2_stored, 16)

            place(FIRST, "k", 0)
            place(FIRST, "q", 0)
            over_batches(sp, batch)
            for n in range(5, AFTER_EVEN):
                load_w2(n)

            def load_rows(j, par):
                at = sp.value_load(tile_row[0:1, j:j + 1] if isinstance(j, int) else tile_row[0:1, bass.ds(j, 1)], min_val=0, max_val=E * REGION)
                sp.dma_start(rows_r[par][:, :, :], rows_dram[bass.ds(at, TILE), :].rearrange("(s p) n -> p s n", p=P)).then_inc(rows_in[par], 16)

            def more_rows(j, par):
                sp.wait_ge(zT_mm, j + 1)
                sp.wait_ge(z_lo_done, j + 1)
                settle(sp)
                load_rows(j + 2, par)

            sp.wait_ge(tables, 1)
            sp.wait_ge(turned_lo, TURNED_STEPS)
            sp.wait_ge(rows_sent, rows_sent_by(B - 2))
            load_rows(0, 0)
            load_rows(1, 1)
            load_w2(AFTER_EVEN)
            load_w2(AFTER_EVEN + 1)
            more_rows(0, 0)
            store_x2(B - 1)
            more_rows(1, 1)
            for n in range(AFTER_EVEN + 2, PIECES):
                load_w2(n)
            more_rows(2, 0)
            sp.wait_ge(tables, 2)
            for e in range(E):
                at = sp.value_load(pad_at[0:1, e:e + 1], min_val=e * REGION, max_val=e * REGION + T)
                sp.dma_start(rows_dram[bass.ds(at, TILE), :].rearrange("(s p) n -> p s n", p=P), pad_rows[:, :, :]).then_inc(pads_sent, 16)
            sp.wait_ge(tables, 3)
            sp.wait_ge(pads_sent, 16 * (1 + E))
            sp.wait_ge(rows_sent, rows_sent_by(B))
            more_rows(3, 1)
            more_rows(4, 0)
            over_tiles(sp, more_rows)
            sp.wait_ge(x2_stored, 16 * B)
            sp.wait_ge(y_added, 16 * 2 * NT)
            sp.dma_start(out_v, acc_dram[0:T, :]).then_inc(out_stored, 16)
            sp.wait_ge(out_stored, 16)

        @block.gpsimd
        def _(pool):
            pool.memset(ident[:, :], 0.0).then_inc(const_pool, 1)
            pool.memset(before[:, :], 1.0).then_inc(const_pool, 1)
            pool.memset(pad_rows[:, :, :], 0.0).then_inc(const_pool, 1)
            pool.memset(half[:, :], -0.5).then_inc(const_pool, 1)
            pool.memset(minus[:, :], -1.0).then_inc(const_pool, 1)
            pool.iota(code_i[:, :, :], pattern=[[0, NT_TOK], [-1, E]], base=E, channel_multiplier=0).then_inc(const_pool, 1)
            pool.iota(region_i[:, :], pattern=[[REGION, E]], base=0, channel_multiplier=0).then_inc(const_pool, 1)
            pool.iota(tok_i[:, :], pattern=[[P, T // P]], base=0, channel_multiplier=1).then_inc(const_pool, 1)
            pool.iota(tile_i[:, :], pattern=[[1, NT]], base=0, channel_multiplier=0).then_inc(const_pool, 1)
            pool.iota(pad_i[:, :], pattern=[[P, 2]], base=T, channel_multiplier=1).then_inc(const_pool, 1)
            pool.wait_ge(const_pool, 10)
            pool.affine_select(out=ident[:, :], in_=ident[:, :], compare_op=ALU.not_equal, fill=1.0, base=0,
                               pattern=[[-1, P]], channel_multiplier=1).then_inc(const_pool, 1)
            pool.affine_select(out=before[:, :], in_=before[:, :], compare_op=ALU.is_gt, fill=0.0, base=0,
                               pattern=[[1, P]], channel_multiplier=-1).then_inc(const_pool, 1)

            def link(s, count, ins):
                ins.then_inc(s, 1)
                pool.wait_ge(s, count)
                settle(pool)

            Z_STEPS = 7

            def scale_of_x(b):
                pool.wait_ge(ln_stats, b + 1)
                settle(pool)
                link(ln_step, b + 1, pool.tensor_scalar(rs[:, 0, :], mv[:, 0, :, 1], LN_EPS, None, ALU.add))
                pool.tensor_tensor(rs[:, 1, :], rs[:, 0, :], half[:, :], ALU.pow).then_inc(x_scale_ready, 1)

            def ctx_low(b):
                pool.wait_ge(ctx_hi_done, b + 1)
                pool.tensor_tensor(ctx_lo[0:KVP], ctx_in[0:KVP], ctx_hi[0:KVP], ALU.subtract).then_inc(ctx_lo_done, 1)

            def residual(b):
                pool.wait_ge(xres_loaded, 16 * (b + 1))
                pool.tensor_tensor(x2, x2, tanh_bo[:, :].unsqueeze(1).to_broadcast([P, NT_TOK, D]), ALU.add).then_inc(res_ready, 1)

            def scale_of_z(b):
                pool.wait_ge(z_stats, b + 1)
                settle(pool)
                c = b * Z_STEPS
                var = mv[:, 1, :, 1]
                pool.tensor_tensor(rs[:, 8, :], mv[:, 1, :, 0], minus[:, :], ALU.mult)
                link(z_step, c + 1, pool.tensor_scalar(rs[:, 2, :], var, LN_EPS, None, ALU.add))
                link(z_step, c + 2, pool.tensor_tensor(rs[:, 3, :], rs[:, 2, :], half[:, :], ALU.pow))
                link(z_step, c + 3, pool.tensor_tensor(rs[:, 4, :], rs[:, 3, :], rs[:, 3, :], ALU.mult))
                link(z_step, c + 4, pool.tensor_tensor(rs[:, 5, :], rs[:, 4, :], var, ALU.mult))
                link(z_step, c + 5, pool.tensor_scalar(rs[:, 5, :], rs[:, 5, :], LN2_EPS, None, ALU.add))
                link(z_step, c + 6, pool.tensor_tensor(rs[:, 6, :], rs[:, 5, :], half[:, :], ALU.pow))
                link(z_step, c + 7, pool.tensor_tensor(rs[:, 7, :], rs[:, 3, :], rs[:, 6, :], ALU.mult))
                pool.tensor_tensor(rs[:, 9, :], rs[:, 8, :], rs[:, 7, :], ALU.mult).then_inc(z_scale_ready, 1)

            def w1_low(n, s):
                cols = slice(n * H, (n + 1) * H) if isinstance(n, int) else bass.ds(n * H, H)
                pool.wait_ge(stage_hi, n + 1)
                pool.tensor_tensor(w1_lo[:, cols], stage[s][:, :], w1_hi[:, cols], ALU.subtract).then_inc(stage_lo, 1)

            def scatter(b):
                pool.wait_ge(rows_ready, b + 1)
                settle(pool)
                for k in range(2):
                    for j in range(NT_TOK):
                        pool.indirect_dma_start(rows_dram[:, :], bass.IndirectOffsetOnAxis(ap=slot_i[:, k, j:j + 1], axis=0),
                                                rows_w[:, j, :], None).then_inc(rows_sent, 16)

            def turned_low(step):
                dst_hi, dst_lo = {"xT": (xT_hi, xT_lo), "zT": (zrT_hi, zrT_lo)}[step.kind]
                pool.wait_ge(turned_hi, step.k + 1)
                pool.wait_ge(turned_copied, step.k + 1)
                pool.tensor_tensor(dst_lo[:, step.half, :], turned[step.half], dst_hi[:, step.half, :], ALU.subtract).then_inc(turned_lo, 1)

            pool.wait_ge(pads_ready, 1)
            pool.dma_start(rows_dram[E * REGION:E * REGION + TILE, :].rearrange("(s p) n -> p s n", p=P), pad_rows[:, :, :]).then_inc(rows_sent, 16)
            scale_of_x(0)
            ctx_low(0)
            for step in FIRST:
                if step.turned:
                    turned_low(step)
            pool.wait_ge(gates_done, 1)
            residual(0)

            def batch(b, par):
                first, final = isinstance(b, int) and b == 0, isinstance(b, int) and b == B - 1
                if not final:
                    scale_of_x(b + 1)
                    ctx_low(b + 1)
                if final:
                    w1_low(b * 2, 0)
                    w1_low(b * 2 + 1, 1)
                for step in steps_of(b):
                    if step.kind == "xT":
                        turned_low(step)
                if not first:
                    scale_of_z(b - 1)
                if not final:
                    w1_low(b * 2, 0)
                for step in steps_of(b):
                    if step.kind == "zT":
                        turned_low(step)
                if not first:
                    residual(b)
                if not final:
                    w1_low(b * 2 + 1, 1)
                if not first:
                    scatter(b - 1)

            over_batches(pool, batch)
            scale_of_z(B - 1)

            def add_rows(j, par):
                pool.wait_ge(y_done, j + 1)
                if not isinstance(j, int) or j > 0:
                    pool.wait_ge(y_added, 32 * j)
                settle(pool)
                for s in range(2):
                    pool.indirect_dma_start(acc_dram[:, :], bass.IndirectOffsetOnAxis(ap=y_idx[par][:, s:s + 1], axis=0),
                                            y_out[par][:, s, :], None, compute_op=ALU.add).then_inc(y_added, 16)

            pool.wait_ge(x2_stored, 16 * B)
            add_rows(0, 0)
            scatter(B - 1)
            add_rows(1, 1)
            add_rows(2, 0)
            with pool.Fori(0, (NT - 3) // 2) as i:
                add_rows(i * 2 + 3, 1)
                add_rows(i * 2 + 4, 0)
            pool.wait_ge(y_added, 32 * NT)

        @block.scalar
        def _(act):
            def ctx_high(b):
                act.wait_ge(ctx_loaded, 16 * (b + 1))
                if not (isinstance(b, int) and b == 0):
                    act.wait_ge(side_mm, (b - 1) * 16 if not isinstance(b, int) else max((b - 1) * 16, 8))
                act.activation(ctx_hi[0:KVP], ctx_in[0:KVP], ACT.Copy).then_inc(ctx_hi_done, 1)

            def side(step, b, par):
                if step.kind in ("out", "logits", "prefix"):
                    return
                act.wait_ge(side_mm, step.n + 1)
                c, src = step.half, bank_m[step.bank]
                if step.turned:
                    act.activation({"xT": xT_hi, "zT": zrT_hi}[step.kind][:, c, :], src, ACT.Copy).then_inc(turned_hi, 1)
                    wait(act, turned_lo, step.k - 1)
                    act.activation(turned[step.half], src, ACT.Copy).then_inc(turned_copied, 1)
                elif step.kind in ("oT", "zT"):
                    act.activation((oT_hi if step.kind == "oT" else zrT_hi)[:, c, :], src, ACT.Copy).then_inc(side_hi, 1)
                elif step.kind == "v":
                    act.activation(v_hi[par][:, 2 * c:2 * c + 2, :].rearrange("p j d -> p (j d)"), src, ACT.Copy, scale=1.0 / W_SCALE).then_inc(side_hi, 1)
                else:
                    if not (isinstance(b, int) and b == 0):
                        act.wait_ge(*((q_placed, Q_DMAS * b) if step.kind == "q" else (k_placed, K_DMAS * b)))
                    act.activation(two_hi[step.kind][:, c, :], src, ACT.Copy, scale=(QSCALE if step.kind == "q" else 1.0) / W_SCALE).then_inc(side_hi, 1)

            def normalise_z(b):
                act.wait_ge(rows_sent, rows_sent_by(b))
                act.wait_ge(z_scale_ready, b + 1)
                for j in range(NT_TOK):
                    last = act.activation(rows_w[:, j, 0:D], x2[:, j, :], ACT.Identity, bias=rs[:, 9, j:j + 1], scale=rs[:, 7, j:j + 1])
                last.then_inc(z_done, 1)

            def w2_high(n):
                if n == 0:
                    act.wait_ge(ln_done, B)
                    act.wait_ge(ctx_lo_done, B)
                    act.wait_ge(side_mm, 16 * (B - 1))
                elif n == AFTER_PRE:
                    act.wait_ge(pv_mm, (B - 1) * UNITS)
                elif n == AFTER_EVEN:
                    act.wait_ge(pv_mm, B * UNITS)
                act.wait_ge(stage_in[n % 2], 16 * (PIECES // 2 + n // 2 + 1))
                act.activation(w2_piece(n, 0), stage[n % 2][:, :], ACT.Copy, scale=W_SCALE).then_inc(w2_hi_done, 1)

            def exponentials(b, u):
                g, t, j = b * UNITS + u, u % 2, u // HEADS
                act.wait_ge(max_done, g + 1)
                wait(act, pT_mm, g - 1)
                if u % HEADS == 0:
                    wait(act, on_done, b * NT_TOK + j - 1)
                act.activation(prob[t], bank_s[t], ACT.Exp, bias=neg_max[:, t:t + 1],
                               accum_out=p_sum[:, j % 2, u % HEADS:u % HEADS + 1]).then_inc(exp_done, 1)

            def batch(b, par):
                first, final = isinstance(b, int) and b == 0, isinstance(b, int) and b == B - 1
                for u in range(UNITS):
                    g, t = b * UNITS + u, u % 2
                    if u < UNITS - 1:
                        exponentials(b, u + 1)
                    elif not final:
                        exponentials(b + 1, 0)
                    act.wait_ge(pT_mm, g + 1)
                    wait(act, pv_mm, g - 1)
                    act.activation(pT_hi[t], bank_t[t], ACT.Copy).then_inc(pT_hi_done, 1)
                    for step in steps_of(b):
                        if step.taken == u:
                            side(step, b - 1 if step.name in POST else b + 1, 1 - par)
                    if u == AT["ctx_high"] and not final:
                        ctx_high(b + 1)
                    if u == AT["z_norm"] and not first:
                        normalise_z(b - 1)
                    for s in range(2):
                        n = b * 2 + s
                        if u == (s if final else AT["w1_scale"][s]):
                            act.wait_ge(stage_in[s], b * 16 + 16)
                            act.activation(stage[s][:, :], stage[s][:, :], ACT.Copy, scale=W_SCALE).then_inc(stage_scaled, 1)
                        if u == (s if final else AT["w1_high"][s]):
                            act.wait_ge(stage_scaled, n + 1)
                            act.activation(w1_hi[:, n * H:(n + 1) * H] if isinstance(n, int) else w1_hi[:, bass.ds(n * H, H)],
                                           stage[s][:, :], ACT.Copy).then_inc(stage_hi, 1)
                    if final and 0 <= u - W2_FIRST_UNIT < AFTER_EVEN:
                        w2_high(u - W2_FIRST_UNIT)
                    if u == AT["gap"] and not first:
                        gap(b - 1)

            def gap(b):
                act.wait_ge(gap_sub, b + 1)
                act.activation(top[:, 5, :], top[:, 4, :], ACT.Exp).then_inc(gap_exp, 1)

            ctx_high(0)
            act.wait_ge(small_in, 16 * SMALL_LOADS)
            act.activation(gx[:, :], gx[:, :], ACT.Tanh).then_inc(gates_tanh, 1)
            act.activation(gf[:, :], gf[:, :], ACT.Tanh).then_inc(gates_tanh, 1)
            for step in FIRST:
                side(step, 0, 0)
            act.dma_start(b2_all[:, :, :].rearrange("p e d -> p (e d)"), bc(b2.rearrange("e d -> (e d)"), P)).then_inc(b2_in, 16)
            exponentials(0, 0)
            over_batches(act, batch)

            def rows_high(j):
                act.wait_ge(z_aff_done, j + 1)
                act.activation(z_hi[:, :, :], z_aff[:, :, :], ACT.Copy).then_inc(z_hi_done, 1)

            def gelus(j):
                e = act.value_load(tile_expert[0:1, j:j + 1] if isinstance(j, int) else tile_expert[0:1, bass.ds(j, 1)], min_val=0, max_val=E - 1)
                for m in range(HC // 2):
                    act.wait_ge(h_mm, j * 4 + m + 1)
                    wait(act, h_lo_done, (j - 1) * 4 + m + 1)
                    for i in range(2):
                        hc = 2 * m + i
                        last = act.activation(hid[:, m, i * TILE:(i + 1) * TILE], bank_h[m][:, i * TILE:(i + 1) * TILE], ACT.Gelu,
                                              bias=b1_s[:, bass.ds(e * HC + hc, 1)], scale=1.0 / W_SCALE)
                    last.then_inc(gelu_done, 1)

            def hidden_high(j, chunks=range(HC // 2)):
                if j == 0:
                    act.wait_ge(side_mm, LAST["out1"].n + 1)
                wait(act, y_mm, j if is_single(j) else j - 1)
                h = 0 if is_single(j) else j % 2
                for m in chunks:
                    cols = slice(m * 2 * TILE, (m + 1) * 2 * TILE)
                    act.wait_ge(gelu_done, j * 4 + m + 1)
                    act.activation(h_hi[h][:, cols], hid[:, m, :], ACT.Copy).then_inc(h_hi_done, 1)

            last = (B - 1) % 2
            act.wait_ge(tables, 1)
            rows_high(0)
            side(LAST["oT0"], B - 1, last)
            side(LAST["oT1"], B - 1, last)
            w2_high(AFTER_EVEN)
            w2_high(AFTER_EVEN + 1)
            rows_high(1)
            gelus(0)
            w2_high(AFTER_EVEN + 2)
            w2_high(AFTER_EVEN + 3)
            normalise_z(B - 1)
            side(LAST["zT0"], B - 1, last)
            side(LAST["zT1"], B - 1, last)
            w2_high(AFTER_EVEN + 4)
            w2_high(AFTER_EVEN + 5)
            rows_high(2)
            gelus(1)
            hidden_high(1)
            gap(B - 1)
            rows_high(3)
            gelus(2)
            hidden_high(2)
            rows_high(4)
            gelus(3)

            def tile(j):
                gelus(j + 1)
                rows_high(j + 2)

            tile(3)
            act.wait_ge(tables, 3)
            tile(4)
            with act.Fori(EARLY_TILES, NT - 2) as i:
                tile(i)
            gelus(NT - 1)

        @block.tensor
        def _(pe):
            def products(dst, pairs, start=True, stop=True):
                for i, (a, b_) in enumerate(pairs):
                    last = pe.matmul(dst, a, b_, start=start and i == 0, stop=stop and i == len(pairs) - 1)
                return last

            def three(a_hi, a_lo, b_hi, b_lo):
                return [(a_hi, b_hi), (a_hi, b_lo), (a_lo, b_hi)]

            def side(step, b, par):
                dst, c, kind = bank_m[step.bank], step.half, step.kind
                from_turned, count = step.bank_before
                wait(pe, turned_copied if from_turned else side_done, count)
                if step.needs:
                    from_turned, count = step.needs
                    pe.wait_ge(turned_lo if from_turned else side_done, count)
                if kind in ("xT", "oT", "zT"):
                    if kind == "xT":
                        pe.wait_ge(ln_done, b + 1)
                        src = xn
                    elif kind == "oT":
                        pe.wait_ge(on_done, (b + 1) * NT_TOK)
                        src = o_n[par]
                    else:
                        pe.wait_ge(z_done, b + 1)
                        src = rows_w
                    for j in range(NT_TOK):
                        last = pe.transpose(dst[:, j * P:(j + 1) * P], src[:, j, c * P:(c + 1) * P], ident[:, :])
                elif kind in ("q", "k"):
                    if step.name == "k0":
                        pe.wait_ge(ctx_lo_done, b + 1)
                    if kind == "q":
                        w, a, rows = (wq_hi, wq_lo), (xT_hi, xT_lo), P
                    else:
                        w, a, rows = (wk_hi, wk_lo), (ctx_hi, ctx_lo), KVP
                    pairs = []
                    for k in range(2):
                        cols = slice(c * P, (c + 1) * P)
                        pairs += three(w[0][:, k, cols], w[1][:, k, cols], a[0][0:rows, k, :], a[1][0:rows, k, :])
                    last = products(dst, pairs)
                elif kind == "v":
                    for i in range(2):
                        toks = slice((2 * c + i) * P, (2 * c + i + 1) * P)
                        pairs = []
                        for k in range(2):
                            pairs += three(ctx_hi[0:KVP, k, toks], ctx_lo[0:KVP, k, toks], wv_hi[:, k, :], wv_lo[:, k, :])
                        last = products(dst[:, i * D:(i + 1) * D], pairs)
                elif kind == "out":
                    for i in range(2):
                        toks = slice((2 * c + i) * P, (2 * c + i + 1) * P)
                        pairs = []
                        for k in range(DC):
                            pairs += three(oT_hi[:, k, toks], oT_lo[:, k, toks], wo_hi[:, k, :], wo_lo[:, k, :])
                        last = products(dst[:, i * D:(i + 1) * D], pairs)
                elif kind == "logits":
                    for j in range(NT_TOK):
                        toks = slice(j * P, (j + 1) * P)
                        pairs = []
                        for k in range(DC):
                            pairs += three(zrT_hi[:, k, toks], zrT_lo[:, k, toks], rw_hi[:, k, :], rw_lo[:, k, :])
                        last = products(dst[:, j * E:(j + 1) * E], pairs)
                else:
                    pe.wait_ge(gap_done, b + 1)
                    for j in range(NT_TOK + 1):
                        pairs = [(ones[:, :], hot16[:, i, :]) for i in range(j)]
                        if j < NT_TOK:
                            pairs.append((before[:, :], hot16[:, j, :]))
                        last = products(dst[:, j * E:(j + 1) * E], pairs)
                last.then_inc(side_mm, 1)

            def scores(b, u, par):
                g, t, h, j = b * UNITS + u, u % 2, u % HEADS, u // HEADS
                wait(pe, exp_done, g - 1)
                if u == 0:
                    pe.wait_ge(k_placed, K_DMAS * (b + 1))
                    pe.wait_ge(q_placed, Q_DMAS * (b + 1))
                q = q_st[par][:, h, j * P:(j + 1) * P]
                products(bank_s[t], [(q, k_hl[par][:, h, :]), (q, k_lh[par][:, h, :])]).then_inc(score_mm, 1)

            def turn(g, u):
                t = u % 2
                pe.wait_ge(exp_done, g + 1)
                wait(pe, pT_lo_done, g - 1)
                for k in range(S // P):
                    last = pe.transpose(bank_t[t][:, k * P:(k + 1) * P], prob[t][:, k * P:(k + 1) * P], ident[:, :])
                last.then_inc(pT_mm, 1)

            def weigh(g, u, par, b):
                t, h, j = u % 2, u % HEADS, u // HEADS
                if h == 0:
                    wait(pe, on_done, b * NT_TOK + j - 1)
                pe.wait_ge(pT_lo_done, g + 1)
                cols, pairs = slice(h * HD, (h + 1) * HD), []
                for k in range(S // P):
                    keys = slice(k * P, (k + 1) * P)
                    pairs += three(pT_hi[t][:, keys], pT_lo[t][:, keys], v_hi[par][:, k, cols], v_lo[par][:, k, cols])
                products(bank_o[j % 2][:, cols], pairs).then_inc(pv_mm, 1)

            pe.wait_ge(const_pool, 12)
            for step in FIRST:
                if step.half == 0 and step.kind in "kqv":
                    pe.wait_ge(proj_lo, "kqv".index(step.kind) + 1)
                side(step, 0, 0)
            pe.wait_ge(router_ready, 1)
            for k in range(DC):
                last = pe.matmul(bank_o[1][:, 0:E], rlb_bc[:, k, :], rw_raw[:, k, :], start=k == 0, stop=k == DC - 1)
            last.then_inc(rbias_mm, 1)
            scores(0, 0, 0)
            scores(0, 1, 0)
            pe.wait_ge(proj_lo, 4)
            pe.wait_ge(rbias_done, 1)

            def batch(b, par):
                first, final = isinstance(b, int) and b == 0, isinstance(b, int) and b == B - 1
                for u in range(UNITS):
                    g = b * UNITS + u
                    turn(g, u)
                    if u < UNITS - 2:
                        scores(b, u + 2, par)
                    elif not final:
                        scores(b + 1, u + 2 - UNITS, 1 - par)
                    for step in steps_of(b):
                        if step.unit == u:
                            side(step, b - 1 if step.name in POST else b + 1, 1 - par)
                    if u > 0:
                        weigh(g - 1, u - 1, par, b)
                    elif not first:
                        weigh(g - 1, UNITS - 1, 1 - par, b - 1)
                    for step in steps_of(b):
                        if step.unit == u + 0.5:
                            side(step, b - 1 if step.name in POST else b + 1, 1 - par)

            over_batches(pe, batch)
            weigh(B * UNITS - 1, UNITS - 1, (B - 1) % 2, B - 1)
            def expert_of(j):
                return pe.value_load(tile_expert[0:1, j:j + 1] if isinstance(j, int) else tile_expert[0:1, bass.ds(j, 1)], min_val=0, max_val=E - 1)

            def rows_turn(j, par):
                bank = bank_o[0] if is_single(j) else bank_z
                pe.wait_ge(rows_in[par], (j // 2 + 1) * 16 if isinstance(j, int) else j * 8 + 16 - 8 * par)
                wait(pe, z_aff_done, j)
                for c in range(DC):
                    for s in range(2):
                        last = pe.transpose(bank[:, c * TILE + s * P:c * TILE + (s + 1) * P], rows_r[par][:, s, c * P:(c + 1) * P], ident[:, :])
                last.then_inc(zT_mm, 1)

            def hidden(j, e):
                pe.wait_ge(z_lo_done, j + 1)
                for m in range(HC // 2):
                    wait(pe, gelu_done, (j - 1) * 4 + m + 1)
                    for i in range(2):
                        pairs = []
                        for c in range(DC):
                            at = e * (DC * H) + c * H + (2 * m + i) * P
                            pairs += three(w1_hi[:, bass.ds(at, P)], w1_lo[:, bass.ds(at, P)], z_hi[:, c, :], z_lo[:, c, :])
                        last = products(bank_h[m][:, i * TILE:(i + 1) * TILE], pairs)
                    last.then_inc(h_mm, 1)

            def back(j, e, par):
                wait(pe, y_done, j if isinstance(j, int) and j <= SINGLE_TILES else j - 1)
                if isinstance(j, int) and j == 0:
                    pe.wait_ge(w2_lo_done, PIECES)
                h, bank = (0, bank_y[1]) if is_single(j) else (par, bank_y[par])
                pe.wait_ge(h_lo_done, j * 4 + 4)
                for s in range(2):
                    pairs = []
                    for hc in range(HC):
                        rows = slice(hc * TILE + s * P, hc * TILE + (s + 1) * P)
                        hi, lo = (bass.ds(e * (2 * HC * D) + low * HC * D + hc * D, D) for low in range(2))
                        pairs += three(h_hi[h][:, rows], h_lo[h][:, rows], arena16[:, hi], arena16[:, lo])
                    last = products(bank[:, s * D:(s + 1) * D], pairs)
                last.then_inc(y_mm, 1)

            def finish(*names):
                for name in names:
                    side(LAST[name], B - 1, (B - 1) % 2)

            pe.wait_ge(tables, 1)
            pe.wait_ge(stage_lo, PIECES)
            pe.wait_ge(on_done, B * NT_TOK - 1)
            rows_turn(0, 0)
            finish("oT0", "oT1", "out0", "out1")
            hidden(0, expert_of(0))
            rows_turn(1, 1)
            hidden(1, expert_of(1))
            finish("zT0", "zT1")
            rows_turn(2, 0)
            back(0, expert_of(0), 0)
            finish("logits")
            hidden(2, expert_of(2))
            finish("prefix")
            pe.wait_ge(side_done, OWN_STEPS - 1)
            rows_turn(3, 1)
            back(1, expert_of(1), 1)
            hidden(3, expert_of(3))
            rows_turn(4, 0)
            back(2, expert_of(2), 0)

            def tile(j, par):
                hidden(j + 1, expert_of(j + 1))
                if isinstance(j, int) and j == SINGLE_TILES:
                    pe.wait_ge(tables, 3)
                rows_turn(j + 2, par)
                back(j, expert_of(j), par)

            tile(3, 1)
            tile(4, 0)
            over_tiles(pe, tile)
            hidden(NT - 1, expert_of(NT - 1))
            back(NT - 2, expert_of(NT - 2), (NT - 2) % 2)
            back(NT - 1, expert_of(NT - 1), (NT - 1) % 2)

        @block.vector
        def _(v):
            v.memset(ones[:, :], 1.0).then_inc(dve, 1)
            v.memset(one8[:, :], 1.0).then_inc(dve, 1)
            v.wait_ge(const_pool, 10)
            v.tensor_copy(code[:, :, :], code_i[:, :, :]).then_inc(dve, 1)
            v.tensor_copy(region_f[:, :], region_i[:, :]).then_inc(dve, 1)
            v.tensor_copy(base[:, :], region_i[:, :]).then_inc(dve, 1)
            v.tensor_copy(tok_f[:, :], tok_i[:, :]).then_inc(dve, 1)
            v.tensor_copy(tile_f[:, :], tile_i[:, :]).then_inc(dve, 1)
            v.tensor_copy(pad_rows[:, :, D + COL_TOKEN], pad_i[:, :]).then_inc(pads_ready, 1)

            def x_stats(b, j):
                if j == 0:
                    v.wait_ge(x_loaded, 16 * (b + 1))
                    wait(v, ln_done, b)
                v.bn_stats(stats[:, 0, j, :], x_in[:, j, :]).then_inc(x_bn, 1)
                if j == NT_TOK - 1:
                    v.wait_ge(x_bn, (b + 1) * NT_TOK)
                    settle(v)
                    for i in range(NT_TOK):
                        last = v.bn_aggr(mv[:, 0, i, :], stats[:, 0, i, :])
                    last.then_inc(ln_stats, 1)

            def normalise_x(b):
                v.wait_ge(x_scale_ready, b + 1)
                settle(v)
                for j in range(NT_TOK):
                    last = v.tensor_scalar(xn[:, j, :], x_in[:, j, :], mv[:, 0, j, 0:1], rs[:, 1, j:j + 1], ALU.subtract, ALU.mult)
                last.then_inc(ln_done, 1)

            def z_statistics(b, j, n):
                if j == 0:
                    v.wait_ge(side_done, n)
                v.bn_stats(stats[:, 1, j, :], x2[:, j, :]).then_inc(z_bn, 1)
                if j == NT_TOK - 1:
                    v.wait_ge(z_bn, (b + 1) * NT_TOK)
                    settle(v)
                    for i in range(NT_TOK):
                        last = v.bn_aggr(mv[:, 1, i, :], stats[:, 1, i, :])
                    last.then_inc(z_stats, 1)

            for j in range(NT_TOK):
                x_stats(0, j)

            def split_projection(name, hi, lo):
                buffer, rows, cols = proj_stage(name)
                i = "kqvo".index(name)
                v.wait_ge(proj_in[name], 16)
                v.tensor_scalar(hi[:, :, :].rearrange("p c n -> p (c n)"), buffer[0:rows, cols], W_SCALE, None, ALU.mult).then_inc(proj_hi, 1)
                v.wait_ge(proj_hi, i + 1)
                v.scalar_tensor_tensor(out=lo[:, :, :].rearrange("p c n -> p (c n)"), in0=buffer[0:rows, cols], scalar=W_SCALE,
                                       in1=hi[:, :, :].rearrange("p c n -> p (c n)"), op0=ALU.mult, op1=ALU.subtract).then_inc(proj_lo, 1)

            split_projection("k", wk_hi, wk_lo)
            normalise_x(0)
            split_projection("q", wq_hi, wq_lo)

            OF_TOKENS = [P, NT_TOK, E]
            CHAIN = 18

            def take_logits(b, step):
                v.wait_ge(side_mm, step.n + 1)
                v.scalar_tensor_tensor(out=logit[:, :, :], in0=bank_m[step.bank][:, 0:NT_TOK * E].rearrange("p (j e) -> p j e", j=NT_TOK),
                                       scalar=1.0 / W_SCALE, in1=rbias[:, :].unsqueeze(1).to_broadcast(OF_TOKENS),
                                       op0=ALU.mult, op1=ALU.add).then_inc(side_done, 1)

            def argmax(c, k, i):
                src, hot = ((logit, hot1), (logit2, hot2))[k]
                if i > 0:
                    v.wait_ge(chain, c + 5 * k + i)
                if i == 0:
                    ins = v.tensor_reduce(top[:, 2 * k, :], src[:, :, :], AX.X, ALU.max)
                elif i == 1:
                    ins = v.tensor_tensor(tmp8[:, :, :], src[:, :, :], top[:, 2 * k, :].unsqueeze(2).to_broadcast(OF_TOKENS), ALU.is_equal)
                elif i == 2:
                    ins = v.tensor_tensor(tmp8[:, :, :], tmp8[:, :, :], code[:, :, :], ALU.mult)
                elif i == 3:
                    ins = v.tensor_reduce(top[:, 2 * k + 1, :], tmp8[:, :, :], AX.X, ALU.max)
                else:
                    ins = v.tensor_tensor(hot[:, :, :], code[:, :, :], top[:, 2 * k + 1, :].unsqueeze(2).to_broadcast(OF_TOKENS), ALU.is_equal)
                ins.then_inc(chain, 1)

            def routing(b, n):
                c = b * CHAIN
                if n < 5:
                    if n == 0:
                        step = LAST["logits"] if isinstance(b, int) and b == B - 1 else [step for step in steps_of(b + 1) if step.name == "logits"][0]
                        v.wait_ge(side_done, step.k + 1)
                    argmax(c, 0, n)
                elif n == 5:
                    v.wait_ge(chain, c + 5)
                    v.scalar_tensor_tensor(out=logit2[:, :, :], in0=hot1[:, :, :], scalar=FAR_BELOW, in1=logit[:, :, :],
                                           op0=ALU.mult, op1=ALU.add).then_inc(masked, 1)
                elif n < 11:
                    if n == 6:
                        v.wait_ge(masked, b + 1)
                    argmax(c, 1, n - 6)
                elif n == 11:
                    v.wait_ge(chain, c + 10)
                    v.tensor_tensor(hot16[:, :, :], hot1[:, :, :], hot2[:, :, :], ALU.add).then_inc(gap_done, 1)
                    v.tensor_tensor(top[:, 4, :], top[:, 2, :], top[:, 0, :], ALU.subtract).then_inc(gap_sub, 1)
                elif n == 12:
                    v.wait_ge(gap_exp, b + 1)
                    v.tensor_scalar(top[:, 6, :], top[:, 5, :], 1.0, None, ALU.add).then_inc(chain, 1)
                elif n == 13:
                    v.wait_ge(chain, c + 11)
                    v.reciprocal(top[:, 6, :], top[:, 6, :]).then_inc(chain, 1)
                elif n == 14:
                    v.wait_ge(chain, c + 12)
                    v.tensor_scalar(top[:, 6, :], top[:, 6, :], gf[:, 0:1], None, ALU.mult).then_inc(chain, 1)
                elif n == 15:
                    v.wait_ge(rows_sent, rows_sent_by(b))
                    v.wait_ge(chain, c + 13)
                    v.tensor_tensor(rows_w[:, :, D + COL_G2], top[:, 6, :], top[:, 5, :], ALU.mult).then_inc(chain, 1)
                    v.tensor_copy(rows_w[:, :, D + COL_E1], top[:, 1, :])
                    v.tensor_copy(rows_w[:, :, D + COL_TOKEN], tok_f[:, b * NT_TOK:(b + 1) * NT_TOK] if isinstance(b, int) else tok_f[:, bass.ds(b * NT_TOK, NT_TOK)])
                elif n == 16:
                    v.wait_ge(chain, c + 14)
                    v.tensor_tensor(rows_w[:, :, D + COL_DG], top[:, 6, :], rows_w[:, :, D + COL_G2], ALU.subtract)

            def places(b, step):
                c = b * CHAIN + 14
                v.wait_ge(side_mm, step.n + 1)
                v.tensor_tensor(place[:, :, :], bank_m[step.bank][:, 0:NT_TOK * E].rearrange("p (j e) -> p j e", j=NT_TOK),
                                base[:, :].unsqueeze(1).to_broadcast(OF_TOKENS), ALU.add).then_inc(chain, 1)
                v.wait_ge(chain, c + 1)
                v.tensor_tensor(base[:, :], bank_m[step.bank][:, NT_TOK * E:(NT_TOK + 1) * E], base[:, :], ALU.add).then_inc(side_done, 1)
                v.tensor_tensor(tmp8[:, :, :], hot1[:, :, :], place[:, :, :], ALU.mult)
                v.tensor_tensor(tmp8b[:, :, :], hot2[:, :, :], place[:, :, :], ALU.mult).then_inc(chain, 1)
                v.wait_ge(chain, c + 2)
                v.tensor_reduce(slot_f[:, 0, :], tmp8[:, :, :], AX.X, ALU.add).then_inc(chain, 1)
                v.tensor_reduce(slot_f[:, 1, :], tmp8b[:, :, :], AX.X, ALU.add).then_inc(chain, 1)
                v.wait_ge(chain, c + 4)
                v.tensor_copy(slot_i[:, :, :], slot_f[:, :, :]).then_inc(rows_ready, 1)

            def side(step, b, par):
                src, c, kind = bank_m[step.bank], step.half, step.kind
                if step.turned:
                    return
                if kind == "logits":
                    return take_logits(b, step)
                if kind == "prefix":
                    return places(b, step)
                if kind == "out":
                    v.wait_ge(side_mm, step.n + 1)
                    v.wait_ge(res_ready, b + 1)
                    half_of = x2[:, 2 * c:2 * c + 2, :].rearrange("p j d -> p (j d)")
                    v.scalar_tensor_tensor(out=half_of, in0=src, scalar=gxw[:, 0:1], in1=half_of, op0=ALU.mult, op1=ALU.add).then_inc(side_done, 1)
                    return
                v.wait_ge(side_hi, step.hi + 1)
                if kind in ("oT", "zT"):
                    hi, lo = (oT_hi, oT_lo) if kind == "oT" else (zrT_hi, zrT_lo)
                    v.tensor_tensor(lo[:, c, :], src, hi[:, c, :], ALU.subtract).then_inc(side_done, 1)
                elif kind == "v":
                    h, l = (t[par][:, 2 * c:2 * c + 2, :].rearrange("p j d -> p (j d)") for t in (v_hi, v_lo))
                    v.scalar_tensor_tensor(out=l, in0=src, scalar=1.0 / W_SCALE, in1=h, op0=ALU.mult, op1=ALU.subtract).then_inc(side_done, 1)
                else:
                    v.scalar_tensor_tensor(out=two_lo[kind][:, c, :], in0=src, scalar=(QSCALE if kind == "q" else 1.0) / W_SCALE, in1=two_hi[kind][:, c, :],
                                           op0=ALU.mult, op1=ALU.subtract).then_inc(side_done, 1)

            for step in FIRST:
                side(step, 0, 0)
                if step.name == "k1":
                    split_projection("v", wv_hi, wv_lo)
            v.wait_ge(small_in, 16 * SMALL_LOADS)
            for k in range(DC):
                v.tensor_copy(rlb_bc[:, k, :], rlb_s[:, k:k + 1].to_broadcast([P, P])).then_inc(dve, 1)
                v.tensor_scalar(rw_sc[:, k, :], rw_raw[:, k, :], rls_s[:, k:k + 1], W_SCALE, ALU.mult, ALU.mult).then_inc(dve, 1)
            v.wait_ge(dve, 11)
            v.tensor_copy(rw_hi[:, :, :], rw_sc[:, :, :]).then_inc(dve, 1)
            v.wait_ge(dve, 12)
            v.tensor_tensor(rw_lo[:, :, :], rw_sc[:, :, :], rw_hi[:, :, :], ALU.subtract).then_inc(router_ready, 1)
            v.wait_ge(gates_tanh, 2)
            v.tensor_scalar(gxw[:, :], gx[:, :], 1.0 / W_SCALE, None, ALU.mult).then_inc(dve, 1)
            v.tensor_scalar(tanh_bo[:, :], tanh_bo[:, :], gx[:, 0:1], None, ALU.mult).then_inc(gates_done, 1)
            split_projection("o", wo_hi, wo_lo)
            v.wait_ge(dve, 13)
            v.wait_ge(rbias_mm, 1)
            v.tensor_tensor(rbias[:, :], bank_o[1][:, 0:E], rbias[:, :], ALU.add).then_inc(rbias_done, 1)

            def batch(b, par):
                first, final = isinstance(b, int) and b == 0, isinstance(b, int) and b == B - 1

                def route(u, gap_in_unit):
                    if not first:
                        for n in ROUTE.get((u, gap_in_unit), ()):
                            routing(b - 1, n)

                for u in range(UNITS):
                    g, t = b * UNITS + u, u % 2
                    if not (final and u >= UNITS - 2):
                        row_max(g + 2, t)
                    if u % HEADS == 0 and u > 0:
                        invert(b, u // HEADS - 1)
                    elif u == 0 and not first:
                        invert(b - 1, NT_TOK - 1)
                    route(u, 0)
                    v.wait_ge(pT_hi_done, g + 1)
                    v.tensor_tensor(pT_lo[t], bank_t[t], pT_hi[t], ALU.subtract).then_inc(pT_lo_done, 1)
                    route(u, 1)
                    if u % HEADS == 0 and u > 0:
                        normalise(b, u // HEADS - 1, par)
                    elif u == 0 and not first:
                        normalise(b - 1, NT_TOK - 1, 1 - par)
                    if final and 0 <= u - W2_FIRST_UNIT < AFTER_EVEN:
                        w2_low(u - W2_FIRST_UNIT)
                    for j in range(NT_TOK):
                        if u == AT["x_stats"][j] and not final:
                            x_stats(b + 1, j)
                        if u == AT["z_stats"][j] and not first:
                            z_statistics(b - 1, j, [step.k for step in steps_of(b) if step.name == "out1"][0] + 1)
                    if final and u == 0:
                        count_full()
                    if final and u == 3:
                        plan(0, EARLY_TILES, None)
                    if final and u == 4:
                        count_taken()
                    if u == AT["x_norm"] and not final:
                        normalise_x(b + 1)
                    route(u, 2)
                    for step in steps_of(b):
                        if step.taken == u:
                            side(step, b - 1 if step.name in POST else b + 1, 1 - par)
                    route(u, 3)

            def w2_low(n):
                v.wait_ge(w2_hi_done, n + 1)
                v.scalar_tensor_tensor(out=w2_piece(n, 1), in0=stage[n % 2][:, :], scalar=W_SCALE, in1=w2_piece(n, 0),
                                       op0=ALU.mult, op1=ALU.subtract).then_inc(w2_lo_done, 1)

            links = [0]

            def linked(ins):
                links[0] += 1
                ins.then_inc(plan_step, 1)
                v.wait_ge(plan_step, links[0])

            def plan(first, last, start):
                n = slice(first, last)
                shape = [P, last - first, E]
                linked(v.tensor_tensor_scan(cum[:, :], one8[:, :], left[:, :], float(first), ALU.mult, ALU.add))
                linked(v.tensor_tensor(past[:, n, :], tile_f[:, n].unsqueeze(2).to_broadcast(shape),
                                       cum[:, :].unsqueeze(1).to_broadcast(shape), ALU.is_ge))
                linked(v.tensor_tensor(past_n[:, n, :], past[:, n, :], weight[:, :].unsqueeze(1).to_broadcast(shape), ALU.mult))
                linked(v.tensor_reduce(tab[:, 0, n], past[:, n, :], AX.X, ALU.add))
                linked(v.tensor_reduce(tab[:, 1, n], past_n[:, n, :], AX.X, ALU.add))
                linked(v.tensor_tensor(tab[:, 1, n], tile_f[:, n], tab[:, 1, n], ALU.add))
                if start is not None:
                    linked(v.tensor_scalar(tab[:, 1, n], tab[:, 1, n], start, -float(first), ALU.add, ALU.add))
                linked(v.tensor_scalar(tab[:, 2, n], tab[:, 0, n], float(E), float(TILE), ALU.is_lt, ALU.mult))
                linked(v.tensor_tensor(tab[:, 1, n], tab[:, 1, n], tab[:, 2, n], ALU.mult))
                linked(v.tensor_scalar(tile_expert[:, n], tab[:, 0, n], float(E - 1), None, ALU.min))
                v.scalar_tensor_tensor(out=tile_row[:, n], in0=tab[:, 0, n], scalar=float(REGION), in1=tab[:, 1, n],
                                       op0=ALU.mult, op1=ALU.add).then_inc(tables, 1)

            def count_full():
                linked(v.tensor_tensor(cnt_f[:, :], base[:, :], region_f[:, :], ALU.subtract))
                linked(v.tensor_copy(cnt_i[:, :], cnt_f[:, :]))
                linked(v.tensor_scalar(cnt_i[:, :], cnt_i[:, :], TILE.bit_length() - 1, None, ALU.arith_shift_right))
                linked(v.tensor_copy(left[:, :], cnt_i[:, :]))
                linked(v.tensor_scalar(weight[:, :], left[:, :], -1.0, None, ALU.mult))

            def count_taken():
                linked(v.tensor_scalar(cnt_f[:, :], cum[:, :], float(EARLY_TILES), None, ALU.min))
                linked(v.tensor_copy(taken[:, 0:1], cnt_f[:, 0:1]))
                linked(v.tensor_tensor(taken[:, 1:E], cnt_f[:, 1:E], cnt_f[:, 0:E - 1], ALU.subtract))
                linked(v.tensor_scalar(taken_step[:, E - 1:E], taken[:, E - 1:E], -1.0, None, ALU.mult))
                linked(v.tensor_tensor(taken_step[:, 0:E - 1], taken[:, 1:E], taken[:, 0:E - 1], ALU.subtract))

            def plan_others():
                v.tensor_copy(pad_at[:, :], base[:, :]).then_inc(tables, 1)
                linked(v.tensor_tensor(cnt_f[:, :], base[:, :], region_f[:, :], ALU.subtract))
                linked(v.tensor_scalar(cnt_i[:, :], cnt_f[:, :], float(TILE - 1), None, ALU.add))
                linked(v.tensor_scalar(cnt_i[:, :], cnt_i[:, :], TILE.bit_length() - 1, None, ALU.arith_shift_right))
                linked(v.tensor_copy(cnt_f[:, :], cnt_i[:, :]))
                linked(v.tensor_tensor(left[:, :], cnt_f[:, :], taken[:, :], ALU.subtract))
                linked(v.tensor_tensor(weight[:, :], taken_step[:, :], left[:, :], ALU.subtract))
                plan(EARLY_TILES, NT, taken[:, 0:1])
                v.wait_ge(tables, 3)

            def row_max(g, t):
                v.wait_ge(score_mm, g + 1)
                wait(v, exp_done, g - 1)
                v.tensor_reduce(neg_max[:, t:t + 1], bank_s[t], AX.X, ALU.max, negate=True).then_inc(max_done, 1)

            def invert(b, j):
                n = b * NT_TOK + j
                v.wait_ge(exp_done, (n + 1) * HEADS)
                wait(v, on_done, n)
                v.reciprocal(p_inv[:, :], p_sum[:, j % 2, :]).then_inc(inv_done, 1)

            def normalise(b, j, par):
                n = b * NT_TOK + j
                v.wait_ge(pv_mm, (n + 1) * HEADS)
                v.wait_ge(inv_done, n + 1)
                v.tensor_tensor(o_n[par][:, j, :].rearrange("p (h d) -> p h d", h=HEADS),
                                bank_o[j % 2][:, 0:D].rearrange("p (h d) -> p h d", h=HEADS),
                                p_inv[:, :].unsqueeze(2).to_broadcast([P, HEADS, HD]), ALU.mult).then_inc(on_done, 1)

            row_max(0, 0)
            row_max(1, 1)
            over_batches(v, batch)
            def expert_of(j):
                return v.value_load(tile_expert[0:1, j:j + 1] if isinstance(j, int) else tile_expert[0:1, bass.ds(j, 1)], min_val=0, max_val=E - 1)

            def rows_split(j, par, e):
                v.wait_ge(zT_mm, j + 1)
                wait(v, z_hi_done, j)
                bank = bank_o[0] if is_single(j) else bank_z
                for c in range(DC):
                    col = bass.ds(e * DC + c, 1)
                    last = v.tensor_scalar(z_aff[:, c, :], bank[:, c * TILE:(c + 1) * TILE], els_s[:, col], elb_s[:, col], ALU.mult, ALU.add)
                last.then_inc(z_aff_done, 1)
                v.tensor_copy(extras[:, j if isinstance(j, int) else bass.ds(j, 1), :, :] if isinstance(j, int) else
                              extras[:, bass.ds(j, 1), :, :].rearrange("p a s n -> p (a s) n"), rows_r[par][:, :, D:ROW])
                v.wait_ge(z_hi_done, j + 1)
                v.tensor_tensor(z_lo[:, :, :], z_aff[:, :, :], z_hi[:, :, :], ALU.subtract).then_inc(z_lo_done, 1)

            def split_hidden(j, par):
                wait(v, y_mm, j if is_single(j) else j - 1)
                h = 0 if is_single(j) else par
                for m in range(HC // 2):
                    cols = slice(m * 2 * TILE, (m + 1) * 2 * TILE)
                    if not scalar_takes_high(j):
                        v.wait_ge(gelu_done, j * 4 + m + 1)
                        v.tensor_copy(h_hi[h][:, cols], hid[:, m, :]).then_inc(h_hi_done, 1)
                    v.wait_ge(h_hi_done, j * 4 + m + 1)
                    v.tensor_tensor(h_lo[h][:, cols], hid[:, m, :], h_hi[h][:, cols], ALU.subtract).then_inc(h_lo_done, 1)

            def finish_rows(j, par, e):
                mine = extras[:, j, :, :] if isinstance(j, int) else extras[:, bass.ds(j, 1), :, :].rearrange("p a s n -> p (a s) n")
                wait(v, y_added, 32 * (j - 1))
                wait(v, y_done, j)
                v.tensor_copy(y_idx[par][:, :], mine[:, :, COL_TOKEN])
                v.scalar_tensor_tensor(out=gate[:, :], in0=mine[:, :, COL_E1], scalar=code[:, 0, bass.ds(e, 1)], in1=mine[:, :, COL_DG],
                                       op0=ALU.is_equal, op1=ALU.mult).then_inc(gate_step, 1)
                v.wait_ge(gate_step, j * 3 + 1)
                v.tensor_tensor(gate[:, :], gate[:, :], mine[:, :, COL_G2], ALU.add).then_inc(gate_step, 1)
                v.wait_ge(y_mm, j + 1)
                if isinstance(j, int) and j == 0:
                    v.wait_ge(b2_in, 16)
                v.scalar_tensor_tensor(out=y_out[par][:, :, :], in0=bank_y[1 if is_single(j) else par][:, :].rearrange("p (s d) -> p s d", s=2), scalar=1.0 / W_SCALE,
                                       in1=b2_all[:, bass.ds(e, 1), :].to_broadcast([P, 2, D]), op0=ALU.mult, op1=ALU.add).then_inc(gate_step, 1)
                v.wait_ge(gate_step, j * 3 + 3)
                for s in range(2):
                    last = v.tensor_scalar(y_out[par][:, s, :], y_out[par][:, s, :], gate[:, s:s + 1], None, ALU.mult)
                last.then_inc(y_done, 1)

            def finish(*names):
                for name in names:
                    side(LAST[name], B - 1, (B - 1) % 2)

            invert(B - 1, NT_TOK - 1)
            normalise(B - 1, NT_TOK - 1, (B - 1) % 2)
            rows_split(0, 0, expert_of(0))
            finish("oT0", "oT1")
            w2_low(AFTER_EVEN)
            w2_low(AFTER_EVEN + 1)
            finish("out0", "out1")
            for j in range(NT_TOK):
                z_statistics(B - 1, j, LAST["out1"].k + 1)
            rows_split(1, 1, expert_of(1))
            split_hidden(0, 0)
            w2_low(AFTER_EVEN + 2)
            w2_low(AFTER_EVEN + 3)
            finish("zT0", "zT1")
            w2_low(AFTER_EVEN + 4)
            w2_low(AFTER_EVEN + 5)
            rows_split(2, 0, expert_of(2))
            finish("logits")
            for n in range(12):
                routing(B - 1, n)
            finish_rows(0, 0, expert_of(0))
            split_hidden(1, 1)
            for n in range(12, 17):
                routing(B - 1, n)
            finish("prefix")
            rows_split(3, 1, expert_of(3))
            plan_others()
            split_hidden(2, 0)
            finish_rows(1, 1, expert_of(1))
            rows_split(4, 0, expert_of(4))
            split_hidden(3, 1)
            finish_rows(2, 0, expert_of(2))

            def tile(j, par):
                split_hidden(j + 1, 1 - par)
                rows_split(j + 2, par, expert_of(j + 2))
                finish_rows(j, par, expert_of(j))

            tile(3, 1)
            tile(4, 0)
            over_tiles(v, tile)
            split_hidden(NT - 1, (NT - 1) % 2)
            finish_rows(NT - 2, (NT - 2) % 2, expert_of(NT - 2))
            finish_rows(NT - 1, (NT - 1) % 2, expert_of(NT - 1))


_OUT_SHAPE = (8, 512, 256)


def kernel(**inputs):
    import numpy as np
    import concourse.bacc as bacc
    from concourse.bass_utils import run_bass_kernel_spmd

    def a(name):
        return np.asarray(inputs[name])

    E = a("L0_ffn_w1").shape[0]
    arrays = {
        "x": a("x"),
        "ctxT": a("ctx_768").transpose(0, 2, 1),
        "g_xattn": a("g_xattn"),
        "g_ffn": a("g_ffn"),
        "WqT": a("L0_xattn_Wq").T,
        "WkT": a("L0_xattn_Wk").T,
        "WvT": a("L0_xattn_Wv").T,
        "WoT": a("L0_xattn_Wo").T,
        "bo": a("L0_xattn_bo"),
        "rls": a("L0_ffn_router_ln_scale").reshape(-1, 128).T,
        "rlb": a("L0_ffn_router_ln_bias").reshape(-1, 128).T,
        "rwT": a("L0_ffn_router_w").T,
        "rb": a("L0_ffn_router_b"),
        "els": a("L0_ffn_expert_ln_scale").reshape(-1, 128).T,
        "elb": a("L0_ffn_expert_ln_bias").reshape(-1, 128).T,
        "w1T": a("L0_ffn_w1").transpose(0, 2, 1),
        "b1": a("L0_ffn_b1").reshape(-1, 128).T,
        "w2T": a("L0_ffn_w2").transpose(0, 2, 1),
        "b2": a("L0_ffn_b2"),
    }
    nc = bacc.Bacc("TRN2", target_bir_lowering=False, num_devices=1)
    maps, args = {}, []
    for name, value in arrays.items():
        value = np.ascontiguousarray(value)
        maps[f"in_{name}"] = value
        args.append(nc.dram_tensor(f"in_{name}", value.shape, mybir.dt.from_np(value.dtype), kind="ExternalInput").ap())
    out = nc.dram_tensor("out", _OUT_SHAPE, F32, kind="ExternalOutput").ap()
    build(nc, *args, out)
    r = run_bass_kernel_spmd(nc, [maps], core_ids=[0])
    return r.results[0]["out"]
```
